# Optimizing a Trainium2 kernel written in Bass

```python
import numpy as np
import jax
import jax.numpy as jnp

def _softmax(x, axis=-1):
    return jax.nn.softmax(x, axis=axis)

def _gelu(x):
    return jax.nn.gelu(x, approximate=True)

def _silu(x):
    return jax.nn.silu(x)

def _sigmoid(x):
    return jax.nn.sigmoid(x)

def _layernorm(x, axis=-1, eps=1e-05):
    m = jnp.mean(x, axis=axis, keepdims=True)
    v = jnp.var(x, axis=axis, keepdims=True)
    return (x - m) / jnp.sqrt(v + eps)

def _scatter_add(tgt, idx, src, axis=0):
    return tgt.at[idx].add(src)

def _segment_sum(src, seg, n):
    return jax.ops.segment_sum(src, seg, n)
kernel_name = 'mk_decoder_preln_d2_seqx_r4_d1471a'

def setup_inputs(seed: int=0):
    np.random.seed(seed)
    _w = jnp.asarray

    def _rec_inputs():
        import jax
        import jax.numpy as jnp
        _rk = jax.random.key(seed)
        x = 7.22e-05 + 1 * jax.random.normal(jax.random.fold_in(_rk, 1), (64, 128, 256), jnp.float32)
        _lenS = 128 - jax.random.randint(jax.random.fold_in(_rk, 7), (64,), 0, max(1, 128 // 4) + 1, jnp.int32)
        _lenS2 = 128 - jax.random.randint(jax.random.fold_in(_rk, 8), (64,), 0, max(1, 128 // 4) + 1, jnp.int32)
        _ctx_1024P = jax.random.normal(jax.random.fold_in(_rk, 11), (64, 16, 256), jnp.float32)
        _ctx_1024c = jax.random.dirichlet(jax.random.fold_in(_rk, 511), 0.3 * jnp.ones((16,), jnp.float32), (64, 128))
        _ctx_1024t = jnp.einsum('bsk,bkd->bsd', _ctx_1024c, _ctx_1024P)
        _ctx_1024t = _ctx_1024t * jax.lax.rsqrt(jnp.mean(jnp.square(_ctx_1024t)) + 1e-12) * 0.953939
        ctx_1024 = 4.13588e-05 + 0.999923 * (_ctx_1024t + 0.3 * jax.random.normal(jax.random.fold_in(_rk, 611), (64, 128, 256), jnp.float32))
        return (x, ctx_1024)
    x, ctx_1024 = _rec_inputs()

    def _L0_attn_setup():
        import jax, jax.numpy as jnp
        import numpy as np
        from jax import lax
        D_MODEL = 256
        D_STATE = 128
        D_CONV = 4
        EXPAND = 2
        HEADDIM = 64
        D_INNER = EXPAND * D_MODEL
        NHEADS = D_INNER // HEADDIM
        CONV_DIM = D_INNER + 2 * D_STATE
        D_IN_PROJ = 2 * D_INNER + 2 * D_STATE + NHEADS
        EPS = 1e-05

        def _ssm_forward(x, in_proj_w, conv_w, conv_b, norm_w, out_proj_w, dt_bias, A_log, D_param):
            B, L, _ = x.shape
            zxbcdt = jnp.einsum('bld,ed->ble', x, in_proj_w)
            z = zxbcdt[..., :D_INNER]
            xBC = zxbcdt[..., D_INNER:D_INNER + CONV_DIM]
            dt = zxbcdt[..., D_INNER + CONV_DIM:]
            xBC_c = lax.conv_general_dilated(xBC.transpose(0, 2, 1), conv_w, window_strides=(1,), padding=[(D_CONV - 1, 0)], feature_group_count=CONV_DIM, dimension_numbers=('NCH', 'OIH', 'NCH'))
            xBC = jax.nn.silu((xBC_c + conv_b[None, :, None]).transpose(0, 2, 1))
            x_part = xBC[..., :D_INNER]
            B_part = xBC[..., D_INNER:D_INNER + D_STATE]
            C_part = xBC[..., D_INNER + D_STATE:]
            x_heads = x_part.reshape(B, L, NHEADS, HEADDIM)
            dt = jax.nn.softplus(dt + dt_bias)
            A = -jnp.exp(A_log)

            def step(state, inp):
                x_t, B_t, C_t, dt_t = inp
                decay = jnp.exp(A[None, :] * dt_t)
                state = state * decay[:, :, None, None] + (x_t * dt_t[:, :, None])[..., None] * B_t[:, None, None, :]
                y_t = jnp.einsum('bhpn,bn->bhp', state, C_t)
                return (state, y_t)
            state0 = jnp.zeros((B, NHEADS, HEADDIM, D_STATE), dtype=x.dtype)
            inputs = (jnp.moveaxis(x_heads, 1, 0), jnp.moveaxis(B_part, 1, 0), jnp.moveaxis(C_part, 1, 0), jnp.moveaxis(dt, 1, 0))
            _, y_seq = lax.scan(step, state0, inputs)
            y = jnp.moveaxis(y_seq, 0, 1).reshape(B, L, D_INNER)
            D_full = jnp.repeat(D_param, HEADDIM)
            y = y + x_part * D_full
            y = y * jax.nn.silu(z)
            y = y * jax.lax.rsqrt(jnp.mean(y * y, axis=-1, keepdims=True) + EPS) * norm_w
            return jnp.einsum('ble,de->bld', y, out_proj_w)
        key = jax.random.key(seed)
        ks = jax.random.split(key, 8)
        B, L = (2, 512)
        x = jax.random.normal(ks[0], (B, L, D_MODEL), dtype=jnp.float32)
        in_proj_w = jax.random.normal(ks[1], (D_IN_PROJ, D_MODEL), dtype=jnp.float32) * 0.02
        conv_w = jax.random.normal(ks[2], (CONV_DIM, 1, D_CONV), dtype=jnp.float32) * 0.2
        conv_b = jax.random.normal(ks[3], (CONV_DIM,), dtype=jnp.float32) * 0.02
        norm_w = jnp.ones((D_INNER,), dtype=jnp.float32)
        out_proj_w = jax.random.normal(ks[4], (D_MODEL, D_INNER), dtype=jnp.float32) * 0.02
        dt_bias = jax.random.normal(ks[5], (NHEADS,), dtype=jnp.float32) * 0.1
        A_log = jax.random.normal(ks[6], (NHEADS,), dtype=jnp.float32) * 0.1
        D_param = jnp.ones((NHEADS,), dtype=jnp.float32)
        return {'x': x, 'in_proj_w': in_proj_w, 'conv_w': conv_w, 'conv_b': conv_b, 'norm_w': norm_w, 'out_proj_w': out_proj_w, 'dt_bias': dt_bias, 'A_log': A_log, 'D_param': D_param}
    _L0_attn_all = _L0_attn_setup()
    _L0_attn_in = {k: v for k, v in _L0_attn_all.items() if k in ('in_proj_w', 'conv_w', 'conv_b', 'norm_w', 'out_proj_w', 'dt_bias', 'A_log', 'D_param')}
    del _L0_attn_all

    def _L0_xattn_setup():
        import jax, jax.numpy as jnp
        import numpy as np
        D_MODEL = 256
        NUM_HEADS = 16
        HEAD_DIM = D_MODEL // NUM_HEADS
        MAX_SEQ = 128

        def rope_tables(seq_len, dim):
            inv_freq = 1.0 / 10000.0 ** (jnp.arange(0, dim, 2, dtype=jnp.float32) / dim)
            t = jnp.arange(seq_len, dtype=jnp.float32)
            freqs = jnp.einsum('i,j->ij', t, inv_freq)
            emb = jnp.concatenate([freqs, freqs], axis=-1)
            return (jnp.cos(emb), jnp.sin(emb))

        def rotate_half(x):
            x1, x2 = jnp.split(x, 2, axis=-1)
            return jnp.concatenate([-x2, x1], axis=-1)
        key = jax.random.key(seed)
        ks = jax.random.split(key, 12)
        B, S, D = (16, 128, D_MODEL)
        s = 1.0 / np.sqrt(D)
        inp = {'query': jax.random.normal(ks[0], (B, S, D), jnp.float32), 'key': jax.random.normal(ks[1], (B, S, D), jnp.float32), 'value': jax.random.normal(ks[2], (B, S, D), jnp.float32), 'Wq': jax.random.normal(ks[3], (D, D), jnp.float32) * s, 'bq': jnp.zeros((D,), jnp.float32), 'Wk': jax.random.normal(ks[4], (D, D), jnp.float32) * s, 'bk': jnp.zeros((D,), jnp.float32), 'Wv': jax.random.normal(ks[5], (D, D), jnp.float32) * s, 'bv': jnp.zeros((D,), jnp.float32), 'Wo': jax.random.normal(ks[6], (D, D), jnp.float32) * s, 'bo': jnp.zeros((D,), jnp.float32)}
        return inp
    _L0_xattn_all = _L0_xattn_setup()
    _L0_xattn_in = {k: v for k, v in _L0_xattn_all.items() if k in ('Wq', 'bq', 'Wk', 'bk', 'Wv', 'bv', 'Wo', 'bo')}
    del _L0_xattn_all

    def _L0_ffn_setup():
        import jax, jax.numpy as jnp
        import numpy as np
        from jax import lax
        T, B, I, M, O = (64, 64, 256, 256, 256)

        def _xavier(key, shape):
            fan_out, fan_in = shape
            limit = float(np.sqrt(6.0 / (fan_in + fan_out)))
            return jax.random.uniform(key, shape, jnp.float32, -limit, limit)
        key = jax.random.key(seed)
        ks = jax.random.split(key, 9)
        x = jax.random.normal(ks[0], (T, B, I), jnp.float32)
        return {'x': x, 'wf': _xavier(ks[1], (M, I)), 'uf': _xavier(ks[2], (M, M)), 'bf': jnp.zeros((M,), jnp.float32), 'wi': _xavier(ks[3], (M, I)), 'ui': _xavier(ks[4], (M, M)), 'bi': jnp.zeros((M,), jnp.float32), 'wc': _xavier(ks[5], (M, I)), 'uc': _xavier(ks[6], (M, M)), 'bc': jnp.zeros((M,), jnp.float32), 'wo': _xavier(ks[7], (O, I)), 'uo': _xavier(ks[8], (O, M)), 'bo': jnp.zeros((O,), jnp.float32), 'in_c': jnp.zeros((M,), jnp.float32)}
    _L0_ffn_all = _L0_ffn_setup()
    _L0_ffn_in = {k: v for k, v in _L0_ffn_all.items() if k in ('wf', 'uf', 'bf', 'wi', 'ui', 'bi', 'wc', 'uc', 'bc', 'wo', 'uo', 'bo', 'in_c')}
    del _L0_ffn_all

    def _L1_attn_setup():
        import jax, jax.numpy as jnp
        import numpy as np
        D_MODEL = 256
        N_HEADS = 16
        KV_HEADS = 4
        D_HEAD = D_MODEL // N_HEADS

        def _rope_factor(n, d_head, dtype):
            i = jnp.arange(d_head)
            theta = jnp.power(jnp.asarray(10000.0, dtype), (-2.0 * (i // 2) / d_head).astype(dtype))
            pos = jnp.arange(n, dtype=dtype)
            ang = pos[:, None] * theta[None, :]
            sign = jnp.where(jnp.arange(n) % 2 == 1, -1.0, 1.0).astype(dtype)
            return jnp.cos(ang) + sign[:, None] * jnp.sin(ang)

        def _rms_norm(x, g):
            eps = jnp.finfo(x.dtype).eps
            inv = jax.lax.rsqrt(jnp.mean(x * x, axis=-1, keepdims=True) + eps)
            return x * inv * g
        key = jax.random.key(seed)
        ks = jax.random.split(key, 5)
        s_in = 1.0 / np.sqrt(D_MODEL)
        x = jax.random.normal(ks[0], (2, 512, D_MODEL), dtype=jnp.float32)
        w_q = jax.random.normal(ks[1], (D_MODEL, D_MODEL), dtype=jnp.float32) * s_in
        w_k = jax.random.normal(ks[2], (D_MODEL, D_HEAD * KV_HEADS), dtype=jnp.float32) * s_in
        w_v = jax.random.normal(ks[3], (D_MODEL, D_HEAD * KV_HEADS), dtype=jnp.float32) * s_in
        w_o = jax.random.normal(ks[4], (D_MODEL, D_MODEL), dtype=jnp.float32) * s_in
        g = jnp.ones((D_MODEL,), dtype=jnp.float32)
        return {'x': x, 'w_q': w_q, 'w_k': w_k, 'w_v': w_v, 'w_o': w_o, 'g': g}
    _L1_attn_all = _L1_attn_setup()
    _L1_attn_in = {k: v for k, v in _L1_attn_all.items() if k in ('w_q', 'w_k', 'w_v', 'w_o', 'g')}
    del _L1_attn_all

    def _L1_xattn_setup():
        import jax, jax.numpy as jnp
        import numpy as np
        EMBED = 256
        B, S = (4, 1024)
        INV_SCALE = float(EMBED ** 0.5)
        key = jax.random.key(seed)
        ks = jax.random.split(key, 6)
        std = 1.0 / np.sqrt(EMBED)
        return {'query': jax.random.normal(ks[0], (B, S, EMBED), jnp.float32), 'key': jax.random.normal(ks[1], (B, S, EMBED), jnp.float32), 'value': jax.random.normal(ks[2], (B, S, EMBED), jnp.float32), 'Wq': jax.random.normal(ks[3], (EMBED, EMBED), jnp.float32) * std, 'bq': jnp.zeros((EMBED,), jnp.float32), 'Wk': jax.random.normal(ks[4], (EMBED, EMBED), jnp.float32) * std, 'bk': jnp.zeros((EMBED,), jnp.float32), 'Wv': jax.random.normal(ks[5], (EMBED, EMBED), jnp.float32) * std, 'bv': jnp.zeros((EMBED,), jnp.float32)}
    _L1_xattn_all = _L1_xattn_setup()
    _L1_xattn_in = {k: v for k, v in _L1_xattn_all.items() if k in ('Wq', 'bq', 'Wk', 'bk', 'Wv', 'bv')}
    del _L1_xattn_all

    def _L1_ffn_setup():
        import jax, jax.numpy as jnp
        import numpy as np
        H = 256
        I = 128
        E = 8
        K = 2
        SI = I * 2
        B, S = (2, 256)

        def _mlp(x, gw, uw, dw):
            return jax.nn.silu(x @ gw.T) * (x @ uw.T) @ dw.T
        key = jax.random.key(seed)
        ks = jax.random.split(key, 9)
        s = 0.02
        return {'x': jax.random.normal(ks[0], (B, S, H), jnp.float32), 'gate_w': jax.random.normal(ks[1], (E, H), jnp.float32) * s, 'lb_bias': jnp.zeros((E,), jnp.float32), 'expert_gate_w': jax.random.normal(ks[2], (E, I, H), jnp.float32) * s, 'expert_up_w': jax.random.normal(ks[3], (E, I, H), jnp.float32) * s, 'expert_down_w': jax.random.normal(ks[4], (E, H, I), jnp.float32) * s, 'shared_gate_w': jax.random.normal(ks[5], (SI, H), jnp.float32) * s, 'shared_up_w': jax.random.normal(ks[6], (SI, H), jnp.float32) * s, 'shared_down_w': jax.random.normal(ks[7], (H, SI), jnp.float32) * s}
    _L1_ffn_all = _L1_ffn_setup()
    _L1_ffn_in = {k: v for k, v in _L1_ffn_all.items() if k in ('gate_w', 'lb_bias', 'expert_gate_w', 'expert_up_w', 'expert_down_w', 'shared_gate_w', 'shared_up_w', 'shared_down_w')}
    del _L1_ffn_all
    return {'x': x, 'ctx_1024': ctx_1024, 'L0_attn_in_proj_w': _L0_attn_in['in_proj_w'], 'L0_attn_conv_w': _L0_attn_in['conv_w'], 'L0_attn_conv_b': _L0_attn_in['conv_b'], 'L0_attn_norm_w': _L0_attn_in['norm_w'], 'L0_attn_out_proj_w': _L0_attn_in['out_proj_w'], 'L0_attn_dt_bias': _L0_attn_in['dt_bias'], 'L0_attn_A_log': _L0_attn_in['A_log'], 'L0_attn_D_param': _L0_attn_in['D_param'], 'L0_xattn_Wq': _L0_xattn_in['Wq'], 'L0_xattn_bq': _L0_xattn_in['bq'], 'L0_xattn_Wk': _L0_xattn_in['Wk'], 'L0_xattn_bk': _L0_xattn_in['bk'], 'L0_xattn_Wv': _L0_xattn_in['Wv'], 'L0_xattn_bv': _L0_xattn_in['bv'], 'L0_xattn_Wo': _L0_xattn_in['Wo'], 'L0_xattn_bo': _L0_xattn_in['bo'], 'L0_ffn_wf': _L0_ffn_in['wf'], 'L0_ffn_uf': _L0_ffn_in['uf'], 'L0_ffn_bf': _L0_ffn_in['bf'], 'L0_ffn_wi': _L0_ffn_in['wi'], 'L0_ffn_ui': _L0_ffn_in['ui'], 'L0_ffn_bi': _L0_ffn_in['bi'], 'L0_ffn_wc': _L0_ffn_in['wc'], 'L0_ffn_uc': _L0_ffn_in['uc'], 'L0_ffn_bc': _L0_ffn_in['bc'], 'L0_ffn_wo': _L0_ffn_in['wo'], 'L0_ffn_uo': _L0_ffn_in['uo'], 'L0_ffn_bo': _L0_ffn_in['bo'], 'L0_ffn_in_c': _L0_ffn_in['in_c'], 'L1_attn_w_q': _L1_attn_in['w_q'], 'L1_attn_w_k': _L1_attn_in['w_k'], 'L1_attn_w_v': _L1_attn_in['w_v'], 'L1_attn_w_o': _L1_attn_in['w_o'], 'L1_attn_g': _L1_attn_in['g'], 'L1_xattn_Wq': _L1_xattn_in['Wq'], 'L1_xattn_bq': _L1_xattn_in['bq'], 'L1_xattn_Wk': _L1_xattn_in['Wk'], 'L1_xattn_bk': _L1_xattn_in['bk'], 'L1_xattn_Wv': _L1_xattn_in['Wv'], 'L1_xattn_bv': _L1_xattn_in['bv'], 'L1_ffn_gate_w': _L1_ffn_in['gate_w'], 'L1_ffn_lb_bias': _L1_ffn_in['lb_bias'], 'L1_ffn_expert_gate_w': _L1_ffn_in['expert_gate_w'], 'L1_ffn_expert_up_w': _L1_ffn_in['expert_up_w'], 'L1_ffn_expert_down_w': _L1_ffn_in['expert_down_w'], 'L1_ffn_shared_gate_w': _L1_ffn_in['shared_gate_w'], 'L1_ffn_shared_up_w': _L1_ffn_in['shared_up_w'], 'L1_ffn_shared_down_w': _L1_ffn_in['shared_down_w']}

def reference(x, ctx_1024, L0_attn_in_proj_w, L0_attn_conv_w, L0_attn_conv_b, L0_attn_norm_w, L0_attn_out_proj_w, L0_attn_dt_bias, L0_attn_A_log, L0_attn_D_param, L0_xattn_Wq, L0_xattn_bq, L0_xattn_Wk, L0_xattn_bk, L0_xattn_Wv, L0_xattn_bv, L0_xattn_Wo, L0_xattn_bo, L0_ffn_wf, L0_ffn_uf, L0_ffn_bf, L0_ffn_wi, L0_ffn_ui, L0_ffn_bi, L0_ffn_wc, L0_ffn_uc, L0_ffn_bc, L0_ffn_wo, L0_ffn_uo, L0_ffn_bo, L0_ffn_in_c, L1_attn_w_q, L1_attn_w_k, L1_attn_w_v, L1_attn_w_o, L1_attn_g, L1_xattn_Wq, L1_xattn_bq, L1_xattn_Wk, L1_xattn_bk, L1_xattn_Wv, L1_xattn_bv, L1_ffn_gate_w, L1_ffn_lb_bias, L1_ffn_expert_gate_w, L1_ffn_expert_up_w, L1_ffn_expert_down_w, L1_ffn_shared_gate_w, L1_ffn_shared_up_w, L1_ffn_shared_down_w):
    import jax
    import jax.numpy as jnp

    def _L0_attn_ref(x, in_proj_w, conv_w, conv_b, norm_w, out_proj_w, dt_bias, A_log, D_param):
        import jax, jax.numpy as jnp
        import numpy as np
        from jax import lax
        D_MODEL = 256
        D_STATE = 128
        D_CONV = 4
        EXPAND = 2
        HEADDIM = 64
        D_INNER = EXPAND * D_MODEL
        NHEADS = D_INNER // HEADDIM
        CONV_DIM = D_INNER + 2 * D_STATE
        D_IN_PROJ = 2 * D_INNER + 2 * D_STATE + NHEADS
        EPS = 1e-05

        def _ssm_forward(x, in_proj_w, conv_w, conv_b, norm_w, out_proj_w, dt_bias, A_log, D_param):
            B, L, _ = x.shape
            zxbcdt = jnp.einsum('bld,ed->ble', x, in_proj_w)
            z = zxbcdt[..., :D_INNER]
            xBC = zxbcdt[..., D_INNER:D_INNER + CONV_DIM]
            dt = zxbcdt[..., D_INNER + CONV_DIM:]
            xBC_c = lax.conv_general_dilated(xBC.transpose(0, 2, 1), conv_w, window_strides=(1,), padding=[(D_CONV - 1, 0)], feature_group_count=CONV_DIM, dimension_numbers=('NCH', 'OIH', 'NCH'))
            xBC = jax.nn.silu((xBC_c + conv_b[None, :, None]).transpose(0, 2, 1))
            x_part = xBC[..., :D_INNER]
            B_part = xBC[..., D_INNER:D_INNER + D_STATE]
            C_part = xBC[..., D_INNER + D_STATE:]
            x_heads = x_part.reshape(B, L, NHEADS, HEADDIM)
            dt = jax.nn.softplus(dt + dt_bias)
            A = -jnp.exp(A_log)

            def step(state, inp):
                x_t, B_t, C_t, dt_t = inp
                decay = jnp.exp(A[None, :] * dt_t)
                state = state * decay[:, :, None, None] + (x_t * dt_t[:, :, None])[..., None] * B_t[:, None, None, :]
                y_t = jnp.einsum('bhpn,bn->bhp', state, C_t)
                return (state, y_t)
            state0 = jnp.zeros((B, NHEADS, HEADDIM, D_STATE), dtype=x.dtype)
            inputs = (jnp.moveaxis(x_heads, 1, 0), jnp.moveaxis(B_part, 1, 0), jnp.moveaxis(C_part, 1, 0), jnp.moveaxis(dt, 1, 0))
            _, y_seq = lax.scan(step, state0, inputs)
            y = jnp.moveaxis(y_seq, 0, 1).reshape(B, L, D_INNER)
            D_full = jnp.repeat(D_param, HEADDIM)
            y = y + x_part * D_full
            y = y * jax.nn.silu(z)
            y = y * jax.lax.rsqrt(jnp.mean(y * y, axis=-1, keepdims=True) + EPS) * norm_w
            return jnp.einsum('ble,de->bld', y, out_proj_w)
        return _ssm_forward(x, in_proj_w, conv_w, conv_b, norm_w, out_proj_w, dt_bias, A_log, D_param)

    def _L0_xattn_ref(query, key, value, Wq, bq, Wk, bk, Wv, bv, Wo, bo):
        import jax, jax.numpy as jnp
        import numpy as np
        D_MODEL = 256
        NUM_HEADS = 16
        HEAD_DIM = D_MODEL // NUM_HEADS
        MAX_SEQ = 128

        def rope_tables(seq_len, dim):
            inv_freq = 1.0 / 10000.0 ** (jnp.arange(0, dim, 2, dtype=jnp.float32) / dim)
            t = jnp.arange(seq_len, dtype=jnp.float32)
            freqs = jnp.einsum('i,j->ij', t, inv_freq)
            emb = jnp.concatenate([freqs, freqs], axis=-1)
            return (jnp.cos(emb), jnp.sin(emb))

        def rotate_half(x):
            x1, x2 = jnp.split(x, 2, axis=-1)
            return jnp.concatenate([-x2, x1], axis=-1)
        B, S, D = query.shape
        H, Hd = (NUM_HEADS, HEAD_DIM)
        scale = Hd ** (-0.5)

        def proj(x, W, b):
            y = jnp.einsum('bsd,ed->bse', x, W) + b
            return y.reshape(B, S, H, Hd).transpose(0, 2, 1, 3)
        q = proj(query, Wq, bq)
        k = proj(key, Wk, bk)
        v = proj(value, Wv, bv)
        cos, sin = rope_tables(S, Hd)
        cos = cos[None, None]
        sin = sin[None, None]
        q = q * cos + rotate_half(q) * sin
        k = k * cos + rotate_half(k) * sin
        attn = jnp.einsum('bhqd,bhkd->bhqk', q, k) * scale
        attn_w = jax.nn.softmax(attn, axis=-1)
        out = jnp.einsum('bhqk,bhkd->bhqd', attn_w, v)
        out = out.transpose(0, 2, 1, 3).reshape(B, S, D)
        out = jnp.einsum('bsd,ed->bse', out, Wo) + bo
        return out

    def _L0_ffn_ref(x, wf, uf, bf, wi, ui, bi, wc, uc, bc, wo, uo, bo, in_c):
        import jax, jax.numpy as jnp
        import numpy as np
        from jax import lax
        T, B, I, M, O = (64, 64, 256, 256, 256)

        def _xavier(key, shape):
            fan_out, fan_in = shape
            limit = float(np.sqrt(6.0 / (fan_in + fan_out)))
            return jax.random.uniform(key, shape, jnp.float32, -limit, limit)
        batch = x.shape[1]
        c0 = jnp.broadcast_to(in_c, (batch, in_c.shape[0]))

        def step(c, xt):
            ft = jax.nn.sigmoid(xt @ wf.T + c @ uf.T + bf)
            it = jax.nn.sigmoid(xt @ wi.T + c @ ui.T + bi)
            gt = jnp.tanh(xt @ wc.T + c @ uc.T + bc)
            c = ft * c + it * gt
            return (c, None)
        c_final, _ = lax.scan(step, c0, x)
        h = jnp.tanh(jnp.einsum('tbi,oi->tbo', x, wo) + c_final @ uo.T + bo)
        return h

    def _L1_attn_ref(x, w_q, w_k, w_v, w_o, g):
        import jax, jax.numpy as jnp
        import numpy as np
        D_MODEL = 256
        N_HEADS = 16
        KV_HEADS = 4
        D_HEAD = D_MODEL // N_HEADS

        def _rope_factor(n, d_head, dtype):
            i = jnp.arange(d_head)
            theta = jnp.power(jnp.asarray(10000.0, dtype), (-2.0 * (i // 2) / d_head).astype(dtype))
            pos = jnp.arange(n, dtype=dtype)
            ang = pos[:, None] * theta[None, :]
            sign = jnp.where(jnp.arange(n) % 2 == 1, -1.0, 1.0).astype(dtype)
            return jnp.cos(ang) + sign[:, None] * jnp.sin(ang)

        def _rms_norm(x, g):
            eps = jnp.finfo(x.dtype).eps
            inv = jax.lax.rsqrt(jnp.mean(x * x, axis=-1, keepdims=True) + eps)
            return x * inv * g
        b, n, _ = x.shape
        reps = N_HEADS // KV_HEADS
        x_norm = _rms_norm(x, g)
        q = (x_norm @ w_q).reshape(b, n, N_HEADS, D_HEAD).transpose(0, 2, 1, 3)
        k = (x_norm @ w_k).reshape(b, n, KV_HEADS, D_HEAD).transpose(0, 2, 1, 3)
        v = (x_norm @ w_v).reshape(b, n, KV_HEADS, D_HEAD).transpose(0, 2, 1, 3)
        rf = _rope_factor(n, D_HEAD, x.dtype)
        q = q * rf
        k = k * rf
        q5 = q.reshape(b, reps, KV_HEADS, n, D_HEAD)
        scale = jnp.asarray(np.sqrt(D_MODEL), x.dtype)
        qkt = jnp.einsum('brkqa,bkca->brkqc', q5, k) / scale
        attn = jax.nn.softmax(qkt, axis=-1)
        s = jnp.einsum('brkqc,bkca->brkqa', attn, v)
        s = s.reshape(b, N_HEADS, n, D_HEAD).transpose(0, 2, 1, 3).reshape(b, n, D_MODEL)
        o = s @ w_o
        return s + o

    def _L1_xattn_ref(query, key, value, Wq, bq, Wk, bk, Wv, bv):
        import jax, jax.numpy as jnp
        import numpy as np
        EMBED = 256
        B, S = (4, 1024)
        INV_SCALE = float(EMBED ** 0.5)
        q = jnp.einsum('bsd,ed->bse', query, Wq) + bq
        k = jnp.einsum('bsd,ed->bse', key, Wk) + bk
        v = jnp.einsum('bsd,ed->bse', value, Wv) + bv
        scores = jnp.einsum('bqe,bke->bqk', q, k) / INV_SCALE
        probs = jax.nn.softmax(scores, axis=-1)
        return jnp.einsum('bqk,bke->bqe', probs, v)

    def _L1_ffn_ref(x, gate_w, lb_bias, expert_gate_w, expert_up_w, expert_down_w, shared_gate_w, shared_up_w, shared_down_w):
        import jax, jax.numpy as jnp
        import numpy as np
        H = 256
        I = 128
        E = 8
        K = 2
        SI = I * 2
        B, S = (2, 256)

        def _mlp(x, gw, uw, dw):
            return jax.nn.silu(x @ gw.T) * (x @ uw.T) @ dw.T
        b, s, h = x.shape
        xf = x.reshape(-1, h)
        logits = xf @ gate_w.T + lb_bias
        scores = jax.nn.sigmoid(logits.astype(jnp.float32))
        topw, topi = jax.lax.top_k(scores, K)
        topw = (topw / (topw.sum(-1, keepdims=True) + 1e-08)).astype(x.dtype)
        out = jnp.zeros_like(xf)
        for e in range(E):
            m = topi == e
            sel = m.any(axis=-1)
            cnt = m.sum()
            wmean = (topw * m).sum() / jnp.maximum(cnt, 1).astype(topw.dtype)
            y = _mlp(xf, expert_gate_w[e], expert_up_w[e], expert_down_w[e])
            out = out + jnp.where(sel[:, None], y * wmean, jnp.zeros((), x.dtype))
        out = out.reshape(b, s, h)
        out = out + _mlp(x, shared_gate_w, shared_up_w, shared_down_w)
        return out
    x = x + _L0_attn_ref(_layernorm(x, axis=-1), L0_attn_in_proj_w, L0_attn_conv_w, L0_attn_conv_b, L0_attn_norm_w, L0_attn_out_proj_w, L0_attn_dt_bias, L0_attn_A_log, L0_attn_D_param)
    x = x + _L0_xattn_ref(_layernorm(x, axis=-1), ctx_1024, ctx_1024, L0_xattn_Wq, L0_xattn_bq, L0_xattn_Wk, L0_xattn_bk, L0_xattn_Wv, L0_xattn_bv, L0_xattn_Wo, L0_xattn_bo)
    x = x + _L0_ffn_ref(_layernorm(x, axis=-1), L0_ffn_wf, L0_ffn_uf, L0_ffn_bf, L0_ffn_wi, L0_ffn_ui, L0_ffn_bi, L0_ffn_wc, L0_ffn_uc, L0_ffn_bc, L0_ffn_wo, L0_ffn_uo, L0_ffn_bo, L0_ffn_in_c)
    x = x + _L1_attn_ref(_layernorm(x, axis=-1), L1_attn_w_q, L1_attn_w_k, L1_attn_w_v, L1_attn_w_o, L1_attn_g)
    x = x + _L1_xattn_ref(_layernorm(x, axis=-1), ctx_1024, ctx_1024, L1_xattn_Wq, L1_xattn_bq, L1_xattn_Wk, L1_xattn_bk, L1_xattn_Wv, L1_xattn_bv)
    x = x + _L1_ffn_ref(_layernorm(x, axis=-1), L1_ffn_gate_w, L1_ffn_lb_bias, L1_ffn_expert_gate_w, L1_ffn_expert_up_w, L1_ffn_expert_down_w, L1_ffn_shared_gate_w, L1_ffn_shared_up_w, L1_ffn_shared_down_w)
    return x

_drawn_inputs = setup_inputs


def setup_inputs(seed=0):
    import zlib

    import numpy as np

    out = dict(_drawn_inputs(seed))
    spreads = {'L0_attn_norm_w': (1.0, 0.2),
     'L0_attn_D_param': (1.0, 0.2),
     'L0_xattn_bq': (0.0, 0.426),
     'L0_xattn_bk': (0.0, 0.8),
     'L0_xattn_bv': (0.0, 0.1),
     'L0_xattn_bo': (0.0, 0.1),
     'L0_ffn_bf': (0.0, 0.8),
     'L0_ffn_bi': (0.0, 0.8),
     'L0_ffn_bc': (0.0, 0.1),
     'L0_ffn_bo': (0.0, 0.1),
     'L0_ffn_in_c': (0.0, 0.8),
     'L1_attn_g': (1.0, 0.2),
     'L1_xattn_bq': (0.0, 0.585),
     'L1_xattn_bk': (0.0, 0.8),
     'L1_xattn_bv': (0.0, 0.1),
     'L1_ffn_lb_bias': (0.0, 0.8)}
    factors = {'L0_attn_dt_bias': 8.0,
     'L0_attn_A_log': 8.0,
     'L1_ffn_gate_w': 8.0,
     'L1_ffn_expert_gate_w': 8.0,
     'L1_ffn_expert_up_w': 8.0,
     'L1_ffn_expert_down_w': 8.0,
     'L1_ffn_shared_gate_w': 5.511,
     'L1_ffn_shared_up_w': 5.415,
     'L1_ffn_shared_down_w': 5.406}
    for name, (base, spread) in spreads.items():
        noise = np.random.default_rng([zlib.crc32(name.encode()), seed]).standard_normal(out[name].shape)
        drawn = base * np.exp(spread * noise) if base else spread * noise
        out[name] = jnp.asarray(drawn.astype(out[name].dtype))
    for name, factor in factors.items():
        out[name] = (out[name] * factor).astype(out[name].dtype)
    return out
```

```python
from contextlib import ExitStack, contextmanager

import numpy as np

import concourse.bass as bass
from concourse import mybir

P = 128
D = 256
DI = 512
NH = 8
HD = 64
CONV = 4
XBC = DI + 2 * P
HEADS = 16
DH = 16
KV = 4
E = 8
HID = 128
EPS = 1e-5
EPS32 = float(np.finfo(np.float32).eps)

F32 = mybir.dt.float32
F32R = mybir.dt.float32r
I32 = mybir.dt.int32
ALU = mybir.AluOpType
ACT = mybir.ActivationFunctionType
AX = mybir.AxisListType
ds = bass.ds

C_ID, C_UP, C_COS, C_SIN, C_RF, C_EVEN, C_ODD, C_IOTA, C_ONE, C_3_2, C_END = (
    0, 128, 256, 272, 288, 304, 305, 306, 314, 442, 443)


def constant_table():
    t = np.zeros((P, C_END), np.float32)
    t[:, C_ID:C_ID + P] = np.eye(P)
    t[:, C_UP:C_UP + P] = np.triu(np.ones((P, P)))
    pos = np.arange(P, dtype=np.float32)
    inv = (1.0 / np.power(np.float32(10000.0), np.arange(0, DH, 2, dtype=np.float32) / np.float32(DH))).astype(np.float32)
    ang = pos[:, None] * np.concatenate([inv, inv])[None, :]
    t[:, C_COS:C_COS + DH] = np.cos(ang)
    t[:, C_SIN:C_SIN + DH] = np.sin(ang) * np.where(np.arange(DH) < DH // 2, -1.0, 1.0)
    theta = np.power(np.float32(10000.0), (-2.0 * (np.arange(DH) // 2) / DH).astype(np.float32))
    ang = pos[:, None] * theta[None, :]
    t[:, C_RF:C_RF + DH] = np.cos(ang) + np.where(np.arange(P) % 2 == 1, -1.0, 1.0)[:, None] * np.sin(ang)
    t[:, C_EVEN] = (np.arange(P) // DH) % 2 == 0
    t[:, C_ODD] = (np.arange(P) // DH) % 2 == 1
    t[:, C_IOTA:C_IOTA + E] = E - np.arange(E)
    t[:, C_ONE:C_ONE + P] = 1.0
    t[:, C_3_2] = 1.5
    return t


SIGNALS = {
    "consts": """
        small_loaded halved bias_rows_ready bo2_mm start_state start_hi start_lo bv_hi bv_lo
        w0_load0 w0_load1 w0_load2 w0_load3 w0_scaled w0_tr w0_hi w0_lo consts_ready
    """.split(),
    "steps": """
        p_stats p_chain p_xn p_tr p_xnT p_dt p_min p_act p_nd p_cum
    """.split(),
    "layer0": """
        m_cur m_xn m_tr m_hi m_lo m_xbc m_raw m_tap m_conv2 m_conv m_z m_ztanh m_zg m_xtanh m_xbcs
        m_xtr m_g m_xt m_xdt m_xd m_gm m_bc m_relv m_rela m_exp m_M m_y m_yx m_y2 m_ss m_seed m_rs
        m_ytr m_yhi m_ylo m_out m_x1 c_stats c_aggr c_seed c_rs c_xn c_ctx c_x1b c_tr c_hi c_lo c_q
        c_kv c_kb c_qb c_v c_rot c_cos c_qr c_qtr c_kT c_qT c_sc c_max c_sub c_exp c_ptr c_pt c_pv
        c_rinv c_o c_otr c_ohi c_olo c_proj c_x2 r_stats r_aggr r_seed r_rs r_xn r_tr r_hi r_lo r_fi
        r_tfi r_go r_tg r_xo r_store r_a r_b r_d r_dhi r_dlo
    """.split(),
    "between": """
        w1_load0 w1_load1 w1_load2 w1_load3 w1_scaled w1_tr w1_hi w1_lo b_v b_vrow b_dhi l1_small
        l1_wg l1_whi l1_wlo
    """.split(),
    "layer1": """
        s_xo s_u s_h s_x3 s_stats s_aggr s_seed s_rs s_xn s_tr s_hi s_lo s_qkv s_qr s_v s_qtr s_kT
        s_qT s_sc s_max s_sub s_exp s_ptr s_pt s_pv s_rinv s_o s_x3s s_otr s_ohi s_olo s_proj s_x4
        d_stats d_aggr d_seed d_rs d_xn d_ctx d_x4b d_tr d_hi d_lo d_qk d_vmm d_qk_sb d_v d_sc d_max
        d_nmax d_exp d_ptr d_pt d_pv d_rinv d_x5 g_stats g_aggr g_seed g_rs g_xn g_tr g_xnT g_lg
        g_sum g_kept
    """.split(),
    "route": """
        w2_load0 w2_load1 w2_load2 w2_load3 w2_scaled w2_tr w2_hi w2_lo t_chain t_sig t_part t_tot
        t_coef
    """.split(),
    "experts": """
        f_xn f_tr f_hi f_lo f_gu f_tanh f_tg f_h f_htr f_hhi f_hlo f_acc f_x6 f_out0 f_out1
    """.split(),
}


def decoder(nc, args, xo_dram, table, out):
    (x, ctx, in_proj, conv_w, conv_b, norm_w, out_proj, dt_bias, A_log, D_param,
     c_Wq, c_bq, c_Wk, c_bk, c_Wv, c_bv, c_Wo, c_bo,
     wf, uf, bf, wi, ui, bi, wc, uc, bc, wo, uo, bo, in_c,
     s_wq, s_wk, s_wv, s_wo, s_g, d_Wq, d_bq, d_Wk, d_bk, d_Wv, d_bv,
     gate_w, lb_bias, e_gate, e_up, e_down, sh_gate, sh_up, sh_down) = args
    NB = x.shape[0]
    NT = NB * E

    with ExitStack() as stack:
        def sb(name, shape, dt=F32):
            return stack.enter_context(nc.sbuf_tensor(name, shape, dt))

        S = {name: stack.enter_context(nc.semaphore(name))
             for name in ["const_loaded"] + [f"x_loaded{c}" for c in range(8)]}

        @contextmanager
        def phase(name):
            own = {n: nc.alloc_semaphore(name=n) for n in SIGNALS[name]}
            S.update(own)
            with nc.Block() as block_:
                yield block_
            nc.clear_and_free_semaphores(list(own.values()))
            nc.all_engine_barrier()

        bank = [stack.enter_context(nc.psum_tensor(f"bank{k}", [P, 512], F32)) for k in range(8)]

        def past(count):
            return not isinstance(count, int) or count > 0

        def live(b):
            return not isinstance(b, int) or 0 <= b < NB

        def pipeline(eng, lag, step):
            for i in range(lag + 1):
                step(i)
            with eng.Fori(lag + 1, NB) as i:
                step(i)
            for i in range(NB, NB + lag):
                step(i)

        def mm3(pe, out_, lhs, rhs, first=True, last=True):
            pe.matmul(out_, lhs[0], rhs[0], start=first, stop=False)
            pe.matmul(out_, lhs[0], rhs[1], start=False, stop=False)
            return pe.matmul(out_, lhs[1], rhs[0], start=False, stop=last)

        def project(pe, out_, act, w, blocks, n0, n1):
            for k in range(blocks):
                last = mm3(pe, out_, (act[:, 0, k, :], act[:, 1, k, :]),
                           (w[:, 0, k, n0:n1], w[:, 1, k, n0:n1]), k == 0, k == blocks - 1)
            return last

        def project_T(pe, out_, act, w, n0, first=True, last_=True):
            for k in range(2):
                last = mm3(pe, out_, (w[:, 0, k, n0:n0 + P], w[:, 1, k, n0:n0 + P]),
                           (act[:, 0, k, :], act[:, 1, k, :]), first and k == 0, last_ and k == 1)
            return last

        const = sb("const", [P, C_END])
        ident = const[:, C_ID:C_ID + P]
        upper = const[:, C_UP:C_UP + P]
        m_even, m_odd = const[:, C_EVEN:C_EVEN + 1], const[:, C_ODD:C_ODD + 1]
        upper_r = sb("upper_r", [P, P], F32R)
        x_res = sb("x_res", [P, NB * D])
        TAB = 3 * NH + 2
        tab = sb("tab", [P, NB * TAB])
        tab3 = tab[:, :].rearrange("p (b n) -> p b n", n=TAB)
        WREG = 18432
        wts = sb("wts", [P, WREG], F32R)
        w_dt = sb("w_dt", [P, 2, NH])
        small = sb("small", [P, 96])
        rows = sb("rows", [P, 4 * D])
        work = sb("work", [P, 9112])
        workr = sb("workr", [P, 3584], F32R)
        tiny = sb("tiny", [P, 96])
        curr = sb("curr", [P, 2, NH], F32R)

        def wview(base, k, n):
            assert base + 2 * k * n <= WREG
            return wts[:, base:base + 2 * k * n].rearrange("p (s k n) -> p s k n", s=2, k=k)

        w_in = wview(0, 2, DI + XBC)
        w_out = wview(5120, 4, D)
        w_cq = wview(7168, 2, D)
        w_ckv = wview(8192, 2, 2 * D)
        w_co = wview(10240, 2, D)
        w_rx = wview(11264, 2, 3 * D)
        w_ru = wview(14336, 2, 3 * D)
        w_rxo = wview(17408, 2, D)
        w_uo = wview(0, 2, D)
        w_sqkv = wview(1024, 2, D + 2 * KV * DH)
        w_so = wview(2560, 2, D)
        w_dq = wview(3584, 2, D)
        w_dk = wview(4608, 2, D)
        w_dv = wview(5632, 2, D)
        w_gu = wview(0, 2, 10 * 2 * P)
        w_dn = wview(10240, 10, D)
        w_gate = sb("w_gate", [P, 2, E])

        col = {}
        at = [0]

        def small_cols(name, n):
            col[name] = small[:, at[0]:at[0] + n]
            at[0] += n
            return col[name]

        cw = small_cols("cw", 6 * CONV).rearrange("p (j k) -> p j k", k=CONV)
        cb = small_cols("cb", 6)
        expA = small_cols("expA", NH)
        dtb = small_cols("dtb", NH)
        dpar = small_cols("dpar", NH)
        gb = small_cols("gb", 6)
        inc = small_cols("inc", 2)
        bvc = small_cols("bvc", 2)
        gcol = small_cols("gcol", 2)
        dbq = small_cols("dbq", 2)
        dbk = small_cols("dbk", 2)
        lbb = small_cols("lbb", E)
        bvr = sb("bvr", [P, 2, 2], F32R)
        bqk_row = rows[:, 0:2 * D]
        bo2_row = rows[:, 2 * D:3 * D]
        bo_row = rows[:, 3 * D:4 * D]

        wpos = [0]

        def wk(n):
            a = work[:, wpos[0]:wpos[0] + n]
            wpos[0] += n
            assert wpos[0] <= 9112, wpos
            return a

        rpos = [0]

        def wr(n):
            a = workr[:, rpos[0]:rpos[0] + n]
            rpos[0] += n
            assert rpos[0] <= 3584, rpos
            return a

        def weights(pre, sets, scratch, jobs):
            stages = [scratch[:, 512 * k:512 * k + 512] for k in range(4)]

            def sync(e):
                for j, (rows_, n, _, _, _) in enumerate(jobs):
                    if past(j - 3): e.wait_ge(S[pre + "_tr"], j - 3)
                    e.dma_start(stages[j % 4][:, 0:n], rows_).then_inc(S[f"{pre}_load{j % 4}"], 16)

            def tensor(e):
                scaled = 0
                for j, (_, n, _, _, sc) in enumerate(jobs):
                    e.wait_ge(S[f"{pre}_load{j % 4}"], 16 * (j // 4 + 1))
                    if sc is not None:
                        scaled += 1
                        e.wait_ge(S[pre + "_scaled"], scaled)
                    if past(j - 3): e.wait_ge(S[pre + "_lo"], j - 3)
                    for c in range(n // P):
                        last = e.transpose(bank[j % 4][:, c * P:c * P + P],
                                           stages[j % 4][:, c * P:c * P + P], ident)
                    last.then_inc(S[pre + "_tr"], 1)

            def scalar(e):
                for j, (_, n, dst, f, _) in enumerate(jobs):
                    e.wait_ge(S[pre + "_tr"], j + 1)
                    src = bank[j % 4][:, 0:n].rearrange("p (c r) -> p c r", r=P)
                    e.activation(dst(0), src, ACT.Copy, scale=f).then_inc(S[pre + "_hi"], 1)

            def vector(e):
                def scale(j):
                    if j < len(jobs) and jobs[j][4] is not None:
                        e.wait_ge(S[f"{pre}_load{j % 4}"], 16 * (j // 4 + 1))
                        st = stages[j % 4][:, 0:jobs[j][1]]
                        e.tensor_tensor(st, st, jobs[j][4], ALU.mult).then_inc(S[pre + "_scaled"], 1)

                for j in range(2):
                    scale(j)
                for j, (_, n, dst, f, _) in enumerate(jobs):
                    e.wait_ge(S[pre + "_hi"], j + 1)
                    src = bank[j % 4][:, 0:n].rearrange("p (c r) -> p c r", r=P)
                    e.scalar_tensor_tensor(out=dst(1), in0=src, scalar=f, in1=dst(0).bitcast(F32),
                                           op0=ALU.mult, op1=ALU.subtract).then_inc(S[pre + "_lo"], 1)
                    scale(j + 2)

            return sync, tensor, scalar, vector

        def to(view, r0):
            return lambda part: view[:, part, :, r0:r0 + P]

        def settled(e):
            e.wait_ge(S["const_loaded"], 16)

        def rsqrt_seed(e, x_, xh_, t_, y_, chain, b):
            e.wait_ge(S[chain], 3 * b + 1)
            e.tensor_scalar(xh_, x_, -0.5, None, ALU.mult)
            e.tensor_scalar(t_.bitcast(I32), x_.bitcast(I32), 1, None, ALU.arith_shift_right)\
                .then_inc(S[chain], 1)
            e.wait_ge(S[chain], 3 * b + 2)
            e.tensor_scalar(y_.bitcast(I32), t_.bitcast(I32), -1.0, float(0x5F3759DF), ALU.mult, ALU.add)\
                .then_inc(S[chain], 1)

        def rsqrt_newton(e, xh_, t_, y_, chain, c0):
            three_halves = const[:, C_3_2:C_3_2 + 1]
            n = 0
            for _ in range(3):
                for out_, a_, b_ in ((t_, y_, y_), (t_, t_, xh_), (t_, t_, three_halves), (y_, y_, t_)):
                    if n:
                        if past(c0 + n): e.wait_ge(S[chain], c0 + n)
                    e.tensor_tensor(out_, a_, b_, ALU.add if b_ is three_halves else ALU.mult)\
                        .then_inc(S[chain], 1)
                    n += 1

        def stat_cols(c):
            return (tiny[:, c:c + 6], tiny[:, c + 6:c + 8], tiny[:, c + 8:c + 9], tiny[:, c + 9:c + 10],
                    tiny[:, c + 10:c + 11], tiny[:, c + 11:c + 12])

        def row_statistics(e, pre, b, src, cols, ready, factor=1.0, add=EPS):
            st, mv, x_, xh_, t_, y_ = cols
            settled(e)
            e.wait_ge(S[ready[0]], ready[1])
            if past(b): e.wait_ge(S[pre + "_xn"], b)
            e.bn_stats(st, src).then_inc(S[pre + "_stats"], 1)
            settled(e)
            e.wait_ge(S[pre + "_stats"], b + 1)
            e.bn_aggr(mv, st).then_inc(S[pre + "_aggr"], 1)
            e.wait_ge(S[pre + "_aggr"], b + 1)
            if past(12 * b): e.wait_ge(S[pre + "_rs"], 12 * b)
            e.tensor_scalar(x_, mv[:, 1:2], factor, add, ALU.mult, ALU.add).then_inc(S[pre + "_seed"], 1)
            rsqrt_seed(e, x_, xh_, t_, y_, pre + "_seed", b)

        nw_row = work[:, 0:DI]
        stage0 = work[:, 2048:4096]
        ff = [(wf, uf), (wi, ui), (wc, uc)]
        jobs0 = [(in_proj[r * P:(r + 1) * P, :], D, to(w_in, r * P), 1.0, None) for r in range(10)]
        jobs0 += [(out_proj[r * P:(r + 1) * P, :], DI, to(w_out, r * P), 1.0, nw_row) for r in range(2)]
        for r in range(2):
            jobs0 += [(c_Wq[r * P:(r + 1) * P, :], D, to(w_cq, r * P), 1.0, None),
                      (c_Wk[r * P:(r + 1) * P, :], D, to(w_ckv, r * P), 1.0, None),
                      (c_Wv[r * P:(r + 1) * P, :], D, to(w_ckv, D + r * P), 1.0, None),
                      (c_Wo[r * P:(r + 1) * P, :], D, to(w_co, r * P), 1.0, None),
                      (wo[r * P:(r + 1) * P, :], D, to(w_rxo, r * P), 1.0, None)]
            for g, (wx, wu) in enumerate(ff):
                jobs0 += [(wx[r * P:(r + 1) * P, :], D, to(w_rx, g * D + r * P), 1.0, None),
                          (wu[r * P:(r + 1) * P, :], D, to(w_ru, g * D + r * P), 0.5, None)]
        w0 = weights("w0", 4, stage0, jobs0)
        dt_stage = work[0:NH, 512:512 + D]
        bo2_in = work[:, 768:768 + D]
        d_state = sb("d_state", [P, 2, P])
        d_parts = sb("d_parts", [P, 2, 2, P], F32R)
        CHUNK = max(1, NB // 8)

        with phase("consts") as block:
            @block.sync
            def _(e):
                e.dma_start(const[:, :], table).then_inc(S["const_loaded"], 16)
                for dst, src in ((cw, conv_w.rearrange("(j p) o k -> p j (o k)", p=P)),
                                 (cb, conv_b.rearrange("(j p) -> p j", p=P)),
                                 (expA, A_log.partition_broadcast(P)), (dtb, dt_bias.partition_broadcast(P)),
                                 (dpar, D_param.partition_broadcast(P)),
                                 (gb[:, 0:2], bf.rearrange("(j p) -> p j", p=P)),
                                 (gb[:, 2:4], bi.rearrange("(j p) -> p j", p=P)),
                                 (gb[:, 4:6], bc.rearrange("(j p) -> p j", p=P)),
                                 (inc, in_c.rearrange("(j p) -> p j", p=P)),
                                 (bvc, c_bv.rearrange("(j p) -> p j", p=P)),
                                 (bqk_row[:, 0:D], c_bq.partition_broadcast(P)),
                                 (bqk_row[:, D:2 * D], c_bk.partition_broadcast(P)),
                                 (bo2_in, c_bo.partition_broadcast(P)), (bo_row, bo.partition_broadcast(P)),
                                 (nw_row, norm_w.partition_broadcast(P)),
                                 (dt_stage, in_proj[DI + XBC:DI + XBC + NH, :])):
                    with nc.allow_non_contiguous_dma(reason="small vectors, once"):
                        e.dma_start(dst, src).then_inc(S["small_loaded"], 16)
                w0[0](e)

            @block.gpsimd
            def _(e):
                for c in range(NB // CHUNK):
                    e.dma_start(x_res[:, c * CHUNK * D:(c + 1) * CHUNK * D].rearrange("p (b d) -> p b d", d=D),
                                x[c * CHUNK:(c + 1) * CHUNK].rearrange("b t d -> t b d")).then_inc(S[f"x_loaded{c}"], 16)

            @block.tensor
            def _(e):
                e.wait_ge(S["const_loaded"], 16)
                w0[1](e)
                e.wait_ge(S["small_loaded"], 16 * 16)
                for c in range(2):
                    last = e.transpose(bank[4][:, c * NH:c * NH + NH], dt_stage[:, c * P:c * P + P],
                                       ident[0:NH, 0:NH])
                last.then_inc(S["w0_tr"], 1)
                e.wait_ge(S["bv_lo"], 1)
                e.wait_ge(S["w0_lo"], len(jobs0))
                for k in range(2):
                    last = mm3(e, bank[5][:, 0:D], (bvr[:, 0, k:k + 1].to_broadcast([P, P]),
                                                    bvr[:, 1, k:k + 1].to_broadcast([P, P])),
                               (w_co[:, 0, k, :], w_co[:, 1, k, :]), k == 0, k == 1)
                last.then_inc(S["bo2_mm"], 1)

            @block.scalar
            def _(e):
                w0[2](e)
                e.wait_ge(S["w0_tr"], len(jobs0) + 1)
                e.activation(w_dt[:, :, :], bank[4][:, 0:2 * NH].rearrange("p (k n) -> p k n", k=2), ACT.Copy)\
                    .then_inc(S["consts_ready"], 1)
                e.wait_ge(S["small_loaded"], 16 * 16)
                e.activation(expA, expA, ACT.Exp).then_inc(S["consts_ready"], 1)

            @block.vector
            def _(e):
                e.wait_ge(S["const_loaded"], 16)
                e.wait_ge(S["small_loaded"], 16 * 16)
                e.tensor_scalar(small[:, 0:30], small[:, 0:30], 0.5, None, ALU.mult)
                e.tensor_scalar(gb[:, 0:4], gb[:, 0:4], 0.5, None, ALU.mult)
                e.tensor_scalar(inc, inc, 2.0, None, ALU.mult).then_inc(S["halved"], 1)
                e.tensor_scalar(nw_row, nw_row, float(np.sqrt(DI)), None, ALU.mult).then_inc(S["halved"], 1)
                e.tensor_copy(upper_r[:, :], upper)
                e.tensor_copy(bvr[:, 0, :], bvc).then_inc(S["bv_hi"], 1)
                e.wait_ge(S["bv_hi"], 1)
                e.tensor_tensor(bvr[:, 1, :], bvc, bvr[:, 0, :].bitcast(F32), ALU.subtract).then_inc(S["bv_lo"], 1)
                e.wait_ge(S["halved"], 2)
                e.tensor_copy(d_state[:, :, :], inc.unsqueeze(2).to_broadcast([P, 2, P])).then_inc(S["start_state"], 1)
                e.wait_ge(S["start_state"], 1)
                e.tensor_copy(d_parts[:, 0], d_state[:, :, :]).then_inc(S["start_hi"], 1)
                e.wait_ge(S["start_hi"], 1)
                e.tensor_tensor(d_parts[:, 1], d_state[:, :, :], d_parts[:, 0].bitcast(F32), ALU.subtract)\
                    .then_inc(S["start_lo"], 1)
                w0[3](e)
                e.wait_ge(S["bo2_mm"], 1)
                e.tensor_tensor(bo2_row, bank[5][:, 0:D], bo2_in, ALU.add).then_inc(S["bias_rows_ready"], 1)

        stats0 = work[:, 0:NB * 6].rearrange("p (b n) -> p b n", n=6)
        pn = work[:, 512:512 + 4 * NB].rearrange("p (k b) -> p k b", k=4)
        pxn = [work[:, 1024:1280], work[:, 1280:1536]]
        pxT = [work[:, 1536:1792], work[:, 1792:2048]]
        pdt = [work[:, 2048 + 512 * k:2048 + 512 * k + NT] for k in range(4)]
        mean_all, rstd_all = tab3[:, :, 3 * NH], tab3[:, :, 3 * NH + 1]
        dt_bank, cum_bank = bank[4], bank[5]

        def heads_of(a):
            return a.rearrange("p (b h) -> p b h", h=NH)

        with phase("steps") as block:
            @block.vector
            def _(e):
                for c in range(NB // CHUNK):
                    e.wait_ge(S[f"x_loaded{c}"], 16)
                    with e.Fori(c * CHUNK, (c + 1) * CHUNK) as b:
                        e.bn_stats(work[:, ds(b * 6, 6)], x_res[:, ds(b * D, D)])
                n = 0

                def link(i):
                    nonlocal n
                    n += 1
                    i.then_inc(S["p_stats"], 1)
                    e.wait_ge(S["p_stats"], n)

                a, d, v, y = (pn[:, k] for k in range(4))
                link(e.engine_nop())
                e.tensor_tensor(a, stats0[:, :, 1], stats0[:, :, 4], ALU.add)
                e.tensor_tensor(v, stats0[:, :, 2], stats0[:, :, 5], ALU.add)
                link(e.tensor_tensor(d, stats0[:, :, 1], stats0[:, :, 4], ALU.subtract))
                e.tensor_scalar(mean_all, a, 0.5, None, ALU.mult)
                e.tensor_scalar(v, v, 1.0 / D, EPS, ALU.mult, ALU.add)
                link(e.tensor_tensor(d, d, d, ALU.mult))
                link(e.scalar_tensor_tensor(out=v, in0=d, scalar=0.25, in1=v, op0=ALU.mult, op1=ALU.add))
                link(e.tensor_scalar(a.bitcast(I32), v.bitcast(I32), 1, None, ALU.arith_shift_right))
                link(e.tensor_scalar(y.bitcast(I32), a.bitcast(I32), -1.0, float(0x5F3759DF), ALU.mult, ALU.add))
                for k in range(3):
                    link(e.tensor_tensor(a, y, y, ALU.mult))
                    link(e.scalar_tensor_tensor(out=a, in0=a, scalar=-0.5, in1=v, op0=ALU.mult, op1=ALU.mult))
                    link(e.scalar_tensor_tensor(out=rstd_all if k == 2 else y, in0=a, scalar=1.5, in1=y,
                                                op0=ALU.add, op1=ALU.mult))

                def norm(b, k):
                    if past(b - 1): e.wait_ge(S["p_tr"], b - 1)
                    e.tensor_scalar(pxn[k], x_res[:, ds(b * D, D)], tab[:, ds(b * TAB + 3 * NH, 1)],
                                    tab[:, ds(b * TAB + 3 * NH + 1, 1)], ALU.subtract, ALU.mult)\
                        .then_inc(S["p_xn"], 1)

                norm(0, 0)
                norm(1, 1)
                with e.Fori(1, NB // 2) as half:
                    b = 2 * half
                    norm(b, 0)
                    norm(b + 1, 1)
                e.wait_ge(S["p_dt"], NB)
                v, ex, dt, nd = pdt
                link(e.tensor_tensor(heads_of(v), heads_of(dt_bank[:, 0:NT]),
                                     dtb.unsqueeze(1).to_broadcast([P, NB, NH]), ALU.add))
                link(e.tensor_scalar(ex, v, -1.0, None, ALU.mult))
                e.tensor_tensor(ex, ex, v, ALU.min).then_inc(S["p_min"], 1)
                e.wait_ge(S["p_act"], 1)
                link(e.scalar_tensor_tensor(out=dt, in0=v, scalar=0.0, in1=nd, op0=ALU.max, op1=ALU.add))
                e.tensor_copy(tab3[:, :, 2 * NH:3 * NH], heads_of(dt))
                link(e.tensor_tensor(heads_of(nd), heads_of(dt), expA.unsqueeze(1).to_broadcast([P, NB, NH]),
                                     ALU.mult))
                e.tensor_copy(tab3[:, :, 0:NH], heads_of(nd)).then_inc(S["p_nd"], 1)
                e.wait_ge(S["p_cum"], 1)
                e.tensor_copy(tab3[:, :, NH:2 * NH], heads_of(cum_bank[:, 0:NT]))

            @block.tensor
            def _(e):
                def transposes(b, k):
                    e.wait_ge(S["p_xn"], b + 1)
                    if past(b - 1): e.wait_ge(S["p_xnT"], b - 1)
                    for c in range(2):
                        last = e.transpose(bank[k][:, c * P:c * P + P], pxn[k][:, c * P:c * P + P], ident)
                    last.then_inc(S["p_tr"], 1)

                def dt_of(b, k):
                    e.wait_ge(S["p_xnT"], b + 1)
                    for c in range(2):
                        last = e.matmul(dt_bank[:, ds(b * NH, NH)], pxT[k][:, c * P:c * P + P], w_dt[:, c, :],
                                        start=c == 0, stop=c == 1)
                    last.then_inc(S["p_dt"], 1)

                transposes(0, 0)
                transposes(1, 1)
                dt_of(0, 0)
                with e.Fori(1, NB // 2) as half:
                    b = 2 * half
                    transposes(b, 0)
                    dt_of(b - 1, 1)
                    transposes(b + 1, 1)
                    dt_of(b, 0)
                dt_of(NB - 1, 1)
                e.wait_ge(S["p_nd"], 1)
                e.matmul(cum_bank[:, 0:NT], upper, pdt[3], start=True, stop=True).then_inc(S["p_cum"], 1)

            @block.scalar
            def _(e):
                def copy(b, k):
                    e.wait_ge(S["p_tr"], b + 1)
                    if past(b - 1): e.wait_ge(S["p_dt"], b - 1)
                    e.activation(pxT[k], bank[k][:, 0:D], ACT.Copy).then_inc(S["p_xnT"], 1)

                copy(0, 0)
                copy(1, 1)
                with e.Fori(1, NB // 2) as half:
                    b = 2 * half
                    copy(b, 0)
                    copy(b + 1, 1)
                e.wait_ge(S["p_min"], 1)
                e.activation(pdt[1], pdt[1], ACT.Exp).then_inc(S["p_chain"], 1)
                e.wait_ge(S["p_chain"], 1)
                e.activation(pdt[3], pdt[1], ACT.Ln, bias=const[:, C_ONE:C_ONE + 1]).then_inc(S["p_act"], 1)

        wpos[0] = rpos[0] = 0
        m_xn_ = wk(D)
        m_xT = wr(2 * D).rearrange("p (s k t) -> p s k t", s=2, k=2)
        m_raw_ = wk(XBC).rearrange("p (j t) -> p j t", t=P)
        m_acc = wk(XBC).rearrange("p (j t) -> p j t", t=P)
        m_xt_ = wk(DI)
        m_xdt_ = wk(DI)
        m_xD = m_xt_
        m_E = wk(NH * P).rearrange("p (h t) -> p h t", t=P)
        m_zg_ = wk(DI)
        m_y_ = m_raw_[:, 0:4, :].rearrange("p j t -> p (j t)")
        m_yT = wr(2 * DI).rearrange("p (s k t) -> p s k t", s=2, k=4)
        m_Gm = wk(P)
        x1 = wk(D)
        cur = tiny[:, 0:TAB]
        c_dec, c_dt = cur[:, NH:2 * NH], cur[:, 2 * NH:3 * NH]
        m_ss_, m_xh_, m_t_, m_r_ = (tiny[:, 26 + k:27 + k] for k in range(4))
        ncum = tiny[:, 80:88]
        c_cols, r_cols = stat_cols(32), stat_cols(68)
        c_xn_ = wk(D)
        c_ctx_ = wk(D)
        c_T = wr(4 * D).rearrange("p (s k t) -> p s k t", s=2, k=4)
        c_qk = wk(2 * D)
        c_rot_ = wk(2 * D)
        c_qT = wk(2 * D).rearrange("p (o k t) -> p o k t", o=2, k=2)
        c_kT_ = wk(D).rearrange("p (k t) -> p k t", k=2)
        VX = DH + 1
        c_vx = wk(HEADS * VX).rearrange("p (h d) -> p h d", d=VX)
        c_P = [wk(512), wk(512)]
        c_PT = wk(512)
        c_o_ = c_qk[:, 0:D]
        c_oT = wr(2 * D).rearrange("p (s k t) -> p s k t", s=2, k=2)
        x1b = c_xn_
        c_mx = tiny[:, 48:52]
        c_ri = tiny[:, 52:68]
        r_xn_ = wk(D)
        r_T = wr(2 * D).rearrange("p (s k t) -> p s k t", s=2, k=2)
        r_tfi_ = sb("r_tfi_", [P, 4, P])
        r_tg_ = sb("r_tg_", [P, 2, P])
        r_xo_ = sb("r_xo_", [P, D])

        def head_cols(blk, odd, g):
            return blk * NH + 2 * g + odd

        def attention_stage(pre, scale, qT, kT, vx, kv_of, Pb, PTb, mx, sc_banks, pt_bank, o_bank):
            def scores(e, b, g):
                e.wait_ge(S[pre + "_kT"], b + 1)
                e.wait_ge(S[pre + "_qT"], 2 * b + 2)
                bk = sc_banks[g % 2]
                if past(4 * b + g - 1): e.wait_ge(S[pre + "_sub"], 4 * b + g - 1)
                for blk in range(2):
                    for odd in range(2):
                        c = (2 * blk + odd) * P
                        last = e.matmul(bk[:, c:c + P], qT[32 * g:32 * g + 32, odd, blk, :],
                                        kT[32 * g:32 * g + 32, blk, :], start=True, stop=True)
                last.then_inc(S[pre + "_sc"], 1)

            def softmax(e, b, g):
                s3 = sc_banks[g % 2][:, :].rearrange("p (h k) -> p h k", k=P)
                e.wait_ge(S[pre + "_sc"], 4 * b + g + 1)
                if past(4 * b + g): e.wait_ge(S[pre + "_sub"], 4 * b + g)
                e.tensor_reduce(mx, s3, AX.X, ALU.max).then_inc(S[pre + "_max"], 1)
                e.wait_ge(S[pre + "_max"], 4 * b + g + 1)
                if past(4 * b + g - 1): e.wait_ge(S[pre + "_ptr"], 4 * b + g - 1)
                e.tensor_tensor(Pb[g % 2].rearrange("p (h k) -> p h k", k=P), s3,
                                mx.unsqueeze(2).to_broadcast([P, 4, P]), ALU.subtract).then_inc(S[pre + "_sub"], 1)

            def exponents(e, b, g):
                e.wait_ge(S[pre + "_sub"], 4 * b + g + 1)
                e.activation(Pb[g % 2], Pb[g % 2], ACT.Exp, scale=scale).then_inc(S[pre + "_exp"], 1)

            def turn(e, b, g):
                e.wait_ge(S[pre + "_exp"], 4 * b + g + 1)
                if past(4 * b + g): e.wait_ge(S[pre + "_pt"], 4 * b + g)
                for h in range(4):
                    last = e.transpose(pt_bank[:, h * P:h * P + P], Pb[g % 2][:, h * P:h * P + P], ident)
                last.then_inc(S[pre + "_ptr"], 1)

            def take(e, b, g):
                e.wait_ge(S[pre + "_ptr"], 4 * b + g + 1)
                if past(4 * b + g): e.wait_ge(S[pre + "_pv"], 4 * b + g)
                e.activation(PTb, pt_bank[:, :], ACT.Copy).then_inc(S[pre + "_pt"], 1)

            def values(e, b, g):
                e.wait_ge(S[pre + "_pt"], 4 * b + g + 1)
                if g == 0:
                    e.wait_ge(S[pre + "_v"], b + 1)
                    if past(b): e.wait_ge(S[pre + "_o"], b)
                for blk in range(2):
                    for odd in range(2):
                        h, c = head_cols(blk, odd, g), (2 * blk + odd) * P
                        last = e.matmul(o_bank[:, h * VX:h * VX + VX], PTb[:, c:c + P], vx[:, kv_of(h), :],
                                        start=True, stop=True)
                last.then_inc(S[pre + "_pv"], 1)

            def normalise(e, b, o_, ri, free, free_count):
                o3 = o_bank[:, 0:HEADS * VX].rearrange("p (h d) -> p h d", d=VX)
                e.wait_ge(S[pre + "_pv"], 4 * b + 4)
                e.reciprocal(ri, o3[:, :, DH]).then_inc(S[pre + "_rinv"], 1)
                e.wait_ge(S[pre + "_rinv"], b + 1)
                for f, c in zip(free, free_count):
                    if past(c): e.wait_ge(S[f], c)
                e.tensor_tensor(o_.rearrange("p (h d) -> p h d", d=DH), o3[:, :, 0:DH],
                                ri.unsqueeze(2).to_broadcast([P, HEADS, DH]), ALU.mult).then_inc(S[pre + "_o"], 1)

            return dict(scores=scores, softmax=softmax, exponents=exponents, turn=turn, take=take,
                        values=values, normalise=normalise)

        att0 = attention_stage("c", DH ** -0.5, c_qT, c_kT_, c_vx, lambda h: h, c_P, c_PT, c_mx,
                               [bank[3], bank[4]], bank[5], bank[6])

        with phase("layer0") as block:
            @block.sync
            def _(e):
                def step(i):
                    b = i - 1
                    if live(b):
                        if past(b): e.wait_ge(S["c_tr"], b)
                        e.dma_start(c_ctx_, ctx[b] if isinstance(b, int) else ctx[ds(b, 1)].rearrange("o t d -> t (o d)"))\
                            .then_inc(S["c_ctx"], 16)
                    b = i - 2
                    if live(b):
                        e.wait_ge(S["r_xo"], b + 1)
                        dst = xo_dram[b] if isinstance(b, int) else xo_dram[ds(b, 1)].rearrange("o t d -> t (o d)")
                        e.dma_start(dst, r_xo_[:, :]).then_inc(S["r_store"], 16)

                pipeline(e, 2, step)
                e.wait_ge(S["r_store"], 16 * NB)

            @block.tensor
            def _(e):
                def m_transpose(b):
                    e.wait_ge(S["m_xn"], b + 1)
                    if past(b): e.wait_ge(S["m_yx"], b)
                    for c in range(2):
                        last = e.transpose(bank[0][:, c * P:c * P + P], m_xn_[:, c * P:c * P + P], ident)
                    last.then_inc(S["m_tr"], 1)

                def m_project(b):
                    e.wait_ge(S["m_lo"], b + 1)
                    if past(b): e.wait_ge(S["m_ylo"], b)
                    for j in range(4):
                        project_T(e, bank[1][:, j * P:j * P + P], m_xT, w_in, DI + j * P)
                    for j in range(2):
                        last = project_T(e, bank[0][:, j * P:j * P + P], m_xT, w_in, 2 * DI + j * P)
                    last.then_inc(S["m_xbc"], 1)

                def m_gate(b):
                    if past(b): e.wait_ge(S["m_x1"], b)
                    project(e, bank[2][:, :], m_xT, w_in, 2, 0, DI).then_inc(S["m_z"], 1)

                def m_tokens(b):
                    e.wait_ge(S["m_xbcs"], b + 1)
                    for j in range(4):
                        last = e.transpose(bank[1][:, j * P:j * P + P], m_acc[:, j, :], ident)
                    last.then_inc(S["m_xtr"], 1)
                    e.matmul(bank[0][:, 0:P], m_acc[:, 4, :], m_acc[:, 5, :], start=True, stop=True)\
                        .then_inc(S["m_g"], 1)

                def m_decays(b, half):
                    e.wait_ge(S["m_cur"], 2 * b + 2)
                    if half == 0:
                        e.wait_ge(S["m_zg"], b + 1)
                    else:
                        e.wait_ge(S["m_xt"], b + 1)
                    for h in range(4):
                        for s in range(2):
                            last = e.matmul(bank[2 - half][:, h * P:h * P + P],
                                            curr[:, s, 4 * half + h:4 * half + h + 1].to_broadcast([P, P]),
                                            upper_r[:, :], start=s == 0, stop=s == 1)
                    last.then_inc(S["m_bc"], 1)

                def m_mix(b, half):
                    e.wait_ge(S["m_M"], 2 * b + 1 + half)
                    if half == 0:
                        e.wait_ge(S["m_xdt"], b + 1)
                        e.wait_ge(S["m_gm"], b + 1)
                    for h in range(4 * half, 4 * half + 4):
                        last = e.matmul(bank[0][:, h * HD:h * HD + HD], m_E[:, h, :],
                                        m_xdt_[:, h * HD:h * HD + HD], start=True, stop=True)
                    last.then_inc(S["m_y"], 1)

                def m_turn(b):
                    e.wait_ge(S["m_y2"], b + 1)
                    e.wait_ge(S["m_rela"], b + 1)
                    for c in range(4):
                        last = e.transpose(bank[1][:, c * P:c * P + P], m_y_[:, c * P:c * P + P], ident)
                    last.then_inc(S["m_ytr"], 1)

                def m_out(b):
                    e.wait_ge(S["m_ylo"], b + 1)
                    e.wait_ge(S["m_relv"], b + 1)
                    project(e, bank[2][:, 0:D], m_yT, w_out, 4, 0, D).then_inc(S["m_out"], 1)

                def c_transpose(b):
                    e.wait_ge(S["c_xn"], b + 1)
                    e.wait_ge(S["c_ctx"], 16 * (b + 1))
                    if past(4 * b): e.wait_ge(S["c_sub"], 4 * b)
                    for c in range(4):
                        src = (c_xn_ if c < 2 else c_ctx_)[:, (c % 2) * P:(c % 2) * P + P]
                        last = e.transpose(bank[3][:, c * P:c * P + P], src, ident)
                    last.then_inc(S["c_tr"], 1)

                def c_project(b):
                    e.wait_ge(S["c_lo"], b + 1)
                    if past(b): e.wait_ge(S["c_x2"], b)
                    if past(b): e.wait_ge(S["c_olo"], b)
                    project(e, bank[4][:, 0:D], c_T[:, :, 0:2, :], w_cq, 2, 0, D).then_inc(S["c_q"], 1)
                    project(e, bank[5][:, :], c_T[:, :, 2:4, :], w_ckv, 2, 0, 2 * D).then_inc(S["c_kv"], 1)

                def c_turn_qk(b):
                    e.wait_ge(S["c_qr"], b + 1)
                    for c in range(4):
                        last = e.transpose(bank[3][:, c * P:c * P + P], c_rot_[:, c * P:c * P + P], ident)
                    last.then_inc(S["c_qtr"], 1)

                def c_turn_o(b):
                    e.wait_ge(S["c_o"], b + 1)
                    e.wait_ge(S["c_pt"], 4 * b + 4)
                    for c in range(2):
                        last = e.transpose(bank[5][:, c * P:c * P + P], c_o_[:, c * P:c * P + P], ident)
                    last.then_inc(S["c_otr"], 1)

                def c_out(b):
                    e.wait_ge(S["c_olo"], b + 1)
                    e.wait_ge(S["c_sub"], 4 * b + 4)
                    project(e, bank[4][:, 0:D], c_oT, w_co, 2, 0, D).then_inc(S["c_proj"], 1)

                def r_transpose(b):
                    e.wait_ge(S["r_xn"], b + 1)
                    if past(b): e.wait_ge(S["r_xo"], b)
                    if past(2 * b): e.wait_ge(S["r_tg"], 2 * b)
                    for c in range(2):
                        last = e.transpose(bank[7][:, c * P:c * P + P], r_xn_[:, c * P:c * P + P], ident)
                    last.then_inc(S["r_tr"], 1)

                def r_forget_input(b):
                    e.wait_ge(S["r_lo"], b + 1)
                    if past(b): e.wait_ge(S["r_dlo"], b)
                    for j in range(4):
                        project_T(e, bank[7][:, j * P:j * P + P], r_T, w_rx, j * P, True, False)
                        last = project_T(e, bank[7][:, j * P:j * P + P], d_parts[:, :, :, :], w_ru, j * P, False, True)
                    last.then_inc(S["r_fi"], 1)

                def r_candidate_out(b):
                    e.wait_ge(S["r_tfi"], 4 * b + 4)
                    for j in range(2):
                        n = 2 * D + j * P
                        project_T(e, bank[7][:, j * P:j * P + P], r_T, w_rx, n, True, False)
                        project_T(e, bank[7][:, j * P:j * P + P], d_parts[:, :, :, :], w_ru, n, False, True)
                    project(e, bank[7][:, D:2 * D], r_T, w_rxo, 2, 0, D).then_inc(S["r_go"], 1)

                def step(i):
                    m, c, r = i, i - 1, i - 2
                    if live(m):
                        m_transpose(m)
                    if live(c):
                        c_transpose(c)
                    if live(r):
                        r_transpose(r)
                    if live(m):
                        m_project(m)
                    if live(c):
                        c_project(c)
                    if live(m):
                        m_gate(m)
                    if live(r):
                        r_forget_input(r)
                    if live(c):
                        c_turn_qk(c)
                        att0["scores"](e, c, 0)
                        att0["scores"](e, c, 1)
                    if live(r):
                        r_candidate_out(r)
                    if live(m):
                        m_tokens(m)
                        m_decays(m, 0)
                    if live(c):
                        att0["turn"](e, c, 0)
                        att0["scores"](e, c, 2)
                    if live(m):
                        m_decays(m, 1)
                    if live(c):
                        att0["values"](e, c, 0)
                        att0["turn"](e, c, 1)
                        att0["scores"](e, c, 3)
                        att0["values"](e, c, 1)
                        att0["turn"](e, c, 2)
                    if live(m):
                        m_mix(m, 0)
                        m_mix(m, 1)
                    if live(c):
                        att0["values"](e, c, 2)
                        att0["turn"](e, c, 3)
                        att0["values"](e, c, 3)
                    if live(m):
                        m_turn(m)
                    if live(c):
                        c_turn_o(c)
                    if live(m):
                        m_out(m)
                    if live(c):
                        c_out(c)

                pipeline(e, 2, step)

            @block.scalar
            def _(e):
                def hi(pre, b, dst, src, free=None):
                    e.wait_ge(S[pre + "_tr"], b + 1)
                    if free and past(free[1]): e.wait_ge(S[free[0]], free[1])
                    e.activation(dst, src, ACT.Copy).then_inc(S[pre + "_hi"], 1)

                def m_taps(b):
                    e.wait_ge(S["m_xbc"], b + 1)
                    if past(b): e.wait_ge(S["m_xbcs"], b)
                    if past(b): e.wait_ge(S["m_ytr"], b)
                    e.activation(m_raw_[:, 0:4, :], bank[1][:, :].rearrange("p (j t) -> p j t", t=P), ACT.Copy)
                    e.activation(m_raw_[:, 4:6, :], bank[0][:, 0:2 * P].rearrange("p (j t) -> p j t", t=P), ACT.Copy)\
                        .then_inc(S["m_raw"], 1)
                    e.wait_ge(S["m_raw"], b + 1)
                    if past(b): e.wait_ge(S["m_g"], b)
                    if past(b): e.wait_ge(S["m_xtr"], b)
                    for j in range(6):
                        last = e.activation(m_acc[:, j, :], m_raw_[:, j, :], ACT.Identity,
                                            bias=cb[:, j:j + 1], scale=cw[:, j, CONV - 1:CONV])
                    last.then_inc(S["m_tap"], 1)

                def m_gate(b):
                    e.wait_ge(S["m_z"], b + 1)
                    if past(b): e.wait_ge(S["m_y2"], b)
                    e.activation(m_zg_, bank[2][:, :], ACT.Tanh, scale=0.5).then_inc(S["m_ztanh"], 1)

                def m_silu(b):
                    e.wait_ge(S["m_conv"], b + 1)
                    e.activation(m_raw_, m_acc, ACT.Tanh).then_inc(S["m_xtanh"], 1)

                def m_tokens(b):
                    e.wait_ge(S["m_xtr"], b + 1)
                    if past(b): e.wait_ge(S["m_yx"], b)
                    if past(b): e.wait_ge(S["m_xdt"], b)
                    e.activation(m_xt_, bank[1][:, :], ACT.Copy).then_inc(S["m_xt"], 1)

                def m_exp(b, half):
                    if half == 1:
                        e.wait_ge(S["m_bc"], 2 * b + 2)
                        e.wait_ge(S["m_cur"], 2 * b + 2)
                        if past(2 * b): e.wait_ge(S["m_y"], 2 * b)
                        for h in range(4, 8):
                            last = e.activation(m_E[:, h, :], bank[1][:, (h - 4) * P:(h - 3) * P], ACT.Relu,
                                                bias=ncum[:, h:h + 1])
                        last.then_inc(S["m_rela"], 1)
                        e.wait_ge(S["m_rela"], b + 1)
                    else:
                        e.wait_ge(S["m_relv"], b + 1)
                    e.activation(m_E[:, 4 * half:4 * half + 4, :], m_E[:, 4 * half:4 * half + 4, :], ACT.Exp,
                                 scale=-1.0).then_inc(S["m_exp"], 1)

                def m_square(b):
                    e.wait_ge(S["m_y2"], b + 1)
                    if past(12 * b): e.wait_ge(S["m_rs"], 12 * b)
                    e.activation(m_E[:, 0:4, :].rearrange("p h t -> p (h t)"), m_y_, ACT.Square, accum_out=m_ss_)\
                        .then_inc(S["m_ss"], 1)

                def m_yhi(b):
                    e.wait_ge(S["m_ytr"], b + 1)
                    if past(b): e.wait_ge(S["m_out"], b)
                    e.activation(m_yT[:, 0], bank[1][:, :].rearrange("p (k t) -> p k t", t=P), ACT.Copy)\
                        .then_inc(S["m_yhi"], 1)

                def c_values(b):
                    e.wait_ge(S["c_kb"], b + 1)
                    if past(4 * b): e.wait_ge(S["c_pv"], 4 * b)
                    e.activation(c_vx[:, :, 0:DH], bank[5][:, D:2 * D].rearrange("p (h d) -> p h d", d=DH), ACT.Copy)\
                        .then_inc(S["c_v"], 1)

                def c_heads(b):
                    e.wait_ge(S["c_qtr"], b + 1)
                    if past(4 * b): e.wait_ge(S["c_sc"], 4 * b)
                    e.activation(c_kT_, bank[3][:, D:2 * D].rearrange("p (k t) -> p k t", k=2), ACT.Copy)\
                        .then_inc(S["c_kT"], 1)
                    for odd, mask in enumerate((m_even, m_odd)):
                        e.activation(c_qT[:, odd], bank[3][:, 0:D].rearrange("p (k t) -> p k t", k=2),
                                     ACT.Copy, scale=mask).then_inc(S["c_qT"], 1)

                def c_ohi(b):
                    e.wait_ge(S["c_otr"], b + 1)
                    if past(b): e.wait_ge(S["c_proj"], b)
                    e.activation(c_oT[:, 0], bank[5][:, 0:D].rearrange("p (k t) -> p k t", k=2), ACT.Copy)\
                        .then_inc(S["c_ohi"], 1)

                def r_gates(b):
                    e.wait_ge(S["r_fi"], b + 1)
                    if past(b): e.wait_ge(S["r_d"], b)
                    for j in range(4):
                        e.activation(r_tfi_[:, j, :], bank[7][:, j * P:j * P + P], ACT.Tanh, scale=0.5,
                                     bias=gb[:, j:j + 1]).then_inc(S["r_tfi"], 1)

                def r_candidate(b):
                    e.wait_ge(S["r_go"], b + 1)
                    for j in range(2):
                        e.activation(r_tg_[:, j, :], bank[7][:, j * P:j * P + P], ACT.Tanh,
                                     bias=gb[:, 4 + j:5 + j]).then_inc(S["r_tg"], 1)
                    if past(16 * b): e.wait_ge(S["r_store"], 16 * b)
                    e.activation(r_xo_[:, :], bank[7][:, D:2 * D], ACT.Copy).then_inc(S["r_xo"], 1)

                def r_state_hi(b):
                    e.wait_ge(S["r_d"], b + 1)
                    e.wait_ge(S["r_go"], b + 1)
                    e.activation(d_parts[:, 0], d_state[:, :, :], ACT.Copy).then_inc(S["r_dhi"], 1)

                def step(i):
                    m, c, r = i, i - 1, i - 2
                    if live(m):
                        hi("m", m, m_xT[:, 0], bank[0][:, 0:D].rearrange("p (k t) -> p k t", k=2), ("m_z", m))
                    if live(c):
                        hi("c", c, c_T[:, 0], bank[3][:, :].rearrange("p (k t) -> p k t", k=4), ("c_kv", c))
                    if live(r):
                        hi("r", r, r_T[:, 0], bank[7][:, 0:D].rearrange("p (k t) -> p k t", k=2), ("r_go", r))
                    if live(m):
                        m_taps(m)
                    if live(c):
                        c_values(c)
                    if live(m):
                        m_gate(m)
                    if live(r):
                        r_gates(r)
                    if live(c):
                        c_heads(c)
                    if live(m):
                        m_silu(m)
                    if live(c):
                        att0["exponents"](e, c, 0)
                    if live(r):
                        r_candidate(r)
                    if live(m):
                        m_tokens(m)
                    if live(c):
                        att0["take"](e, c, 0)
                        att0["exponents"](e, c, 1)
                    if live(m):
                        m_exp(m, 0)
                        m_exp(m, 1)
                    if live(r):
                        r_state_hi(r)
                    if live(c):
                        att0["take"](e, c, 1)
                        att0["exponents"](e, c, 2)
                        att0["take"](e, c, 2)
                        att0["exponents"](e, c, 3)
                        att0["take"](e, c, 3)
                    if live(m):
                        m_square(m)
                        m_yhi(m)
                    if live(c):
                        c_ohi(c)

                pipeline(e, 2, step)

            @block.vector
            def _(e):
                def lo(pre, b, dst, src, high):
                    e.wait_ge(S[pre + "hi"], b + 1)
                    e.tensor_tensor(dst, src, high.bitcast(F32), ALU.subtract).then_inc(S[pre + "lo"], 1)

                def apply_norm(pre, b, dst, src, mean, rstd):
                    e.tensor_scalar(dst, src, mean, rstd, ALU.subtract, ALU.mult).then_inc(S[pre + "_xn"], 1)

                def m_current(b):
                    if past(2 * b): e.wait_ge(S["m_bc"], 2 * b)
                    if past(b): e.wait_ge(S["m_xdt"], b)
                    if past(b): e.wait_ge(S["m_rela"], b)
                    e.tensor_scalar(curr[:, 0, :], tab[:, ds(b * TAB, NH)], 1.0, None, ALU.mult)
                    e.tensor_scalar(ncum, tab[:, ds(b * TAB + NH, NH)], -1.0, None, ALU.mult)
                    e.tensor_scalar(cur, tab[:, ds(b * TAB, TAB)], 1.0, None, ALU.mult).then_inc(S["m_cur"], 1)
                    e.wait_ge(S["m_cur"], 2 * b + 1)
                    e.tensor_tensor(curr[:, 1, :], cur[:, 0:NH], curr[:, 0, :].bitcast(F32), ALU.subtract)\
                        .then_inc(S["m_cur"], 1)
                    if past(b): e.wait_ge(S["m_tr"], b)
                    apply_norm("m", b, m_xn_, x_res[:, ds(b * D, D)], cur[:, 3 * NH:3 * NH + 1],
                               cur[:, 3 * NH + 1:3 * NH + 2])

                def m_convolve(b):
                    e.wait_ge(S["m_tap"], b + 1)
                    for k in range(1, CONV):
                        if k > 1:
                            e.wait_ge(S["m_conv2"], 2 * b + k - 1)
                        for j in range(6):
                            last = e.scalar_tensor_tensor(
                                out=m_acc[:, j, k:P], in0=m_raw_[:, j, 0:P - k],
                                scalar=cw[:, j, CONV - 1 - k:CONV - k], in1=m_acc[:, j, k:P],
                                op0=ALU.mult, op1=ALU.add)
                        last.then_inc(S["m_conv2" if k < CONV - 1 else "m_conv"], 1)

                def m_silu(b):
                    e.wait_ge(S["m_xtanh"], b + 1)
                    e.scalar_tensor_tensor(out=m_acc, in0=m_raw_, scalar=1.0, in1=m_acc,
                                           op0=ALU.add, op1=ALU.mult).then_inc(S["m_xbcs"], 1)

                def m_gate(b):
                    e.wait_ge(S["m_ztanh"], b + 1)
                    e.scalar_tensor_tensor(out=m_zg_, in0=m_zg_, scalar=1.0, in1=bank[2][:, :],
                                           op0=ALU.add, op1=ALU.mult).then_inc(S["m_zg"], 1)

                def m_masked(b):
                    e.wait_ge(S["m_g"], b + 1)
                    e.tensor_tensor(m_Gm, bank[0][:, 0:P], upper, ALU.mult).then_inc(S["m_gm"], 1)

                def m_relative(b):
                    e.wait_ge(S["m_bc"], 2 * b + 1)
                    if past(2 * b): e.wait_ge(S["m_y"], 2 * b)
                    for h in range(4):
                        last = e.tensor_scalar(m_E[:, h, :], bank[2][:, h * P:h * P + P], c_dec[:, h:h + 1], 0.0,
                                               ALU.subtract, ALU.max)
                    last.then_inc(S["m_relv"], 1)

                def m_weights(b, half):
                    e.wait_ge(S["m_exp"], 2 * b + 1 + half)
                    part = m_E[:, 4 * half:4 * half + 4, :]
                    if half == 0:
                        e.wait_ge(S["m_gm"], b + 1)
                    e.tensor_tensor(part, part, m_Gm.unsqueeze(1).to_broadcast([P, 4, P]), ALU.mult)\
                        .then_inc(S["m_M"], 1)

                def m_gated(b):
                    e.wait_ge(S["m_y"], 2 * b + 2)
                    e.wait_ge(S["m_xd"], b + 1)
                    if past(b): e.wait_ge(S["m_ytr"], b)
                    e.tensor_tensor(m_y_, bank[0][:, :], m_xD, ALU.add).then_inc(S["m_yx"], 1)
                    e.wait_ge(S["m_yx"], b + 1)
                    e.tensor_tensor(m_y_, m_y_, m_zg_, ALU.mult).then_inc(S["m_y2"], 1)

                def m_root(b):
                    e.wait_ge(S["m_ss"], b + 1)
                    e.tensor_scalar(m_ss_, m_ss_, float(4 * DI * EPS), None, ALU.add).then_inc(S["m_seed"], 1)
                    if past(b): e.wait_ge(S["m_x1"], b)
                    rsqrt_seed(e, m_ss_, m_xh_, m_t_, m_r_, "m_seed", b)

                def m_ylow(b):
                    e.wait_ge(S["m_yhi"], b + 1)
                    e.tensor_tensor(m_yT[:, 1], bank[1][:, :].rearrange("p (k t) -> p k t", t=P),
                                    m_yT[:, 0].bitcast(F32), ALU.subtract).then_inc(S["m_ylo"], 1)

                def m_residual(b):
                    e.wait_ge(S["m_out"], b + 1)
                    e.wait_ge(S["m_rs"], 12 * b + 12)
                    if past(b): e.wait_ge(S["c_x1b"], b)
                    e.scalar_tensor_tensor(out=x1, in0=bank[2][:, 0:D], scalar=m_r_, in1=x_res[:, ds(b * D, D)],
                                           op0=ALU.mult, op1=ALU.add).then_inc(S["m_x1"], 1)

                def c_norm(b):
                    e.wait_ge(S["c_rs"], 12 * b + 12)
                    if past(b): e.wait_ge(S["c_x2"], b)
                    apply_norm("c", b, c_xn_, x1, c_cols[1][:, 0:1], c_cols[5])

                def c_bias(b):
                    e.wait_ge(S["c_kv"], b + 1)
                    if past(b): e.wait_ge(S["c_otr"], b)
                    e.tensor_tensor(c_qk[:, D:2 * D], bank[5][:, 0:D], bqk_row[:, D:2 * D], ALU.add)\
                        .then_inc(S["c_kb"], 1)
                    e.tensor_tensor(c_qk[:, 0:D], bank[4][:, 0:D], bqk_row[:, 0:D], ALU.add).then_inc(S["c_qb"], 1)

                def c_rotate(b):
                    e.wait_ge(S["c_rot"], b + 1)
                    e.tensor_tensor(c_qk.rearrange("p (h d) -> p h d", d=DH), c_qk.rearrange("p (h d) -> p h d", d=DH),
                                    const[:, C_COS:C_COS + DH].unsqueeze(1).to_broadcast([P, 2 * HEADS, DH]),
                                    ALU.mult).then_inc(S["c_cos"], 1)
                    e.wait_ge(S["c_cos"], b + 1)
                    e.tensor_tensor(c_rot_, c_rot_, c_qk, ALU.add).then_inc(S["c_qr"], 1)

                def c_residual(b):
                    e.wait_ge(S["c_proj"], b + 1)
                    e.wait_ge(S["c_x1b"], b + 1)
                    e.tensor_tensor(x_res[:, ds(b * D, D)], bank[4][:, 0:D], x1b, ALU.add).then_inc(S["c_x2"], 1)

                def r_norm(b):
                    e.wait_ge(S["r_rs"], 12 * b + 12)
                    if past(b): e.wait_ge(S["r_tr"], b)
                    apply_norm("r", b, r_xn_, x_res[:, ds(b * D, D)], r_cols[1][:, 0:1], r_cols[5])

                def r_update(b):
                    e.wait_ge(S["r_tfi"], 4 * b + 4)
                    if past(b): e.wait_ge(S["r_dhi"], b)
                    e.scalar_tensor_tensor(out=r_tfi_[:, 0:2, :], in0=r_tfi_[:, 0:2, :], scalar=1.0,
                                           in1=d_state[:, :, :], op0=ALU.add, op1=ALU.mult).then_inc(S["r_a"], 1)
                    e.wait_ge(S["r_tg"], 2 * b + 2)
                    e.scalar_tensor_tensor(out=r_tfi_[:, 2:4, :], in0=r_tfi_[:, 2:4, :], scalar=1.0,
                                           in1=r_tg_[:, :, :], op0=ALU.add, op1=ALU.mult).then_inc(S["r_b"], 1)
                    e.wait_ge(S["r_b"], b + 1)
                    e.scalar_tensor_tensor(out=d_state[:, :, :], in0=r_tfi_[:, 0:2, :], scalar=0.5,
                                           in1=r_tfi_[:, 2:4, :], op0=ALU.mult, op1=ALU.add)\
                        .then_inc(S["r_d"], 1)

                def r_state_lo(b):
                    e.wait_ge(S["r_dhi"], b + 1)
                    e.tensor_tensor(d_parts[:, 1], d_state[:, :, :], d_parts[:, 0].bitcast(F32), ALU.subtract)\
                        .then_inc(S["r_dlo"], 1)

                e.memset(c_vx[:, :, DH:VX], 1.0)

                def step(i):
                    m, c, r = i, i - 1, i - 2
                    if live(m):
                        m_current(m)
                    if live(c):
                        c_norm(c)
                    if live(r):
                        r_norm(r)
                    if live(m):
                        lo("m_", m, m_xT[:, 1], bank[0][:, 0:D].rearrange("p (k t) -> p k t", k=2), m_xT[:, 0])
                    if live(c):
                        lo("c_", c, c_T[:, 1], bank[3][:, :].rearrange("p (k t) -> p k t", k=4), c_T[:, 0])
                    if live(r):
                        lo("r_", r, r_T[:, 1], bank[7][:, 0:D].rearrange("p (k t) -> p k t", k=2), r_T[:, 0])
                    if live(c):
                        c_bias(c)
                    if live(m):
                        m_convolve(m)
                    if live(c):
                        c_rotate(c)
                    if live(m):
                        m_gate(m)
                        m_silu(m)
                    if live(c):
                        att0["softmax"](e, c, 0)
                        att0["softmax"](e, c, 1)
                    if live(r):
                        r_update(r)
                    if live(m):
                        m_masked(m)
                        m_relative(m)
                    if live(c):
                        att0["softmax"](e, c, 2)
                    if live(m):
                        m_weights(m, 0)
                        m_weights(m, 1)
                    if live(r):
                        r_state_lo(r)
                    if live(c):
                        att0["softmax"](e, c, 3)
                    if live(m):
                        m_gated(m)
                        m_root(m)
                    if live(c):
                        att0["normalise"](e, c, c_o_, c_ri, ["c_otr"], [c])
                    if live(m):
                        m_ylow(m)
                    if live(c):
                        lo("c_o", c, c_oT[:, 1], bank[5][:, 0:D].rearrange("p (k t) -> p k t", k=2), c_oT[:, 0])
                    if live(m):
                        m_residual(m)
                        row_statistics(e, "c", m, x1, c_cols, ("m_x1", m + 1))
                    if live(c):
                        c_residual(c)
                        row_statistics(e, "r", c, x_res[:, ds(c * D, D)], r_cols, ("c_x2", c + 1))

                pipeline(e, 2, step)

            @block.gpsimd
            def _(e):
                def scale_tokens(b):
                    x3 = m_xt_.rearrange("p (h d) -> p h d", d=HD)
                    e.wait_ge(S["m_xt"], b + 1)
                    e.wait_ge(S["m_cur"], 2 * b + 2)
                    if past(2 * b): e.wait_ge(S["m_y"], 2 * b)
                    e.tensor_tensor(m_xdt_.rearrange("p (h d) -> p h d", d=HD), x3,
                                    c_dt.unsqueeze(2).to_broadcast([P, NH, HD]), ALU.mult).then_inc(S["m_xdt"], 1)
                    e.wait_ge(S["m_xdt"], b + 1)
                    e.tensor_tensor(m_xD.rearrange("p (h d) -> p h d", d=HD), x3,
                                    dpar.unsqueeze(2).to_broadcast([P, NH, HD]), ALU.mult).then_inc(S["m_xd"], 1)

                def rotate(b):
                    e.wait_ge(S["c_kb"], b + 1)
                    e.wait_ge(S["c_qb"], b + 1)
                    if past(b): e.wait_ge(S["c_qtr"], b)
                    e.tensor_tensor(c_rot_.rearrange("p (h o d) -> p h o d", o=2, d=DH // 2),
                                    c_qk.rearrange("p (h o d) -> p h o d", o=2, d=DH // 2)[:, :, ::-1, :],
                                    const[:, C_SIN:C_SIN + DH].rearrange("p (o d) -> p o d", o=2).unsqueeze(1)
                                    .to_broadcast([P, 2 * HEADS, 2, DH // 2]), ALU.mult).then_inc(S["c_rot"], 1)

                def add_bias(b):
                    e.wait_ge(S["c_tr"], b + 1)
                    e.tensor_tensor(x1b, x1, bo2_row, ALU.add).then_inc(S["c_x1b"], 1)

                def newton(pre, b, xh_, t_, y_):
                    e.wait_ge(S[pre + "_seed"], 3 * b + 3)
                    rsqrt_newton(e, xh_, t_, y_, pre + "_rs", 12 * b)

                def step(i):
                    m, c, r = i, i - 1, i - 2
                    if live(c):
                        add_bias(c)
                        rotate(c)
                    if live(m):
                        scale_tokens(m)
                        newton("m", m, m_xh_, m_t_, m_r_)
                        newton("c", m, *c_cols[3:])
                    if live(c):
                        newton("r", c, *r_cols[3:])

                pipeline(e, 2, step)

        v_row, dbv_row = rows[:, 0:D], rows[:, D:2 * D]
        NQ = D + 2 * KV * DH
        qkv_stage = work[:, 0:2 * NQ].rearrange("p (k n) -> p k n", k=2)
        so_stage = work[:, 768:768 + 2 * D].rearrange("p (k n) -> p k n", k=2)
        gate_stage = work[0:E, 1280:1280 + D]
        jobs1 = []
        for r in range(2):
            jobs1 += [(uo[r * P:(r + 1) * P, :], D, to(w_uo, r * P), 0.5, None),
                      (d_Wq[r * P:(r + 1) * P, :], D, to(w_dq, r * P), 1.0, None),
                      (d_Wk[r * P:(r + 1) * P, :], D, to(w_dk, r * P), 1.0, None),
                      (d_Wv[r * P:(r + 1) * P, :], D, to(w_dv, r * P), 1.0, None)]
        w1 = weights("w1", 4, work[:, 2048:4096], jobs1)
        with phase("between") as block:
            @block.sync
            def _(e):
                for dst, src in ((qkv_stage[:, :, 0:D], s_wq.rearrange("(k p) n -> p k n", p=P)),
                                 (qkv_stage[:, :, D:D + KV * DH], s_wk.rearrange("(k p) n -> p k n", p=P)),
                                 (qkv_stage[:, :, D + KV * DH:NQ], s_wv.rearrange("(k p) n -> p k n", p=P)),
                                 (so_stage, s_wo.rearrange("(k p) n -> p k n", p=P)),
                                 (gcol, s_g.rearrange("(j p) -> p j", p=P)),
                                 (dbq, d_bq.rearrange("(j p) -> p j", p=P)),
                                 (dbk, d_bk.rearrange("(j p) -> p j", p=P)),
                                 (dbv_row, d_bv.partition_broadcast(P)), (lbb, lb_bias.partition_broadcast(P)),
                                 (gate_stage, gate_w)):
                    with nc.allow_non_contiguous_dma(reason="small vectors, once"):
                        e.dma_start(dst, src).then_inc(S["l1_small"], 16)
                w1[0](e)

            @block.tensor
            def _(e):
                w1[1](e)
                e.wait_ge(S["l1_small"], 160)
                for c in range(2):
                    last = e.transpose(bank[4][:, c * E:c * E + E], gate_stage[:, c * P:c * P + P], ident[0:E, 0:E])
                last.then_inc(S["w1_tr"], 1)
                e.wait_ge(S["w1_lo"], len(jobs1))
                project(e, bank[5][:, 0:D], d_parts[:, :, :, :], w_uo, 2, 0, D).then_inc(S["b_v"], 1)

            @block.scalar
            def _(e):
                w1[2](e)
                e.wait_ge(S["w1_tr"], len(jobs1) + 1)
                e.activation(w_gate[:, :, :], bank[4][:, 0:2 * E].rearrange("p (k n) -> p k n", k=2), ACT.Copy)\
                    .then_inc(S["b_dhi"], 1)
                e.wait_ge(S["l1_wg"], 1)
                e.activation(w_sqkv[:, 0], qkv_stage, ACT.Copy).then_inc(S["l1_whi"], 1)
                e.activation(w_so[:, 0], so_stage, ACT.Copy).then_inc(S["l1_whi"], 1)

            @block.vector
            def _(e):
                e.wait_ge(S["l1_small"], 160)
                for k in range(2):
                    last = e.tensor_scalar(qkv_stage[:, k, :], qkv_stage[:, k, :], gcol[:, k:k + 1], None, ALU.mult)
                last.then_inc(S["l1_wg"], 1)
                w1[3](e)
                e.wait_ge(S["l1_whi"], 2)
                e.tensor_tensor(w_sqkv[:, 1], qkv_stage, w_sqkv[:, 0].bitcast(F32), ALU.subtract)
                e.tensor_tensor(w_so[:, 1], so_stage, w_so[:, 0].bitcast(F32), ALU.subtract).then_inc(S["l1_wlo"], 1)
                e.wait_ge(S["b_v"], 1)
                e.tensor_tensor(v_row, bank[5][:, 0:D], bo_row, ALU.add).then_inc(S["b_vrow"], 1)

        wpos[0] = rpos[0] = 0
        s_xo_ = wk(D)
        s_h_ = wk(D)
        s_x3_ = wk(D)
        s_xn_ = wk(D)
        s_T = wr(2 * D).rearrange("p (s k t) -> p s k t", s=2, k=2)
        NR = D + 2 * KV * DH
        s_qr_ = wk(NR)
        s_qT_ = wk(2 * D).rearrange("p (o k t) -> p o k t", o=2, k=2)
        s_kT_ = wk(P)
        s_vx = wk(KV * VX).rearrange("p (h d) -> p h d", d=VX)
        s_P = [wk(512), wk(512)]
        s_PT = wk(512)
        s_o_ = wk(D)
        s_oT = wr(2 * D).rearrange("p (s k t) -> p s k t", s=2, k=2)
        s_mx, s_ri = tiny[:, 0:4], tiny[:, 4:20]

        s_cols, d_cols, g_cols = stat_cols(20), stat_cols(32), stat_cols(44)
        x4 = wk(D)
        d_xn_ = wk(D)
        d_ctx_ = wk(D)
        d_T = wr(4 * D).rearrange("p (s k t) -> p s k t", s=2, k=4)
        d_qkT = wk(4 * P).rearrange("p (k t) -> p k t", k=4)
        d_v_ = wk(D)
        d_P_ = wk(P)
        d_PT = wk(P)
        d_mx, d_nm, d_sum, d_ri = (tiny[:, 56 + k:57 + k] for k in range(4))
        g_xn_ = wk(D)
        g_T = wk(D)
        g_mr = tiny[:, 60:62]

        att1 = attention_stage("s", 1.0 / float(np.sqrt(D)), s_qT_, s_kT_.unsqueeze(1).to_broadcast([P, 2, P]),
                               s_vx, lambda h: h % KV, s_P, s_PT, s_mx, [bank[2], bank[3]], bank[4], bank[1])

        with phase("layer1") as block:
            @block.sync
            def _(e):
                def step(i):
                    if live(i):
                        if past(i): e.wait_ge(S["s_u"], i)
                        e.dma_start(s_xo_, xo_dram[i] if isinstance(i, int) else
                                    xo_dram[ds(i, 1)].rearrange("o t d -> t (o d)")).then_inc(S["s_xo"], 16)
                    b = i - 2
                    if live(b):
                        if past(b): e.wait_ge(S["d_tr"], b)
                        e.dma_start(d_ctx_, ctx[b] if isinstance(b, int) else
                                    ctx[ds(b, 1)].rearrange("o t d -> t (o d)")).then_inc(S["d_ctx"], 16)

                pipeline(e, 3, step)

            @block.tensor
            def _(e):
                def s_transpose(b):
                    e.wait_ge(S["s_xn"], b + 1)
                    if past(b): e.wait_ge(S["s_olo"], b)
                    for c in range(2):
                        last = e.transpose(bank[0][:, c * P:c * P + P], s_xn_[:, c * P:c * P + P], ident)
                    last.then_inc(S["s_tr"], 1)

                def s_project(b):
                    e.wait_ge(S["s_lo"], b + 1)
                    if past(b): e.wait_ge(S["s_x4"], b)
                    project(e, bank[1][:, 0:NQ], s_T, w_sqkv, 2, 0, NQ).then_inc(S["s_qkv"], 1)

                def s_turn_qk(b):
                    e.wait_ge(S["s_qr"], 2 * b + 2)
                    for c in range(3):
                        last = e.transpose(bank[0][:, c * P:c * P + P], s_qr_[:, c * P:c * P + P], ident)
                    last.then_inc(S["s_qtr"], 1)

                def s_turn_o(b):
                    e.wait_ge(S["s_o"], b + 1)
                    for c in range(2):
                        last = e.transpose(bank[0][:, c * P:c * P + P], s_o_[:, c * P:c * P + P], ident)
                    last.then_inc(S["s_otr"], 1)

                def s_out(b):
                    e.wait_ge(S["s_olo"], b + 1)
                    project(e, bank[1][:, 0:D], s_oT, w_so, 2, 0, D).then_inc(S["s_proj"], 1)

                def d_transpose(b):
                    e.wait_ge(S["d_xn"], b + 1)
                    e.wait_ge(S["d_ctx"], 16 * (b + 1))
                    if past(b): e.wait_ge(S["d_qk_sb"], b)
                    for c in range(4):
                        src = (d_xn_ if c < 2 else d_ctx_)[:, (c % 2) * P:(c % 2) * P + P]
                        last = e.transpose(bank[5][:, c * P:c * P + P], src, ident)
                    last.then_inc(S["d_tr"], 1)

                def d_project(b):
                    e.wait_ge(S["d_lo"], b + 1)
                    for c in range(4):
                        last = project_T(e, bank[5][:, c * P:c * P + P], d_T[:, :, 2 * (c // 2):2 * (c // 2) + 2, :],
                                         w_dq if c < 2 else w_dk, (c % 2) * P)
                    last.then_inc(S["d_qk"], 1)
                    if past(b): e.wait_ge(S["d_x5"], b)
                    project(e, bank[6][:, 0:D], d_T[:, :, 2:4, :], w_dv, 2, 0, D).then_inc(S["d_vmm"], 1)

                def d_scores(b):
                    e.wait_ge(S["d_qk_sb"], b + 1)
                    e.wait_ge(S["d_v"], b + 1)
                    for k in range(2):
                        last = e.matmul(bank[6][:, 0:P], d_qkT[:, k, :], d_qkT[:, 2 + k, :], start=k == 0, stop=k == 1)
                    last.then_inc(S["d_sc"], 1)

                def d_turn(b):
                    e.wait_ge(S["d_exp"], b + 1)
                    e.transpose(bank[6][:, 0:P], d_P_, ident).then_inc(S["d_ptr"], 1)

                def d_values(b):
                    e.wait_ge(S["d_pt"], b + 1)
                    e.matmul(bank[6][:, 0:D], d_PT, d_v_, start=True, stop=True).then_inc(S["d_pv"], 1)

                def g_transpose(b):
                    e.wait_ge(S["g_xn"], b + 1)
                    if past(b): e.wait_ge(S["g_lg"], b)
                    for c in range(2):
                        last = e.transpose(bank[7][:, c * P:c * P + P], g_xn_[:, c * P:c * P + P], ident)
                    last.then_inc(S["g_tr"], 1)

                def g_logits(b):
                    e.wait_ge(S["g_xnT"], b + 1)
                    for c in range(2):
                        last = e.matmul(bank[7][:, D:D + E], g_T[:, c * P:c * P + P], w_gate[:, c, :],
                                        start=c == 0, stop=c == 1)
                    last.then_inc(S["g_sum"], 1)

                def step(i):
                    s, d, g = i - 1, i - 2, i - 3
                    if live(s):
                        s_transpose(s)
                    if live(d):
                        d_transpose(d)
                    if live(g):
                        g_transpose(g)
                    if live(s):
                        s_project(s)
                    if live(d):
                        d_project(d)
                    if live(s):
                        s_turn_qk(s)
                    if live(g):
                        g_logits(g)
                    if live(s):
                        att1["scores"](e, s, 0)
                        att1["scores"](e, s, 1)
                    if live(d):
                        d_scores(d)
                    if live(s):
                        att1["turn"](e, s, 0)
                        att1["scores"](e, s, 2)
                        att1["values"](e, s, 0)
                    if live(d):
                        d_turn(d)
                    if live(s):
                        att1["turn"](e, s, 1)
                        att1["scores"](e, s, 3)
                        att1["values"](e, s, 1)
                        att1["turn"](e, s, 2)
                    if live(d):
                        d_values(d)
                    if live(s):
                        att1["values"](e, s, 2)
                        att1["turn"](e, s, 3)
                        att1["values"](e, s, 3)
                        s_turn_o(s)
                        s_out(s)

                pipeline(e, 3, step)

            @block.scalar
            def _(e):
                def copy(ready, count, dst, src, done, free=None):
                    if past(count): e.wait_ge(S[ready], count)
                    if free and past(free[1]): e.wait_ge(S[free[0]], free[1])
                    e.activation(dst, src, ACT.Copy).then_inc(S[done], 1)

                def blocks(bk, n):
                    return bank[bk][:, 0:n * P].rearrange("p (k t) -> p k t", k=n)

                def s_tanh(b):
                    e.wait_ge(S["s_u"], b + 1)
                    e.activation(s_h_, s_h_, ACT.Tanh).then_inc(S["s_h"], 1)

                def s_heads(b):
                    e.wait_ge(S["s_qtr"], b + 1)
                    if past(4 * b): e.wait_ge(S["s_sc"], 4 * b)
                    e.activation(s_kT_, bank[0][:, D:D + P], ACT.Copy).then_inc(S["s_kT"], 1)
                    for odd, mask in enumerate((m_even, m_odd)):
                        e.activation(s_qT_[:, odd], blocks(0, 2), ACT.Copy, scale=mask).then_inc(S["s_qT"], 1)

                def d_heads(b):
                    e.wait_ge(S["d_qk"], b + 1)
                    if past(b): e.wait_ge(S["d_sc"], b)
                    for c in range(4):
                        bias = (dbq if c < 2 else dbk)[:, c % 2:c % 2 + 1]
                        last = e.activation(d_qkT[:, c, :], bank[5][:, c * P:c * P + P], ACT.Identity, bias=bias)
                    last.then_inc(S["d_qk_sb"], 1)

                def d_exp(b):
                    e.wait_ge(S["d_nmax"], b + 1)
                    if past(b): e.wait_ge(S["d_ptr"], b)
                    if past(b): e.wait_ge(S["d_rinv"], b)
                    e.activation(d_P_, bank[6][:, 0:P], ACT.Exp, scale=1.0 / float(np.sqrt(D)), bias=d_nm,
                                 accum_out=d_sum).then_inc(S["d_exp"], 1)

                def step(i):
                    s, d, g = i - 1, i - 2, i - 3
                    if live(s):
                        copy("s_tr", s + 1, s_T[:, 0], blocks(0, 2), "s_hi", ("s_qkv", s))
                    if live(d):
                        copy("d_tr", d + 1, d_T[:, 0], blocks(5, 4), "d_hi", ("d_vmm", d))
                    if live(g):
                        copy("g_tr", g + 1, g_T, bank[7][:, 0:D], "g_xnT", ("g_sum", g))
                    if live(s):
                        copy("s_qr", 2 * s + 2, s_vx[:, :, 0:DH],
                             bank[1][:, D + KV * DH:NQ].rearrange("p (h d) -> p h d", d=DH), "s_v", ("s_pv", 4 * s))
                    if live(d):
                        d_heads(d)
                        copy("d_vmm", d + 1, d_v_, bank[6][:, 0:D], "d_v", ("d_pv", d))
                    if live(s):
                        s_heads(s)
                        att1["exponents"](e, s, 0)
                    if live(d):
                        d_exp(d)
                    if live(s):
                        att1["take"](e, s, 0)
                        att1["exponents"](e, s, 1)
                    if live(d):
                        copy("d_ptr", d + 1, d_PT, bank[6][:, 0:P], "d_pt", ("d_pv", d))
                    if live(s):
                        att1["take"](e, s, 1)
                        att1["exponents"](e, s, 2)
                        att1["take"](e, s, 2)
                        att1["exponents"](e, s, 3)
                        att1["take"](e, s, 3)
                    if live(i):
                        s_tanh(i)
                    if live(s):
                        copy("s_otr", s + 1, s_oT[:, 0], blocks(0, 2), "s_ohi", ("s_proj", s))

                pipeline(e, 3, step)

            @block.vector
            def _(e):
                def lo(pre, b, dst, src, high):
                    e.wait_ge(S[pre + "hi"], b + 1)
                    e.tensor_tensor(dst, src, high.bitcast(F32), ALU.subtract).then_inc(S[pre + "lo"], 1)

                def blocks(bk, n):
                    return bank[bk][:, 0:n * P].rearrange("p (k t) -> p k t", k=n)

                def stats(pre, b, src, cols, ready, factor=1.0, add=EPS):
                    row_statistics(e, pre, b, src, cols, ready, factor, add)

                def s_head(b):
                    e.wait_ge(S["s_xo"], 16 * (b + 1))
                    if past(b): e.wait_ge(S["s_x3"], b)
                    e.tensor_tensor(s_h_, s_xo_, v_row, ALU.add).then_inc(S["s_u"], 1)

                def s_join(b):
                    e.wait_ge(S["s_h"], b + 1)
                    if past(b): e.wait_ge(S["s_x4"], b)
                    e.tensor_tensor(s_x3_, s_h_, x_res[:, ds(b * D, D)], ALU.add).then_inc(S["s_x3"], 1)
                    stats("s", b, s_x3_, s_cols, ("s_x3", b + 1), 1.0 + EPS32, EPS * EPS32)

                def normed(pre, b, dst, src, cols, *free):
                    e.wait_ge(S[pre + "_rs"], 12 * b + 12)
                    if past(free[1]): e.wait_ge(S[free[0]], free[1])
                    e.tensor_scalar(dst, src, cols[1][:, 0:1], cols[5], ALU.subtract, ALU.mult)\
                        .then_inc(S[pre + "_xn"], 1)

                def s_rotary(b):
                    e.wait_ge(S["s_qkv"], b + 1)
                    if past(b): e.wait_ge(S["s_qtr"], b)
                    rf = const[:, C_RF:C_RF + DH]
                    e.tensor_tensor(s_qr_[:, 0:D].rearrange("p (h d) -> p h d", d=DH),
                                    bank[1][:, 0:D].rearrange("p (h d) -> p h d", d=DH),
                                    rf.unsqueeze(1).to_broadcast([P, HEADS, DH]), ALU.mult).then_inc(S["s_qr"], 1)
                    for r in range(2):
                        n = D + r * KV * DH
                        last = e.tensor_tensor(s_qr_[:, n:n + KV * DH].rearrange("p (h d) -> p h d", d=DH),
                                               bank[1][:, D:D + KV * DH].rearrange("p (h d) -> p h d", d=DH),
                                               rf.unsqueeze(1).to_broadcast([P, KV, DH]), ALU.mult)
                    last.then_inc(S["s_qr"], 1)

                def s_sum(b):
                    e.wait_ge(S["s_o"], b + 1)
                    e.tensor_tensor(s_x3_, s_x3_, s_o_, ALU.add).then_inc(S["s_x3s"], 1)

                def s_residual(b):
                    e.wait_ge(S["s_proj"], b + 1)
                    e.wait_ge(S["s_x3s"], b + 1)
                    if past(b): e.wait_ge(S["d_x5"], b)
                    e.tensor_tensor(x4, bank[1][:, 0:D], s_x3_, ALU.add).then_inc(S["s_x4"], 1)
                    stats("d", b, x4, d_cols, ("s_x4", b + 1))

                def d_maximum(b):
                    e.wait_ge(S["d_sc"], b + 1)
                    if past(b): e.wait_ge(S["d_nmax"], b)
                    e.tensor_reduce(d_mx, bank[6][:, 0:P], AX.X, ALU.max).then_inc(S["d_max"], 1)
                    e.wait_ge(S["d_max"], b + 1)
                    if past(b): e.wait_ge(S["d_exp"], b)
                    e.tensor_scalar(d_nm, d_mx, -1.0 / float(np.sqrt(D)), None, ALU.mult).then_inc(S["d_nmax"], 1)

                def d_residual(b):
                    e.wait_ge(S["d_exp"], b + 1)
                    if past(b): e.wait_ge(S["d_x5"], b)
                    e.reciprocal(d_ri, d_sum).then_inc(S["d_rinv"], 1)
                    e.wait_ge(S["d_pv"], b + 1)
                    e.wait_ge(S["d_x4b"], b + 1)
                    e.wait_ge(S["d_rinv"], b + 1)
                    e.scalar_tensor_tensor(out=x_res[:, ds(b * D, D)], in0=bank[6][:, 0:D], scalar=d_ri,
                                           in1=x4, op0=ALU.mult, op1=ALU.add).then_inc(S["d_x5"], 1)
                    stats("g", b, x_res[:, ds(b * D, D)], g_cols, ("d_x5", b + 1))

                def g_norm(b):
                    normed("g", b, g_xn_, x_res[:, ds(b * D, D)], g_cols, "g_tr", b)
                    e.tensor_scalar(tab[:, ds(b * TAB + 3 * NH, 1)], g_cols[1][:, 0:1], 1.0, None, ALU.mult)
                    e.tensor_scalar(tab[:, ds(b * TAB + 3 * NH + 1, 1)], g_cols[5], 1.0, None, ALU.mult)\
                        .then_inc(S["g_kept"], 1)

                def g_logits(b):
                    e.wait_ge(S["g_sum"], b + 1)
                    e.tensor_tensor(tab[:, ds(b * TAB, E)], bank[7][:, D:D + E], lbb, ALU.add).then_inc(S["g_lg"], 1)

                e.memset(s_vx[:, :, DH:VX], 1.0)

                def step(i):
                    s, d, g = i - 1, i - 2, i - 3
                    if live(s):
                        normed("s", s, s_xn_, s_x3_, s_cols, "s_tr", s)
                    if live(d):
                        normed("d", d, d_xn_, x4, d_cols, "d_tr", d)
                    if live(g):
                        g_norm(g)
                    if live(s):
                        lo("s_", s, s_T[:, 1], blocks(0, 2), s_T[:, 0])
                    if live(d):
                        lo("d_", d, d_T[:, 1], blocks(5, 4), d_T[:, 0])
                    if live(s):
                        s_rotary(s)
                    if live(g):
                        g_logits(g)
                    if live(s):
                        att1["softmax"](e, s, 0)
                    if live(d):
                        d_maximum(d)
                    if live(s):
                        att1["softmax"](e, s, 1)
                        att1["softmax"](e, s, 2)
                        att1["softmax"](e, s, 3)
                    if live(d):
                        d_residual(d)
                    if live(s):
                        att1["normalise"](e, s, s_o_, s_ri, ["s_otr", "s_x3s"], [s, s])
                        s_sum(s)
                    if live(i):
                        s_head(i)
                    if live(s):
                        lo("s_o", s, s_oT[:, 1], blocks(0, 2), s_oT[:, 0])
                        s_residual(s)
                    if live(i):
                        s_join(i)

                pipeline(e, 3, step)

            @block.gpsimd
            def _(e):
                def newton(pre, b, cols):
                    e.wait_ge(S[pre + "_seed"], 3 * b + 3)
                    rsqrt_newton(e, cols[3], cols[4], cols[5], pre + "_rs", 12 * b)

                def step(i):
                    s, d, g = i - 1, i - 2, i - 3
                    if live(d):
                        e.wait_ge(S["d_xn"], d + 1)
                        e.tensor_tensor(x4, x4, dbv_row, ALU.add).then_inc(S["d_x4b"], 1)
                        newton("g", d, g_cols)
                    if live(s):
                        newton("d", s, d_cols)
                    if live(i):
                        newton("s", i, s_cols)

                pipeline(e, 3, step)

        jobs2 = []
        for x_ in range(E):
            jobs2 += [(e_gate[x_], D, to(w_gu, x_ * 2 * P), 1.0, None), (e_up[x_], D, to(w_gu, (2 * x_ + 1) * P), 1.0, None)]
            for r in range(2):
                jobs2.append((e_down[x_, r * P:(r + 1) * P, :], P, to(w_dn[:, :, x_:x_ + 1, :], r * P), 1.0, None))
        for r in range(2):
            jobs2 += [(sh_gate[r * P:(r + 1) * P, :], D, to(w_gu, (16 + 2 * r) * P), 1.0, None),
                      (sh_up[r * P:(r + 1) * P, :], D, to(w_gu, (17 + 2 * r) * P), 1.0, None),
                      (sh_down[r * P:(r + 1) * P, :], D, to(w_dn[:, :, E:E + 2, :], r * P), 1.0, None)]
        w2 = weights("w2", 4, work[:, 4096:6144], jobs2)
        t_s, t_first, t_second, t_tmp = (work[:, 512 * k:512 * k + NT].rearrange("p (b e) -> p b e", e=E) for k in range(4))
        t_max, t_max2, t_key, t_rcp = (work[:, 2048 + NB * k:2048 + NB * k + NB] for k in range(4))
        t_part, t_mean = work[:, 2304:2304 + 2 * E], work[:, 2336:2336 + 2 * E]
        logits = tab3[:, :, 0:E]
        coef = tab3[:, :, E:2 * E]

        with phase("route") as block:
            @block.sync
            def _(e):
                w2[0](e)

            @block.tensor
            def _(e):
                w2[1](e)
                e.wait_ge(S["t_part"], 1)
                e.matmul(bank[4][:, 0:2 * E], const[:, C_ONE:C_ONE + P], t_part, start=True, stop=True)\
                    .then_inc(S["t_tot"], 1)

            @block.scalar
            def _(e):
                e.activation(t_s, logits, ACT.Exp, scale=-1.0).then_inc(S["t_sig"], 1)
                w2[2](e)

            @block.vector
            def _(e):
                n = 0

                def link(i):
                    nonlocal n
                    n += 1
                    i.then_inc(S["t_chain"], 1)
                    e.wait_ge(S["t_chain"], n)

                def wide(a):
                    return a.unsqueeze(2).to_broadcast([P, NB, E])

                def first_of_max(s_, max_, first_):
                    link(e.tensor_reduce(max_, s_, AX.X, ALU.max))
                    link(e.tensor_tensor(t_tmp, s_, wide(max_), ALU.is_equal))
                    link(e.tensor_tensor(t_tmp, t_tmp, const[:, C_IOTA:C_IOTA + E].unsqueeze(1).to_broadcast([P, NB, E]),
                                         ALU.mult))
                    link(e.tensor_reduce(t_key, t_tmp, AX.X, ALU.max))
                    link(e.tensor_tensor(first_, t_tmp, wide(t_key), ALU.is_equal))

                e.wait_ge(S["t_sig"], 1)
                link(e.tensor_scalar(t_s, t_s, 1.0, None, ALU.add))
                link(e.reciprocal(t_s, t_s))
                first_of_max(t_s, t_max, t_first)
                link(e.scalar_tensor_tensor(out=t_second, in0=t_first, scalar=-4.0, in1=t_s, op0=ALU.mult, op1=ALU.add))
                first_of_max(t_second, t_max2, t_second)
                link(e.tensor_tensor(t_rcp, t_max, t_max2, ALU.add))
                link(e.tensor_scalar(t_rcp, t_rcp, 1e-8, None, ALU.add))
                link(e.reciprocal(t_rcp, t_rcp))
                link(e.tensor_tensor(t_first, t_first, t_second, ALU.add))
                link(e.tensor_tensor(t_s, t_s, t_first, ALU.mult))
                link(e.tensor_tensor(t_s, t_s, wide(t_rcp), ALU.mult))
                e.tensor_reduce(t_part[:, 0:E], t_s.rearrange("p b e -> p e b"), AX.X, ALU.add)
                e.tensor_reduce(t_part[:, E:2 * E], t_first.rearrange("p b e -> p e b"), AX.X, ALU.add)\
                    .then_inc(S["t_part"], 1)
                w2[3](e)
                e.wait_ge(S["t_tot"], 1)
                link(e.tensor_scalar(t_mean[:, E:2 * E], bank[4][:, E:2 * E], 1.0, None, ALU.max))
                link(e.reciprocal(t_mean[:, E:2 * E], t_mean[:, E:2 * E]))
                link(e.scalar_tensor_tensor(out=t_mean[:, 0:E], in0=bank[4][:, 0:E], scalar=0.5, in1=t_mean[:, E:2 * E],
                                            op0=ALU.mult, op1=ALU.mult))
                e.tensor_tensor(coef, t_first, t_mean[:, 0:E].unsqueeze(1).to_broadcast([P, NB, E]), ALU.mult)\
                    .then_inc(S["t_coef"], 1)

        NG = 5
        wpos[0] = rpos[0] = 0
        f_xn_ = [wk(D), wk(D)]
        f_T = [wr(2 * D).rearrange("p (s k t) -> p s k t", s=2, k=2) for _ in range(2)]
        f_t = [wk(2 * P).rearrange("p (x i) -> p x i", x=2) for _ in range(2)]
        f_h_ = [wk(2 * P).rearrange("p (x i) -> p x i", x=2) for _ in range(2)]
        f_hT = [wr(2 * D).rearrange("p (s k t) -> p s k t", s=2, k=2) for _ in range(2)]
        f_coef = [tiny[:, 0:E], tiny[:, E:2 * E]]
        f_stage = [wk(D), wk(D)]

        def pairs(e, steps, tail):
            steps(0)
            steps(1)
            with e.Fori(2, NB // 2 - 1) as h:
                steps(h)
            steps(NB // 2 - 1)
            tail(NB // 2)

        def before(h):
            return not isinstance(h, int) or h > 0

        def after(h):
            return not isinstance(h, int) or h < NB // 2 - 1

        with phase("experts") as block:
            @block.sync
            def _(e):
                def steps(h):
                    for k in range(2):
                        b = 2 * h + k
                        e.wait_ge(S["f_x6"], b + 1)
                        e.dma_start(out[b] if isinstance(b, int) else out[ds(b, 1)].rearrange("o t d -> t (o d)"),
                                    f_stage[k]).then_inc(S[f"f_out{k}"], 16)

                pairs(e, steps, lambda h: None)
                for k in range(2):
                    e.wait_ge(S[f"f_out{k}"], 16 * (NB // 2))

            @block.tensor
            def _(e):
                def transpose(b, k):
                    e.wait_ge(S["f_xn"], b + 1)
                    if past(b): e.wait_ge(S["f_lo"], b)
                    for c in range(2):
                        last = e.transpose(bank[6][:, c * P:c * P + P], f_xn_[k][:, c * P:c * P + P], ident)
                    last.then_inc(S["f_tr"], 1)

                def up(n, b, g, q, k):
                    e.wait_ge(S["f_lo"], b + 1)
                    if past(n - 1): e.wait_ge(S["f_h"], n - 1)
                    project(e, bank[q][:, :], f_T[k], w_gu, 2, 4 * P * g, 4 * P * (g + 1)).then_inc(S["f_gu"], 1)

                def turn(n, q):
                    e.wait_ge(S["f_h"], n + 1)
                    if past(n - 1): e.wait_ge(S["f_hlo"], n - 1)
                    for j in range(2):
                        last = e.transpose(bank[2 + q][:, j * P:j * P + P], f_h_[q][:, j, :], ident)
                    last.then_inc(S["f_htr"], 1)

                def down(n, b, g, q, k):
                    e.wait_ge(S["f_hlo"], n + 1)
                    if g == 0:
                        if past(b - 1): e.wait_ge(S["f_x6"], b - 1)
                    for j in range(2):
                        last = mm3(e, bank[4 + k][:, 0:D], (f_hT[q][:, 0, j, :], f_hT[q][:, 1, j, :]),
                                   (w_dn[:, 0, 2 * g + j, :], w_dn[:, 1, 2 * g + j, :]),
                                   g == 0 and j == 0, g == NG - 1 and j == 1)
                    last.then_inc(S["f_acc"], 1)

                def later(h, m):
                    if m < 0:
                        h, m = h - 1, m + 2 * NG
                    return 2 * NG * h + m, 2 * h + m // NG, m % NG, m % 2, m // NG

                def steps(h):
                    for m in range(2 * NG):
                        n, b, g, q, k = later(h, m)
                        up(n, b, g, q, k)
                        if m >= 1 or before(h):
                            n, b, g, q, k = later(h, m - 1)
                            turn(n, q)
                        if m >= 2 or before(h):
                            down(*later(h, m - 2))
                        if m == 2:
                            transpose(2 * h + 1, 1)
                        if m == 7 and after(h):
                            transpose(2 * h + 2, 0)

                def tail(h):
                    n, b, g, q, k = later(h, -1)
                    turn(n, q)
                    down(*later(h, -2))
                    down(*later(h, -1))

                transpose(0, 0)
                pairs(e, steps, tail)

            @block.scalar
            def _(e):
                def high(b, k):
                    e.wait_ge(S["f_tr"], b + 1)
                    if past(NG * (b - 1)): e.wait_ge(S["f_gu"], NG * (b - 1))
                    e.activation(f_T[k][:, 0], bank[6][:, 0:D].rearrange("p (k t) -> p k t", k=2), ACT.Copy)\
                        .then_inc(S["f_hi"], 1)

                def gate(n, q):
                    e.wait_ge(S["f_gu"], n + 1)
                    if past(n - 1): e.wait_ge(S["f_h"], n - 1)
                    e.activation(f_t[q], bank[q][:, :].rearrange("p (x o i) -> p x o i", x=2, o=2)[:, :, 0, :],
                                 ACT.Tanh, scale=0.5).then_inc(S["f_tanh"], 1)

                def hidden(n, q):
                    e.wait_ge(S["f_htr"], n + 1)
                    if past(n - 1): e.wait_ge(S["f_acc"], n - 1)
                    e.activation(f_hT[q][:, 0], bank[2 + q][:, 0:2 * P].rearrange("p (k t) -> p k t", k=2), ACT.Copy)\
                        .then_inc(S["f_hhi"], 1)

                def steps(h):
                    for m in range(2 * NG):
                        n = 2 * NG * h + m
                        gate(n, m % 2)
                        if m >= 1 or before(h):
                            hidden(n - 1, (m - 1) % 2)
                        if m == 2:
                            high(2 * h + 1, 1)
                        if m == 7 and after(h):
                            high(2 * h + 2, 0)

                high(0, 0)
                pairs(e, steps, lambda h: hidden(2 * NG * h - 1, 1))

            @block.vector
            def _(e):
                def norm(b, k):
                    if past(b - 1): e.wait_ge(S["f_tr"], b - 1)
                    if past(NG * (b - 1)): e.wait_ge(S["f_h"], NG * (b - 1))
                    e.tensor_scalar(f_coef[k], tab[:, ds(b * TAB + E, E)], 1.0, None, ALU.mult)
                    e.tensor_scalar(f_xn_[k], x_res[:, ds(b * D, D)], tab[:, ds(b * TAB + 3 * NH, 1)],
                                    tab[:, ds(b * TAB + 3 * NH + 1, 1)], ALU.subtract, ALU.mult)\
                        .then_inc(S["f_xn"], 1)

                def low(b, k):
                    e.wait_ge(S["f_hi"], b + 1)
                    e.tensor_tensor(f_T[k][:, 1], bank[6][:, 0:D].rearrange("p (k t) -> p k t", k=2),
                                    f_T[k][:, 0].bitcast(F32), ALU.subtract).then_inc(S["f_lo"], 1)

                def gated(n, g, q, k):
                    v = bank[q][:, :].rearrange("p (x o i) -> p x o i", x=2, o=2)
                    e.wait_ge(S["f_tanh"], n + 1)
                    e.scalar_tensor_tensor(out=f_t[q], in0=f_t[q], scalar=1.0, in1=v[:, :, 0, :],
                                           op0=ALU.add, op1=ALU.mult).then_inc(S["f_tg"], 1)
                    e.wait_ge(S["f_tg"], n + 1)
                    if past(n - 1): e.wait_ge(S["f_htr"], n - 1)
                    for j in range(2):
                        w = f_coef[k][:, 2 * g + j:2 * g + j + 1] if g < NG - 1 else 0.5
                        last = e.scalar_tensor_tensor(out=f_h_[q][:, j, :], in0=f_t[q][:, j, :], scalar=w,
                                                      in1=v[:, j, 1, :], op0=ALU.mult, op1=ALU.mult)
                    last.then_inc(S["f_h"], 1)

                def hidden(n, q):
                    e.wait_ge(S["f_hhi"], n + 1)
                    e.tensor_tensor(f_hT[q][:, 1], bank[2 + q][:, 0:2 * P].rearrange("p (k t) -> p k t", k=2),
                                    f_hT[q][:, 0].bitcast(F32), ALU.subtract).then_inc(S["f_hlo"], 1)

                def finish(b, k, h_):
                    e.wait_ge(S["f_acc"], NG * (b + 1))
                    if past(16 * h_): e.wait_ge(S[f"f_out{k}"], 16 * h_)
                    e.tensor_tensor(f_stage[k], bank[4 + k][:, 0:D], x_res[:, ds(b * D, D)], ALU.add)\
                        .then_inc(S["f_x6"], 1)

                def steps(h):
                    for m in range(2 * NG):
                        n = 2 * NG * h + m
                        gated(n, m % NG, m % 2, m // NG)
                        if m >= 1 or before(h):
                            hidden(n - 1, (m - 1) % 2)
                        if m == 1:
                            norm(2 * h + 1, 1)
                        if m == 2:
                            low(2 * h + 1, 1)
                            if before(h):
                                finish(2 * h - 1, 1, h - 1)
                        if m == 6 and after(h):
                            norm(2 * h + 2, 0)
                        if m == 7:
                            if after(h):
                                low(2 * h + 2, 0)
                            finish(2 * h, 0, h)

                def tail(h):
                    hidden(2 * NG * h - 1, 1)
                    finish(2 * h - 1, 1, h - 1)

                norm(0, 0)
                low(0, 0)
                pairs(e, steps, tail)


_INS = ["x", "ctx_1024",
        "L0_attn_in_proj_w", "L0_attn_conv_w", "L0_attn_conv_b", "L0_attn_norm_w", "L0_attn_out_proj_w",
        "L0_attn_dt_bias", "L0_attn_A_log", "L0_attn_D_param",
        "L0_xattn_Wq", "L0_xattn_bq", "L0_xattn_Wk", "L0_xattn_bk", "L0_xattn_Wv", "L0_xattn_bv",
        "L0_xattn_Wo", "L0_xattn_bo",
        "L0_ffn_wf", "L0_ffn_uf", "L0_ffn_bf", "L0_ffn_wi", "L0_ffn_ui", "L0_ffn_bi",
        "L0_ffn_wc", "L0_ffn_uc", "L0_ffn_bc", "L0_ffn_wo", "L0_ffn_uo", "L0_ffn_bo", "L0_ffn_in_c",
        "L1_attn_w_q", "L1_attn_w_k", "L1_attn_w_v", "L1_attn_w_o", "L1_attn_g",
        "L1_xattn_Wq", "L1_xattn_bq", "L1_xattn_Wk", "L1_xattn_bk", "L1_xattn_Wv", "L1_xattn_bv",
        "L1_ffn_gate_w", "L1_ffn_lb_bias", "L1_ffn_expert_gate_w", "L1_ffn_expert_up_w",
        "L1_ffn_expert_down_w", "L1_ffn_shared_gate_w", "L1_ffn_shared_up_w", "L1_ffn_shared_down_w"]


def kernel(**inputs):
    import numpy as _np
    import concourse.bacc as _bacc
    from concourse.bass_utils import run_bass_kernel_spmd as _run

    nc = _bacc.Bacc("TRN2", target_bir_lowering=False, num_devices=1)
    arrays, args = {}, []
    for name in _INS:
        a = _np.ascontiguousarray(inputs[name])
        arrays[f"in_{name}"] = a
        args.append(nc.dram_tensor(f"in_{name}", a.shape, mybir.dt.from_np(a.dtype), kind="ExternalInput").ap())
    shape = arrays["in_x"].shape
    out = nc.dram_tensor("out_dram", shape, F32, kind="ExternalOutput").ap()
    xo = nc.dram_tensor("recurrence_out", shape, F32, kind="Internal").ap()
    table = nc.inline_tensor(constant_table(), name="constant_table").ap()
    decoder(nc, args, xo, table, out)
    r = _run(nc, [arrays], core_ids=[0])
    return r.results[0]["out_dram"]
```

```python
from contextlib import ExitStack, contextmanager

import numpy as np

import concourse.bass as bass
from concourse import mybir

P = 128
D = 256
DI = 512
NH = 8
HD = 64
CONV = 4
XBC = DI + 2 * P
HEADS = 16
DH = 16
KV = 4
E = 8
HID = 128
EPS = 1e-5
EPS32 = float(np.finfo(np.float32).eps)

F32 = mybir.dt.float32
F32R = mybir.dt.float32r
I32 = mybir.dt.int32
ALU = mybir.AluOpType
ACT = mybir.ActivationFunctionType
AX = mybir.AxisListType
ds = bass.ds

C_ID, C_UP, C_COS, C_SIN, C_RF, C_EVEN, C_ODD, C_IOTA, C_ONE, C_3_2, C_END = (
    0, 128, 256, 272, 288, 304, 305, 306, 314, 442, 443)


def constant_table():
    t = np.zeros((P, C_END), np.float32)
    t[:, C_ID:C_ID + P] = np.eye(P)
    t[:, C_UP:C_UP + P] = np.triu(np.ones((P, P)))
    pos = np.arange(P, dtype=np.float32)
    inv = (1.0 / np.power(np.float32(10000.0), np.arange(0, DH, 2, dtype=np.float32) / np.float32(DH))).astype(np.float32)
    ang = pos[:, None] * np.concatenate([inv, inv])[None, :]
    t[:, C_COS:C_COS + DH] = np.cos(ang)
    t[:, C_SIN:C_SIN + DH] = np.sin(ang) * np.where(np.arange(DH) < DH // 2, -1.0, 1.0)
    theta = np.power(np.float32(10000.0), (-2.0 * (np.arange(DH) // 2) / DH).astype(np.float32))
    ang = pos[:, None] * theta[None, :]
    t[:, C_RF:C_RF + DH] = np.cos(ang) + np.where(np.arange(P) % 2 == 1, -1.0, 1.0)[:, None] * np.sin(ang)
    t[:, C_EVEN] = (np.arange(P) // DH) % 2 == 0
    t[:, C_ODD] = (np.arange(P) // DH) % 2 == 1
    t[:, C_IOTA:C_IOTA + E] = E - np.arange(E)
    t[:, C_ONE:C_ONE + P] = 1.0
    t[:, C_3_2] = 1.5
    return t


SIGNALS = {
    "consts": """
        small_loaded halved bias_rows_ready bo2_mm start_state start_hi start_lo bv_hi bv_lo
        w0_load0 w0_load1 w0_load2 w0_load3 w0_scaled w0_tr w0_hi w0_lo consts_ready
    """.split(),
    "steps": """
        p_stats p_chain p_xn p_tr p_xnT p_dt p_min p_act p_nd p_cum
    """.split(),
    "layer0": """
        m_cur m_xn m_tr m_hi m_lo m_xbc m_raw m_tap m_conv2 m_conv m_z m_ztanh m_zg m_xtanh m_xbcs
        m_xtr m_g m_xt m_xdt m_xd m_gm m_bc m_relv m_rela m_exp m_M m_y m_yx m_y2 m_ss m_seed m_rs
        m_ytr m_yhi m_ylo m_out m_x1 c_stats c_aggr c_seed c_rs c_xn c_ctx c_x1b c_tr c_hi c_lo c_q
        c_kv c_kb c_qb c_v c_rot c_cos c_qr c_qtr c_kT c_qT c_sc c_max c_sub c_exp c_ptr c_pt c_pv
        c_rinv c_o c_otr c_ohi c_olo c_proj c_x2 r_stats r_aggr r_seed r_rs r_xn r_tr r_hi r_lo r_fi
        r_tfi r_go r_tg r_xo r_store r_a r_b r_d r_dhi r_dlo
    """.split(),
    "between": """
        w1_load0 w1_load1 w1_load2 w1_load3 w1_scaled w1_tr w1_hi w1_lo b_v b_vrow b_dhi l1_small
        l1_wg l1_whi l1_wlo
    """.split(),
    "layer1": """
        s_xo s_u s_h s_x3 s_stats s_aggr s_seed s_rs s_xn s_tr s_hi s_lo s_qkv s_qr s_v s_qtr s_kT
        s_qT s_sc s_max s_sub s_exp s_ptr s_pt s_pv s_rinv s_o s_x3s s_otr s_ohi s_olo s_proj s_x4
        d_stats d_aggr d_seed d_rs d_xn d_ctx d_x4b d_tr d_hi d_lo d_qk d_vmm d_qk_sb d_v d_sc d_max
        d_nmax d_exp d_ptr d_pt d_pv d_rinv d_x5 g_stats g_aggr g_seed g_rs g_xn g_tr g_xnT g_lg
        g_sum
    """.split(),
    "route": """
        w2_load0 w2_load1 w2_load2 w2_load3 w2_scaled w2_tr w2_hi w2_lo t_chain t_sig t_part t_tot
        t_coef
    """.split(),
    "experts": """
        f_xn f_tr f_hi f_lo f_gu f_tanh f_tg f_h f_htr f_hhi f_hlo f_acc f_x6 f_out0 f_out1
    """.split(),
}


def decoder(nc, args, xo_dram, table, out):
    (x, ctx, in_proj, conv_w, conv_b, norm_w, out_proj, dt_bias, A_log, D_param,
     c_Wq, c_bq, c_Wk, c_bk, c_Wv, c_bv, c_Wo, c_bo,
     wf, uf, bf, wi, ui, bi, wc, uc, bc, wo, uo, bo, in_c,
     s_wq, s_wk, s_wv, s_wo, s_g, d_Wq, d_bq, d_Wk, d_bk, d_Wv, d_bv,
     gate_w, lb_bias, e_gate, e_up, e_down, sh_gate, sh_up, sh_down) = args
    NB = x.shape[0]
    NT = NB * E

    with ExitStack() as stack:
        def sb(name, shape, dt=F32):
            return stack.enter_context(nc.sbuf_tensor(name, shape, dt))

        S = {name: stack.enter_context(nc.semaphore(name))
             for name in ["const_loaded"] + [f"x_loaded{c}" for c in range(8)]}

        @contextmanager
        def phase(name):
            own = {n: nc.alloc_semaphore(name=n) for n in SIGNALS[name]}
            S.update(own)
            with nc.Block() as block_:
                yield block_
            nc.clear_and_free_semaphores(list(own.values()))
            nc.all_engine_barrier()

        bank = [stack.enter_context(nc.psum_tensor(f"bank{k}", [P, 512], F32)) for k in range(8)]

        def past(count):
            return not isinstance(count, int) or count > 0

        def live(b):
            return not isinstance(b, int) or 0 <= b < NB

        def tile(dram, b):
            return dram[b] if isinstance(b, int) else dram[ds(b, 1)].rearrange("o t d -> t (o d)")

        def pipeline(eng, lag, step):
            for i in range(lag + 1):
                step(i)
            with eng.Fori(lag + 1, NB) as i:
                step(i)
            for i in range(NB, NB + lag):
                step(i)

        def mm3(pe, out_, lhs, rhs, first=True, last=True):
            pe.matmul(out_, lhs[0], rhs[0], start=first, stop=False)
            pe.matmul(out_, lhs[0], rhs[1], start=False, stop=False)
            return pe.matmul(out_, lhs[1], rhs[0], start=False, stop=last)

        def project(pe, out_, act, w, blocks, n0, n1):
            for k in range(blocks):
                last = mm3(pe, out_, (act[:, 0, k, :], act[:, 1, k, :]),
                           (w[:, 0, k, n0:n1], w[:, 1, k, n0:n1]), k == 0, k == blocks - 1)
            return last

        def project_T(pe, out_, act, w, n0, first=True, last_=True):
            for k in range(2):
                last = mm3(pe, out_, (w[:, 0, k, n0:n0 + P], w[:, 1, k, n0:n0 + P]),
                           (act[:, 0, k, :], act[:, 1, k, :]), first and k == 0, last_ and k == 1)
            return last

        const = sb("const", [P, C_END])
        ident = const[:, C_ID:C_ID + P]
        upper = const[:, C_UP:C_UP + P]
        m_even, m_odd = const[:, C_EVEN:C_EVEN + 1], const[:, C_ODD:C_ODD + 1]
        upper_r = sb("upper_r", [P, P], F32R)
        x_res = sb("x_res", [P, NB * D])
        TAB = 3 * NH + 2
        tab = sb("tab", [P, NB * TAB])
        tab3 = tab[:, :].rearrange("p (b n) -> p b n", n=TAB)
        WREG = 18432
        wts = sb("wts", [P, WREG], F32R)
        w_dt = sb("w_dt", [P, 2, NH])
        small = sb("small", [P, 96])
        rows = sb("rows", [P, 4 * D])
        work = sb("work", [P, 9112])
        workr = sb("workr", [P, 3584], F32R)
        tiny = sb("tiny", [P, 96])
        curr = sb("curr", [P, 2, NH], F32R)

        def wview(base, k, n):
            assert base + 2 * k * n <= WREG
            return wts[:, base:base + 2 * k * n].rearrange("p (s k n) -> p s k n", s=2, k=k)

        w_in = wview(0, 2, DI + XBC)
        w_out = wview(5120, 4, D)
        w_cq = wview(7168, 2, D)
        w_ckv = wview(8192, 2, 2 * D)
        w_co = wview(10240, 2, D)
        w_rx = wview(11264, 2, 3 * D)
        w_ru = wview(14336, 2, 3 * D)
        w_rxo = wview(17408, 2, D)
        w_uo = wview(0, 2, D)
        w_sqkv = wview(1024, 2, D + 2 * KV * DH)
        w_so = wview(2560, 2, D)
        w_dq = wview(3584, 2, D)
        w_dk = wview(4608, 2, D)
        w_dv = wview(5632, 2, D)
        w_gu = wview(0, 2, 10 * 2 * P)
        w_dn = wview(10240, 10, D)
        w_gate = sb("w_gate", [P, 2, E])

        col = {}
        at = [0]

        def small_cols(name, n):
            col[name] = small[:, at[0]:at[0] + n]
            at[0] += n
            return col[name]

        cw = small_cols("cw", 6 * CONV).rearrange("p (j k) -> p j k", k=CONV)
        cb = small_cols("cb", 6)
        expA = small_cols("expA", NH)
        dtb = small_cols("dtb", NH)
        dpar = small_cols("dpar", NH)
        gb = small_cols("gb", 6)
        inc = small_cols("inc", 2)
        bvc = small_cols("bvc", 2)
        gcol = small_cols("gcol", 2)
        dbq = small_cols("dbq", 2)
        dbk = small_cols("dbk", 2)
        lbb = small_cols("lbb", E)
        bvr = sb("bvr", [P, 2, 2], F32R)
        bqk_row = rows[:, 0:2 * D]
        bo2_row = rows[:, 2 * D:3 * D]
        bo_row = rows[:, 3 * D:4 * D]

        wpos = [0]

        def wk(n):
            a = work[:, wpos[0]:wpos[0] + n]
            wpos[0] += n
            assert wpos[0] <= 9112, wpos
            return a

        rpos = [0]

        def wr(n):
            a = workr[:, rpos[0]:rpos[0] + n]
            rpos[0] += n
            assert rpos[0] <= 3584, rpos
            return a

        def weights(pre, sets, scratch, jobs):
            stages = [scratch[:, 512 * k:512 * k + 512] for k in range(4)]

            def sync(e):
                for j, (rows_, n, _, _, _) in enumerate(jobs):
                    if past(j - 3): e.wait_ge(S[pre + "_tr"], j - 3)
                    e.dma_start(stages[j % 4][:, 0:n], rows_).then_inc(S[f"{pre}_load{j % 4}"], 16)

            def tensor(e):
                scaled = 0
                for j, (_, n, _, _, sc) in enumerate(jobs):
                    e.wait_ge(S[f"{pre}_load{j % 4}"], 16 * (j // 4 + 1))
                    if sc is not None:
                        scaled += 1
                        e.wait_ge(S[pre + "_scaled"], scaled)
                    if past(j - 3): e.wait_ge(S[pre + "_lo"], j - 3)
                    for c in range(n // P):
                        last = e.transpose(bank[j % 4][:, c * P:c * P + P],
                                           stages[j % 4][:, c * P:c * P + P], ident)
                    last.then_inc(S[pre + "_tr"], 1)

            def scalar(e):
                for j, (_, n, dst, f, _) in enumerate(jobs):
                    e.wait_ge(S[pre + "_tr"], j + 1)
                    src = bank[j % 4][:, 0:n].rearrange("p (c r) -> p c r", r=P)
                    e.activation(dst(0), src, ACT.Copy, scale=f).then_inc(S[pre + "_hi"], 1)

            def vector(e):
                def scale(j):
                    if j < len(jobs) and jobs[j][4] is not None:
                        e.wait_ge(S[f"{pre}_load{j % 4}"], 16 * (j // 4 + 1))
                        st = stages[j % 4][:, 0:jobs[j][1]]
                        e.tensor_tensor(st, st, jobs[j][4], ALU.mult).then_inc(S[pre + "_scaled"], 1)

                for j in range(2):
                    scale(j)
                for j, (_, n, dst, f, _) in enumerate(jobs):
                    e.wait_ge(S[pre + "_hi"], j + 1)
                    src = bank[j % 4][:, 0:n].rearrange("p (c r) -> p c r", r=P)
                    e.scalar_tensor_tensor(out=dst(1), in0=src, scalar=f, in1=dst(0).bitcast(F32),
                                           op0=ALU.mult, op1=ALU.subtract).then_inc(S[pre + "_lo"], 1)
                    scale(j + 2)

            return sync, tensor, scalar, vector

        def to(view, r0):
            return lambda part: view[:, part, :, r0:r0 + P]

        def settled(e):
            e.wait_ge(S["const_loaded"], 16)

        def rsqrt_seed(e, x_, xh_, t_, y_, chain, b):
            e.wait_ge(S[chain], 3 * b + 1)
            e.tensor_scalar(xh_, x_, -0.5, None, ALU.mult)
            e.tensor_scalar(t_.bitcast(I32), x_.bitcast(I32), 1, None, ALU.arith_shift_right)\
                .then_inc(S[chain], 1)
            e.wait_ge(S[chain], 3 * b + 2)
            e.tensor_scalar(y_.bitcast(I32), t_.bitcast(I32), -1.0, float(0x5F3759DF), ALU.mult, ALU.add)\
                .then_inc(S[chain], 1)

        def rsqrt_newton(e, xh_, t_, y_, chain, c0):
            three_halves = const[:, C_3_2:C_3_2 + 1]
            n = 0
            for _ in range(3):
                for out_, a_, b_ in ((t_, y_, y_), (t_, t_, xh_), (t_, t_, three_halves), (y_, y_, t_)):
                    if n:
                        if past(c0 + n): e.wait_ge(S[chain], c0 + n)
                    e.tensor_tensor(out_, a_, b_, ALU.add if b_ is three_halves else ALU.mult)\
                        .then_inc(S[chain], 1)
                    n += 1

        def stat_cols(c):
            return (tiny[:, c:c + 6], tiny[:, c + 6:c + 8], tiny[:, c + 8:c + 9], tiny[:, c + 9:c + 10],
                    tiny[:, c + 10:c + 11], tiny[:, c + 11:c + 12])

        def row_statistics(e, pre, b, src, cols, ready, factor=1.0, add=EPS):
            st, mv, x_, xh_, t_, y_ = cols
            settled(e)
            e.wait_ge(S[ready[0]], ready[1])
            if past(b): e.wait_ge(S[pre + "_xn"], b)
            e.bn_stats(st, src).then_inc(S[pre + "_stats"], 1)
            settled(e)
            e.wait_ge(S[pre + "_stats"], b + 1)
            e.bn_aggr(mv, st).then_inc(S[pre + "_aggr"], 1)
            e.wait_ge(S[pre + "_aggr"], b + 1)
            if past(12 * b): e.wait_ge(S[pre + "_rs"], 12 * b)
            e.tensor_scalar(x_, mv[:, 1:2], factor, add, ALU.mult, ALU.add).then_inc(S[pre + "_seed"], 1)
            rsqrt_seed(e, x_, xh_, t_, y_, pre + "_seed", b)

        nw_row = work[:, 0:DI]
        stage0 = work[:, 2048:4096]
        ff = [(wf, uf), (wi, ui), (wc, uc)]
        jobs0 = [(in_proj[r * P:(r + 1) * P, :], D, to(w_in, r * P), 1.0, None) for r in range(10)]
        jobs0 += [(out_proj[r * P:(r + 1) * P, :], DI, to(w_out, r * P), 1.0, nw_row) for r in range(2)]
        for r in range(2):
            jobs0 += [(c_Wq[r * P:(r + 1) * P, :], D, to(w_cq, r * P), 1.0, None),
                      (c_Wk[r * P:(r + 1) * P, :], D, to(w_ckv, r * P), 1.0, None),
                      (c_Wv[r * P:(r + 1) * P, :], D, to(w_ckv, D + r * P), 1.0, None),
                      (c_Wo[r * P:(r + 1) * P, :], D, to(w_co, r * P), 1.0, None),
                      (wo[r * P:(r + 1) * P, :], D, to(w_rxo, r * P), 1.0, None)]
            for g, (wx, wu) in enumerate(ff):
                jobs0 += [(wx[r * P:(r + 1) * P, :], D, to(w_rx, g * D + r * P), 1.0, None),
                          (wu[r * P:(r + 1) * P, :], D, to(w_ru, g * D + r * P), 0.5, None)]
        w0 = weights("w0", 4, stage0, jobs0)
        dt_stage = work[0:NH, 512:512 + D]
        bo2_in = work[:, 768:768 + D]
        d_state = sb("d_state", [P, 2, P])
        d_parts = sb("d_parts", [P, 2, 2, P], F32R)
        CHUNK = max(1, NB // 8)

        with phase("consts") as block:
            @block.sync
            def _(e):
                e.dma_start(const[:, :], table).then_inc(S["const_loaded"], 16)
                for dst, src in ((cw, conv_w.rearrange("(j p) o k -> p j (o k)", p=P)),
                                 (cb, conv_b.rearrange("(j p) -> p j", p=P)),
                                 (expA, A_log.partition_broadcast(P)), (dtb, dt_bias.partition_broadcast(P)),
                                 (dpar, D_param.partition_broadcast(P)),
                                 (gb[:, 0:2], bf.rearrange("(j p) -> p j", p=P)),
                                 (gb[:, 2:4], bi.rearrange("(j p) -> p j", p=P)),
                                 (gb[:, 4:6], bc.rearrange("(j p) -> p j", p=P)),
                                 (inc, in_c.rearrange("(j p) -> p j", p=P)),
                                 (bvc, c_bv.rearrange("(j p) -> p j", p=P)),
                                 (bqk_row[:, 0:D], c_bq.partition_broadcast(P)),
                                 (bqk_row[:, D:2 * D], c_bk.partition_broadcast(P)),
                                 (bo2_in, c_bo.partition_broadcast(P)), (bo_row, bo.partition_broadcast(P)),
                                 (nw_row, norm_w.partition_broadcast(P)),
                                 (dt_stage, in_proj[DI + XBC:DI + XBC + NH, :])):
                    with nc.allow_non_contiguous_dma(reason="small vectors, once"):
                        e.dma_start(dst, src).then_inc(S["small_loaded"], 16)
                w0[0](e)

            @block.gpsimd
            def _(e):
                for c in range(NB // CHUNK):
                    e.dma_start(x_res[:, c * CHUNK * D:(c + 1) * CHUNK * D].rearrange("p (b d) -> p b d", d=D),
                                x[c * CHUNK:(c + 1) * CHUNK].rearrange("b t d -> t b d")).then_inc(S[f"x_loaded{c}"], 16)

            @block.tensor
            def _(e):
                e.wait_ge(S["const_loaded"], 16)
                w0[1](e)
                e.wait_ge(S["small_loaded"], 16 * 16)
                for c in range(2):
                    last = e.transpose(bank[4][:, c * NH:c * NH + NH], dt_stage[:, c * P:c * P + P],
                                       ident[0:NH, 0:NH])
                last.then_inc(S["w0_tr"], 1)
                e.wait_ge(S["bv_lo"], 1)
                e.wait_ge(S["w0_lo"], len(jobs0))
                for k in range(2):
                    last = mm3(e, bank[5][:, 0:D], (bvr[:, 0, k:k + 1].to_broadcast([P, P]),
                                                    bvr[:, 1, k:k + 1].to_broadcast([P, P])),
                               (w_co[:, 0, k, :], w_co[:, 1, k, :]), k == 0, k == 1)
                last.then_inc(S["bo2_mm"], 1)

            @block.scalar
            def _(e):
                w0[2](e)
                e.wait_ge(S["w0_tr"], len(jobs0) + 1)
                e.activation(w_dt[:, :, :], bank[4][:, 0:2 * NH].rearrange("p (k n) -> p k n", k=2), ACT.Copy)\
                    .then_inc(S["consts_ready"], 1)
                e.wait_ge(S["small_loaded"], 16 * 16)
                e.activation(expA, expA, ACT.Exp).then_inc(S["consts_ready"], 1)

            @block.vector
            def _(e):
                e.wait_ge(S["const_loaded"], 16)
                e.wait_ge(S["small_loaded"], 16 * 16)
                e.tensor_scalar(small[:, 0:30], small[:, 0:30], 0.5, None, ALU.mult)
                e.tensor_scalar(gb[:, 0:4], gb[:, 0:4], 0.5, None, ALU.mult)
                e.tensor_scalar(inc, inc, 2.0, None, ALU.mult).then_inc(S["halved"], 1)
                e.tensor_scalar(nw_row, nw_row, float(np.sqrt(DI)), None, ALU.mult).then_inc(S["halved"], 1)
                e.tensor_copy(upper_r[:, :], upper)
                e.tensor_copy(bvr[:, 0, :], bvc).then_inc(S["bv_hi"], 1)
                e.wait_ge(S["bv_hi"], 1)
                e.tensor_tensor(bvr[:, 1, :], bvc, bvr[:, 0, :].bitcast(F32), ALU.subtract).then_inc(S["bv_lo"], 1)
                e.wait_ge(S["halved"], 2)
                e.tensor_copy(d_state[:, :, :], inc.unsqueeze(2).to_broadcast([P, 2, P])).then_inc(S["start_state"], 1)
                e.wait_ge(S["start_state"], 1)
                e.tensor_copy(d_parts[:, 0], d_state[:, :, :]).then_inc(S["start_hi"], 1)
                e.wait_ge(S["start_hi"], 1)
                e.tensor_tensor(d_parts[:, 1], d_state[:, :, :], d_parts[:, 0].bitcast(F32), ALU.subtract)\
                    .then_inc(S["start_lo"], 1)
                w0[3](e)
                e.wait_ge(S["bo2_mm"], 1)
                e.tensor_tensor(bo2_row, bank[5][:, 0:D], bo2_in, ALU.add).then_inc(S["bias_rows_ready"], 1)

        stats0 = work[:, 0:NB * 6].rearrange("p (b n) -> p b n", n=6)
        pn = work[:, 512:512 + 4 * NB].rearrange("p (k b) -> p k b", k=4)
        pxn = [work[:, 1024:1280], work[:, 1280:1536]]
        pxT = [work[:, 1536:1792], work[:, 1792:2048]]
        pdt = [work[:, 2048 + 512 * k:2048 + 512 * k + NT] for k in range(4)]
        mean_all, rstd_all = tab3[:, :, 3 * NH], tab3[:, :, 3 * NH + 1]
        dt_bank, cum_bank = bank[4], bank[5]

        def heads_of(a):
            return a.rearrange("p (b h) -> p b h", h=NH)

        with phase("steps") as block:
            @block.vector
            def _(e):
                for c in range(NB // CHUNK):
                    e.wait_ge(S[f"x_loaded{c}"], 16)
                    with e.Fori(c * CHUNK, (c + 1) * CHUNK) as b:
                        e.bn_stats(work[:, ds(b * 6, 6)], x_res[:, ds(b * D, D)])
                n = 0

                def link(i):
                    nonlocal n
                    n += 1
                    i.then_inc(S["p_stats"], 1)
                    e.wait_ge(S["p_stats"], n)

                a, d, v, y = (pn[:, k] for k in range(4))
                link(e.engine_nop())
                e.tensor_tensor(a, stats0[:, :, 1], stats0[:, :, 4], ALU.add)
                e.tensor_tensor(v, stats0[:, :, 2], stats0[:, :, 5], ALU.add)
                link(e.tensor_tensor(d, stats0[:, :, 1], stats0[:, :, 4], ALU.subtract))
                e.tensor_scalar(mean_all, a, 0.5, None, ALU.mult)
                e.tensor_scalar(v, v, 1.0 / D, EPS, ALU.mult, ALU.add)
                link(e.tensor_tensor(d, d, d, ALU.mult))
                link(e.scalar_tensor_tensor(out=v, in0=d, scalar=0.25, in1=v, op0=ALU.mult, op1=ALU.add))
                link(e.tensor_scalar(a.bitcast(I32), v.bitcast(I32), 1, None, ALU.arith_shift_right))
                link(e.tensor_scalar(y.bitcast(I32), a.bitcast(I32), -1.0, float(0x5F3759DF), ALU.mult, ALU.add))
                for k in range(3):
                    link(e.tensor_tensor(a, y, y, ALU.mult))
                    link(e.scalar_tensor_tensor(out=a, in0=a, scalar=-0.5, in1=v, op0=ALU.mult, op1=ALU.mult))
                    link(e.scalar_tensor_tensor(out=rstd_all if k == 2 else y, in0=a, scalar=1.5, in1=y,
                                                op0=ALU.add, op1=ALU.mult))

                def norm(b, k):
                    if past(b - 1): e.wait_ge(S["p_tr"], b - 1)
                    e.tensor_scalar(pxn[k], x_res[:, ds(b * D, D)], tab[:, ds(b * TAB + 3 * NH, 1)],
                                    tab[:, ds(b * TAB + 3 * NH + 1, 1)], ALU.subtract, ALU.mult)\
                        .then_inc(S["p_xn"], 1)

                norm(0, 0)
                norm(1, 1)
                with e.Fori(1, NB // 2) as half:
                    b = 2 * half
                    norm(b, 0)
                    norm(b + 1, 1)
                e.wait_ge(S["p_dt"], NB)
                v, ex, dt, nd = pdt
                link(e.tensor_tensor(heads_of(v), heads_of(dt_bank[:, 0:NT]),
                                     dtb.unsqueeze(1).to_broadcast([P, NB, NH]), ALU.add))
                link(e.tensor_scalar(ex, v, -1.0, None, ALU.mult))
                e.tensor_tensor(ex, ex, v, ALU.min).then_inc(S["p_min"], 1)
                e.wait_ge(S["p_act"], 1)
                link(e.scalar_tensor_tensor(out=dt, in0=v, scalar=0.0, in1=nd, op0=ALU.max, op1=ALU.add))
                e.tensor_copy(tab3[:, :, 2 * NH:3 * NH], heads_of(dt))
                link(e.tensor_tensor(heads_of(nd), heads_of(dt), expA.unsqueeze(1).to_broadcast([P, NB, NH]),
                                     ALU.mult))
                e.tensor_copy(tab3[:, :, 0:NH], heads_of(nd)).then_inc(S["p_nd"], 1)
                e.wait_ge(S["p_cum"], 1)
                e.tensor_copy(tab3[:, :, NH:2 * NH], heads_of(cum_bank[:, 0:NT]))

            @block.tensor
            def _(e):
                def transposes(b, k):
                    e.wait_ge(S["p_xn"], b + 1)
                    if past(b - 1): e.wait_ge(S["p_xnT"], b - 1)
                    for c in range(2):
                        last = e.transpose(bank[k][:, c * P:c * P + P], pxn[k][:, c * P:c * P + P], ident)
                    last.then_inc(S["p_tr"], 1)

                def dt_of(b, k):
                    e.wait_ge(S["p_xnT"], b + 1)
                    for c in range(2):
                        last = e.matmul(dt_bank[:, ds(b * NH, NH)], pxT[k][:, c * P:c * P + P], w_dt[:, c, :],
                                        start=c == 0, stop=c == 1)
                    last.then_inc(S["p_dt"], 1)

                transposes(0, 0)
                transposes(1, 1)
                dt_of(0, 0)
                with e.Fori(1, NB // 2) as half:
                    b = 2 * half
                    transposes(b, 0)
                    dt_of(b - 1, 1)
                    transposes(b + 1, 1)
                    dt_of(b, 0)
                dt_of(NB - 1, 1)
                e.wait_ge(S["p_nd"], 1)
                e.matmul(cum_bank[:, 0:NT], upper, pdt[3], start=True, stop=True).then_inc(S["p_cum"], 1)

            @block.scalar
            def _(e):
                def copy(b, k):
                    e.wait_ge(S["p_tr"], b + 1)
                    if past(b - 1): e.wait_ge(S["p_dt"], b - 1)
                    e.activation(pxT[k], bank[k][:, 0:D], ACT.Copy).then_inc(S["p_xnT"], 1)

                copy(0, 0)
                copy(1, 1)
                with e.Fori(1, NB // 2) as half:
                    b = 2 * half
                    copy(b, 0)
                    copy(b + 1, 1)
                e.wait_ge(S["p_min"], 1)
                e.activation(pdt[1], pdt[1], ACT.Exp).then_inc(S["p_chain"], 1)
                e.wait_ge(S["p_chain"], 1)
                e.activation(pdt[3], pdt[1], ACT.Ln, bias=const[:, C_ONE:C_ONE + 1]).then_inc(S["p_act"], 1)

        wpos[0] = rpos[0] = 0
        m_xn_ = wk(D)
        m_xT = wr(2 * D).rearrange("p (s k t) -> p s k t", s=2, k=2)
        m_raw_ = wk(XBC).rearrange("p (j t) -> p j t", t=P)
        m_acc = wk(XBC).rearrange("p (j t) -> p j t", t=P)
        m_xt_ = wk(DI)
        m_xdt_ = wk(DI)
        m_xD = m_xt_
        m_E = wk(NH * P).rearrange("p (h t) -> p h t", t=P)
        m_zg_ = wk(DI)
        m_y_ = m_raw_[:, 0:4, :].rearrange("p j t -> p (j t)")
        m_yT = wr(2 * DI).rearrange("p (s k t) -> p s k t", s=2, k=4)
        m_Gm = wk(P)
        cur = tiny[:, 0:TAB]
        c_dec, c_dt = cur[:, NH:2 * NH], cur[:, 2 * NH:3 * NH]
        m_ss_, m_xh_, m_t_, m_r_ = (tiny[:, 26 + k:27 + k] for k in range(4))
        ncum = tiny[:, 80:88]
        c_cols, r_cols = stat_cols(32), stat_cols(68)
        c_xn_ = wk(D)
        c_ctx_ = wk(D)
        c_T = wr(4 * D).rearrange("p (s k t) -> p s k t", s=2, k=4)
        c_qk = wk(2 * D)
        c_rot_ = wk(2 * D)
        c_qT = wk(2 * D).rearrange("p (o k t) -> p o k t", o=2, k=2)
        c_kT_ = wk(D).rearrange("p (k t) -> p k t", k=2)
        VX = DH + 1
        c_vx = wk(HEADS * VX).rearrange("p (h d) -> p h d", d=VX)
        c_P = [wk(512), wk(512)]
        c_PT = wk(512)
        c_o_ = c_qk[:, 0:D]
        c_oT = wr(2 * D).rearrange("p (s k t) -> p s k t", s=2, k=2)
        c_mx = tiny[:, 48:52]
        c_ri = tiny[:, 52:68]
        r_xn_ = wk(D)
        r_T = wr(2 * D).rearrange("p (s k t) -> p s k t", s=2, k=2)
        r_tfi_ = sb("r_tfi_", [P, 4, P])
        r_tg_ = sb("r_tg_", [P, 2, P])
        r_xo_ = sb("r_xo_", [P, D])

        def head_cols(blk, odd, g):
            return blk * NH + 2 * g + odd

        def attention_stage(pre, scale, qT, kT, vx, kv_of, Pb, PTb, mx, sc_banks, pt_bank, o_bank, o_free):
            def scores(e, b, g):
                e.wait_ge(S[pre + "_kT"], b + 1)
                e.wait_ge(S[pre + "_qT"], 2 * b + 2)
                bk = sc_banks[g % 2]
                if past(4 * b + g - 1): e.wait_ge(S[pre + "_sub"], 4 * b + g - 1)
                for blk in range(2):
                    for odd in range(2):
                        c = (2 * blk + odd) * P
                        last = e.matmul(bk[:, c:c + P], qT[32 * g:32 * g + 32, odd, blk, :],
                                        kT[32 * g:32 * g + 32, blk, :], start=True, stop=True)
                last.then_inc(S[pre + "_sc"], 1)

            def softmax(e, b, g):
                s3 = sc_banks[g % 2][:, :].rearrange("p (h k) -> p h k", k=P)
                e.wait_ge(S[pre + "_sc"], 4 * b + g + 1)
                if past(4 * b + g): e.wait_ge(S[pre + "_sub"], 4 * b + g)
                e.tensor_reduce(mx, s3, AX.X, ALU.max).then_inc(S[pre + "_max"], 1)
                e.wait_ge(S[pre + "_max"], 4 * b + g + 1)
                if past(4 * b + g - 1): e.wait_ge(S[pre + "_ptr"], 4 * b + g - 1)
                e.tensor_tensor(Pb[g % 2].rearrange("p (h k) -> p h k", k=P), s3,
                                mx.unsqueeze(2).to_broadcast([P, 4, P]), ALU.subtract).then_inc(S[pre + "_sub"], 1)

            def exponents(e, b, g):
                e.wait_ge(S[pre + "_sub"], 4 * b + g + 1)
                e.activation(Pb[g % 2], Pb[g % 2], ACT.Exp, scale=scale).then_inc(S[pre + "_exp"], 1)

            def turn(e, b, g):
                e.wait_ge(S[pre + "_exp"], 4 * b + g + 1)
                if g == 0: e.wait_ge(S[pre + "_v"], b + 1)
                if past(4 * b + g): e.wait_ge(S[pre + "_pt"], 4 * b + g)
                for h in range(4):
                    last = e.transpose(pt_bank[:, h * P:h * P + P], Pb[g % 2][:, h * P:h * P + P], ident)
                last.then_inc(S[pre + "_ptr"], 1)

            def take(e, b, g):
                e.wait_ge(S[pre + "_ptr"], 4 * b + g + 1)
                if past(4 * b + g): e.wait_ge(S[pre + "_pv"], 4 * b + g)
                e.activation(PTb, pt_bank[:, :], ACT.Copy).then_inc(S[pre + "_pt"], 1)

            def values(e, b, g):
                e.wait_ge(S[pre + "_pt"], 4 * b + g + 1)
                if g == 0:
                    e.wait_ge(S[pre + "_v"], b + 1)
                    if past(b): e.wait_ge(S[o_free], b)
                for blk in range(2):
                    for odd in range(2):
                        h, c = head_cols(blk, odd, g), (2 * blk + odd) * P
                        last = e.matmul(o_bank[:, h * VX:h * VX + VX], PTb[:, c:c + P], vx[:, kv_of(h), :],
                                        start=True, stop=True)
                last.then_inc(S[pre + "_pv"], 1)

            def normalise(e, b, o_, ri, free, free_count):
                o3 = o_bank[:, 0:HEADS * VX].rearrange("p (h d) -> p h d", d=VX)
                e.wait_ge(S[pre + "_pv"], 4 * b + 4)
                e.reciprocal(ri, o3[:, :, DH]).then_inc(S[pre + "_rinv"], 1)
                e.wait_ge(S[pre + "_rinv"], b + 1)
                for f, c in zip(free, free_count):
                    if past(c): e.wait_ge(S[f], c)
                e.tensor_tensor(o_.rearrange("p (h d) -> p h d", d=DH), o3[:, :, 0:DH],
                                ri.unsqueeze(2).to_broadcast([P, HEADS, DH]), ALU.mult).then_inc(S[pre + "_o"], 1)

            return dict(scores=scores, softmax=softmax, exponents=exponents, turn=turn, take=take,
                        values=values, normalise=normalise)

        att0 = attention_stage("c", DH ** -0.5, c_qT, c_kT_, c_vx, lambda h: h, c_P, c_PT, c_mx,
                               [bank[3], bank[4]], bank[5], bank[6], "c_o")

        with phase("layer0") as block:
            @block.sync
            def _(e):
                def load_context(b):
                    if past(b): e.wait_ge(S["c_tr"], b)
                    e.dma_start(c_ctx_, tile(ctx, b)).then_inc(S["c_ctx"], 16)

                def store_output(b):
                    e.wait_ge(S["r_xo"], b + 1)
                    e.dma_start(tile(xo_dram, b), r_xo_[:, :]).then_inc(S["r_store"], 16)

                def step(i):
                    b = i
                    if live(b):
                        load_context(b)
                    b = i - 3
                    if live(b):
                        store_output(b)

                pipeline(e, 3, step)
                e.wait_ge(S["r_store"], 16 * NB)

            @block.tensor
            def _(e):
                def m_transpose(b):
                    e.wait_ge(S["m_xn"], b + 1)
                    if past(b): e.wait_ge(S["m_yx"], b)
                    for c in range(2):
                        last = e.transpose(bank[0][:, c * P:c * P + P], m_xn_[:, c * P:c * P + P], ident)
                    last.then_inc(S["m_tr"], 1)

                def m_project(b):
                    e.wait_ge(S["m_lo"], b + 1)
                    if past(b): e.wait_ge(S["m_ylo"], b)
                    for j in range(4):
                        project_T(e, bank[1][:, j * P:j * P + P], m_xT, w_in, DI + j * P)
                    for j in range(2):
                        last = project_T(e, bank[0][:, j * P:j * P + P], m_xT, w_in, 2 * DI + j * P)
                    last.then_inc(S["m_xbc"], 1)

                def m_gate(b):
                    e.wait_ge(S["m_lo"], b + 1)
                    if past(b): e.wait_ge(S["m_x1"], b)
                    project(e, bank[2][:, :], m_xT, w_in, 2, 0, DI).then_inc(S["m_z"], 1)

                def m_tokens(b):
                    e.wait_ge(S["m_xbcs"], b + 1)
                    for j in range(4):
                        last = e.transpose(bank[1][:, j * P:j * P + P], m_acc[:, j, :], ident)
                    last.then_inc(S["m_xtr"], 1)
                    e.matmul(bank[0][:, 0:P], m_acc[:, 4, :], m_acc[:, 5, :], start=True, stop=True)\
                        .then_inc(S["m_g"], 1)

                def m_decays(b, half):
                    e.wait_ge(S["m_cur"], 2 * b + 2)
                    if half == 0:
                        e.wait_ge(S["m_zg"], b + 1)
                    else:
                        e.wait_ge(S["m_xt"], b + 1)
                    for h in range(4):
                        for s in range(2):
                            last = e.matmul(bank[2 - half][:, h * P:h * P + P],
                                            curr[:, s, 4 * half + h:4 * half + h + 1].to_broadcast([P, P]),
                                            upper_r[:, :], start=s == 0, stop=s == 1)
                    last.then_inc(S["m_bc"], 1)

                def m_mix(b, half):
                    e.wait_ge(S["m_M"], 2 * b + 1 + half)
                    if half == 0:
                        e.wait_ge(S["m_xdt"], b + 1)
                        e.wait_ge(S["m_gm"], b + 1)
                    for h in range(4 * half, 4 * half + 4):
                        last = e.matmul(bank[0][:, h * HD:h * HD + HD], m_E[:, h, :],
                                        m_xdt_[:, h * HD:h * HD + HD], start=True, stop=True)
                    last.then_inc(S["m_y"], 1)

                def m_turn(b):
                    e.wait_ge(S["m_y2"], b + 1)
                    e.wait_ge(S["m_rela"], b + 1)
                    for c in range(4):
                        last = e.transpose(bank[1][:, c * P:c * P + P], m_y_[:, c * P:c * P + P], ident)
                    last.then_inc(S["m_ytr"], 1)

                def m_out(b):
                    e.wait_ge(S["m_ylo"], b + 1)
                    e.wait_ge(S["m_relv"], b + 1)
                    project(e, bank[2][:, 0:D], m_yT, w_out, 4, 0, D).then_inc(S["m_out"], 1)

                def c_transpose(b):
                    e.wait_ge(S["c_xn"], b + 1)
                    e.wait_ge(S["c_ctx"], 16 * (b + 1))
                    if past(4 * b): e.wait_ge(S["c_sub"], 4 * b)
                    for c in range(4):
                        src = (c_xn_ if c < 2 else c_ctx_)[:, (c % 2) * P:(c % 2) * P + P]
                        last = e.transpose(bank[3][:, c * P:c * P + P], src, ident)
                    last.then_inc(S["c_tr"], 1)

                def c_project(b):
                    e.wait_ge(S["c_lo"], b + 1)
                    if past(b): e.wait_ge(S["c_x2"], b)
                    if past(b): e.wait_ge(S["c_olo"], b)
                    project(e, bank[4][:, 0:D], c_T[:, :, 0:2, :], w_cq, 2, 0, D).then_inc(S["c_q"], 1)
                    project(e, bank[5][:, :], c_T[:, :, 2:4, :], w_ckv, 2, 0, 2 * D).then_inc(S["c_kv"], 1)

                def c_turn_qk(b):
                    e.wait_ge(S["c_qr"], b + 1)
                    for c in range(4):
                        last = e.transpose(bank[3][:, c * P:c * P + P], c_rot_[:, c * P:c * P + P], ident)
                    last.then_inc(S["c_qtr"], 1)

                def c_turn_o(b):
                    e.wait_ge(S["c_o"], b + 1)
                    e.wait_ge(S["c_pt"], 4 * b + 4)
                    for c in range(2):
                        last = e.transpose(bank[5][:, c * P:c * P + P], c_o_[:, c * P:c * P + P], ident)
                    last.then_inc(S["c_otr"], 1)

                def c_out(b):
                    e.wait_ge(S["c_olo"], b + 1)
                    e.wait_ge(S["c_sub"], 4 * b + 4)
                    project(e, bank[4][:, 0:D], c_oT, w_co, 2, 0, D).then_inc(S["c_proj"], 1)

                def r_transpose(b):
                    e.wait_ge(S["r_xn"], b + 1)
                    if past(b): e.wait_ge(S["r_xo"], b)
                    if past(2 * b): e.wait_ge(S["r_tg"], 2 * b)
                    for c in range(2):
                        last = e.transpose(bank[7][:, c * P:c * P + P], r_xn_[:, c * P:c * P + P], ident)
                    last.then_inc(S["r_tr"], 1)

                def r_forget_input(b):
                    e.wait_ge(S["r_lo"], b + 1)
                    if past(b): e.wait_ge(S["r_dlo"], b)
                    for j in range(4):
                        project_T(e, bank[7][:, j * P:j * P + P], r_T, w_rx, j * P, True, False)
                        last = project_T(e, bank[7][:, j * P:j * P + P], d_parts[:, :, :, :], w_ru, j * P, False, True)
                    last.then_inc(S["r_fi"], 1)

                def r_candidate_out(b):
                    e.wait_ge(S["r_tfi"], 4 * b + 4)
                    for j in range(2):
                        n = 2 * D + j * P
                        project_T(e, bank[7][:, j * P:j * P + P], r_T, w_rx, n, True, False)
                        project_T(e, bank[7][:, j * P:j * P + P], d_parts[:, :, :, :], w_ru, n, False, True)
                    project(e, bank[7][:, D:2 * D], r_T, w_rxo, 2, 0, D).then_inc(S["r_go"], 1)

                def step(i):
                    b = i - 2
                    if live(b):
                        att0["scores"](e, b, 0)
                        att0["scores"](e, b, 1)
                    b = i
                    if live(b):
                        m_transpose(b)
                    b = i - 1
                    if live(b):
                        m_turn(b)
                    b = i - 3
                    if live(b):
                        r_transpose(b)
                    b = i - 2
                    if live(b):
                        att0["scores"](e, b, 2)
                        att0["turn"](e, b, 0)
                        att0["scores"](e, b, 3)
                        att0["values"](e, b, 0)
                        att0["turn"](e, b, 1)
                    b = i
                    if live(b):
                        m_project(b)
                    b = i - 1
                    if live(b):
                        m_out(b)
                    b = i - 2
                    if live(b):
                        att0["values"](e, b, 1)
                        att0["turn"](e, b, 2)
                    b = i - 3
                    if live(b):
                        r_forget_input(b)
                    b = i - 2
                    if live(b):
                        att0["turn"](e, b, 3)
                        att0["values"](e, b, 2)
                    b = i
                    if live(b):
                        m_gate(b)
                    b = i - 2
                    if live(b):
                        att0["values"](e, b, 3)
                    b = i - 1
                    if live(b):
                        c_transpose(b)
                    b = i
                    if live(b):
                        m_tokens(b)
                    b = i - 2
                    if live(b):
                        c_turn_o(b)
                    b = i
                    if live(b):
                        m_decays(b, 0)
                    b = i - 2
                    if live(b):
                        c_out(b)
                    b = i
                    if live(b):
                        m_decays(b, 1)
                    b = i - 1
                    if live(b):
                        c_project(b)
                    b = i - 3
                    if live(b):
                        r_candidate_out(b)
                    b = i
                    if live(b):
                        m_mix(b, 0)
                    b = i - 1
                    if live(b):
                        c_turn_qk(b)
                    b = i
                    if live(b):
                        m_mix(b, 1)

                pipeline(e, 3, step)

            @block.scalar
            def _(e):
                def hi(pre, b, dst, src, *free):
                    e.wait_ge(S[pre + "_tr"], b + 1)
                    for user in free:
                        if past(b): e.wait_ge(S[user], b)
                    e.activation(dst, src, ACT.Copy).then_inc(S[pre + "_hi"], 1)

                def m_taps(b):
                    e.wait_ge(S["m_xbc"], b + 1)
                    if past(b): e.wait_ge(S["m_xbcs"], b)
                    if past(b): e.wait_ge(S["m_ytr"], b)
                    if past(b): e.wait_ge(S["m_ss"], b)
                    e.activation(m_raw_[:, 0:4, :], bank[1][:, :].rearrange("p (j t) -> p j t", t=P), ACT.Copy)
                    e.activation(m_raw_[:, 4:6, :], bank[0][:, 0:2 * P].rearrange("p (j t) -> p j t", t=P), ACT.Copy)\
                        .then_inc(S["m_raw"], 1)
                    e.wait_ge(S["m_raw"], b + 1)
                    if past(b): e.wait_ge(S["m_g"], b)
                    if past(b): e.wait_ge(S["m_xtr"], b)
                    for j in range(6):
                        last = e.activation(m_acc[:, j, :], m_raw_[:, j, :], ACT.Identity,
                                            bias=cb[:, j:j + 1], scale=cw[:, j, CONV - 1:CONV])
                    last.then_inc(S["m_tap"], 1)

                def m_gate(b):
                    e.wait_ge(S["m_z"], b + 1)
                    if past(b): e.wait_ge(S["m_y2"], b)
                    e.activation(m_zg_, bank[2][:, :], ACT.Tanh, scale=0.5).then_inc(S["m_ztanh"], 1)

                def m_silu(b):
                    e.wait_ge(S["m_conv"], b + 1)
                    e.activation(m_raw_, m_acc, ACT.Tanh).then_inc(S["m_xtanh"], 1)

                def m_tokens(b):
                    e.wait_ge(S["m_xtr"], b + 1)
                    if past(b): e.wait_ge(S["m_yx"], b)
                    if past(b): e.wait_ge(S["m_xdt"], b)
                    e.activation(m_xt_, bank[1][:, :], ACT.Copy).then_inc(S["m_xt"], 1)

                def m_exp(b, half):
                    if half == 1:
                        e.wait_ge(S["m_bc"], 2 * b + 2)
                        e.wait_ge(S["m_cur"], 2 * b + 2)
                        if past(2 * b): e.wait_ge(S["m_y"], 2 * b)
                        for h in range(4, 8):
                            last = e.activation(m_E[:, h, :], bank[1][:, (h - 4) * P:(h - 3) * P], ACT.Relu,
                                                bias=ncum[:, h:h + 1])
                        last.then_inc(S["m_rela"], 1)
                        e.wait_ge(S["m_rela"], b + 1)
                    else:
                        e.wait_ge(S["m_relv"], b + 1)
                    e.activation(m_E[:, 4 * half:4 * half + 4, :], m_E[:, 4 * half:4 * half + 4, :], ACT.Exp,
                                 scale=-1.0).then_inc(S["m_exp"], 1)

                def m_square(b):
                    e.wait_ge(S["m_y2"], b + 1)
                    if past(12 * b): e.wait_ge(S["m_rs"], 12 * b)
                    e.activation(m_E[:, 0:4, :].rearrange("p h t -> p (h t)"), m_y_, ACT.Square, accum_out=m_ss_)\
                        .then_inc(S["m_ss"], 1)

                def m_yhi(b):
                    e.wait_ge(S["m_ytr"], b + 1)
                    if past(b): e.wait_ge(S["m_out"], b)
                    e.activation(m_yT[:, 0], bank[1][:, :].rearrange("p (k t) -> p k t", t=P), ACT.Copy)\
                        .then_inc(S["m_yhi"], 1)

                def c_values(b):
                    e.wait_ge(S["c_kb"], b + 1)
                    if past(4 * b): e.wait_ge(S["c_pv"], 4 * b)
                    e.activation(c_vx[:, :, 0:DH], bank[5][:, D:2 * D].rearrange("p (h d) -> p h d", d=DH), ACT.Copy)\
                        .then_inc(S["c_v"], 1)

                def c_heads(b):
                    e.wait_ge(S["c_qtr"], b + 1)
                    if past(4 * b): e.wait_ge(S["c_sc"], 4 * b)
                    e.activation(c_kT_, bank[3][:, D:2 * D].rearrange("p (k t) -> p k t", k=2), ACT.Copy)\
                        .then_inc(S["c_kT"], 1)
                    for odd, mask in enumerate((m_even, m_odd)):
                        e.activation(c_qT[:, odd], bank[3][:, 0:D].rearrange("p (k t) -> p k t", k=2),
                                     ACT.Copy, scale=mask).then_inc(S["c_qT"], 1)

                def c_ohi(b):
                    e.wait_ge(S["c_otr"], b + 1)
                    if past(b): e.wait_ge(S["c_proj"], b)
                    e.activation(c_oT[:, 0], bank[5][:, 0:D].rearrange("p (k t) -> p k t", k=2), ACT.Copy)\
                        .then_inc(S["c_ohi"], 1)

                def r_gates(b):
                    e.wait_ge(S["r_fi"], b + 1)
                    if past(b): e.wait_ge(S["r_d"], b)
                    for j in range(4):
                        e.activation(r_tfi_[:, j, :], bank[7][:, j * P:j * P + P], ACT.Tanh, scale=0.5,
                                     bias=gb[:, j:j + 1]).then_inc(S["r_tfi"], 1)

                def r_candidate(b):
                    e.wait_ge(S["r_go"], b + 1)
                    for j in range(2):
                        e.activation(r_tg_[:, j, :], bank[7][:, j * P:j * P + P], ACT.Tanh,
                                     bias=gb[:, 4 + j:5 + j]).then_inc(S["r_tg"], 1)
                    if past(16 * b): e.wait_ge(S["r_store"], 16 * b)
                    e.activation(r_xo_[:, :], bank[7][:, D:2 * D], ACT.Copy).then_inc(S["r_xo"], 1)

                def r_state_hi(b):
                    e.wait_ge(S["r_d"], b + 1)
                    e.wait_ge(S["r_go"], b + 1)
                    e.activation(d_parts[:, 0], d_state[:, :, :], ACT.Copy).then_inc(S["r_dhi"], 1)

                def step(i):
                    b = i - 2
                    if live(b):
                        att0["exponents"](e, b, 0)
                    b = i
                    if live(b):
                        hi("m", b, m_xT[:, 0], bank[0][:, 0:D].rearrange("p (k t) -> p k t", k=2), "m_xbc", "m_z")
                    b = i - 1
                    if live(b):
                        m_yhi(b)
                    b = i - 3
                    if live(b):
                        hi("r", b, r_T[:, 0], bank[7][:, 0:D].rearrange("p (k t) -> p k t", k=2), "r_go")
                    b = i - 2
                    if live(b):
                        att0["take"](e, b, 0)
                        att0["exponents"](e, b, 1)
                        att0["exponents"](e, b, 2)
                    b = i - 1
                    if live(b):
                        m_square(b)
                    b = i - 2
                    if live(b):
                        att0["take"](e, b, 1)
                    b = i - 4
                    if live(b):
                        r_state_hi(b)
                    b = i
                    if live(b):
                        m_taps(b)
                    b = i - 2
                    if live(b):
                        att0["take"](e, b, 2)
                        att0["exponents"](e, b, 3)
                    b = i
                    if live(b):
                        m_silu(b)
                    b = i - 2
                    if live(b):
                        att0["take"](e, b, 3)
                    b = i
                    if live(b):
                        m_gate(b)
                    b = i - 1
                    if live(b):
                        hi("c", b, c_T[:, 0], bank[3][:, :].rearrange("p (k t) -> p k t", k=4), "c_kv")
                    b = i - 2
                    if live(b):
                        c_ohi(b)
                    b = i
                    if live(b):
                        m_tokens(b)
                    b = i - 3
                    if live(b):
                        r_gates(b)
                    b = i
                    if live(b):
                        m_exp(b, 0)
                        m_exp(b, 1)
                    b = i - 1
                    if live(b):
                        c_heads(b)
                        c_values(b)
                    b = i - 3
                    if live(b):
                        r_candidate(b)

                pipeline(e, 4, step)

            @block.vector
            def _(e):
                def lo(pre, b, dst, src, high):
                    e.wait_ge(S[pre + "hi"], b + 1)
                    e.tensor_tensor(dst, src, high.bitcast(F32), ALU.subtract).then_inc(S[pre + "lo"], 1)

                def apply_norm(pre, b, dst, src, mean, rstd):
                    e.tensor_scalar(dst, src, mean, rstd, ALU.subtract, ALU.mult).then_inc(S[pre + "_xn"], 1)

                def m_current(b):
                    if past(2 * b): e.wait_ge(S["m_bc"], 2 * b)
                    if past(b): e.wait_ge(S["m_xdt"], b)
                    if past(b): e.wait_ge(S["m_rela"], b)
                    if past(b): e.wait_ge(S["m_relv"], b)
                    e.tensor_scalar(curr[:, 0, :], tab[:, ds(b * TAB, NH)], 1.0, None, ALU.mult)
                    e.tensor_scalar(ncum, tab[:, ds(b * TAB + NH, NH)], -1.0, None, ALU.mult)
                    e.tensor_scalar(cur, tab[:, ds(b * TAB, TAB)], 1.0, None, ALU.mult).then_inc(S["m_cur"], 1)
                    e.wait_ge(S["m_cur"], 2 * b + 1)
                    e.tensor_tensor(curr[:, 1, :], cur[:, 0:NH], curr[:, 0, :].bitcast(F32), ALU.subtract)\
                        .then_inc(S["m_cur"], 1)
                    if past(b): e.wait_ge(S["m_tr"], b)
                    apply_norm("m", b, m_xn_, x_res[:, ds(b * D, D)], cur[:, 3 * NH:3 * NH + 1],
                               cur[:, 3 * NH + 1:3 * NH + 2])

                def m_convolve(b):
                    e.wait_ge(S["m_tap"], b + 1)
                    for k in range(1, CONV):
                        if k > 1:
                            e.wait_ge(S["m_conv2"], 2 * b + k - 1)
                        for j in range(6):
                            last = e.scalar_tensor_tensor(
                                out=m_acc[:, j, k:P], in0=m_raw_[:, j, 0:P - k],
                                scalar=cw[:, j, CONV - 1 - k:CONV - k], in1=m_acc[:, j, k:P],
                                op0=ALU.mult, op1=ALU.add)
                        last.then_inc(S["m_conv2" if k < CONV - 1 else "m_conv"], 1)

                def m_silu(b):
                    e.wait_ge(S["m_xtanh"], b + 1)
                    e.scalar_tensor_tensor(out=m_acc, in0=m_raw_, scalar=1.0, in1=m_acc,
                                           op0=ALU.add, op1=ALU.mult).then_inc(S["m_xbcs"], 1)

                def m_gate(b):
                    e.wait_ge(S["m_ztanh"], b + 1)
                    e.scalar_tensor_tensor(out=m_zg_, in0=m_zg_, scalar=1.0, in1=bank[2][:, :],
                                           op0=ALU.add, op1=ALU.mult).then_inc(S["m_zg"], 1)

                def m_masked(b):
                    e.wait_ge(S["m_g"], b + 1)
                    if past(b): e.wait_ge(S["m_M"], 2 * b)
                    e.tensor_tensor(m_Gm, bank[0][:, 0:P], upper, ALU.mult).then_inc(S["m_gm"], 1)

                def m_relative(b):
                    e.wait_ge(S["m_bc"], 2 * b + 1)
                    if past(2 * b): e.wait_ge(S["m_y"], 2 * b)
                    if past(b): e.wait_ge(S["m_ss"], b)
                    for h in range(4):
                        last = e.tensor_scalar(m_E[:, h, :], bank[2][:, h * P:h * P + P], c_dec[:, h:h + 1], 0.0,
                                               ALU.subtract, ALU.max)
                    last.then_inc(S["m_relv"], 1)

                def m_weights(b, half):
                    e.wait_ge(S["m_exp"], 2 * b + 1 + half)
                    part = m_E[:, 4 * half:4 * half + 4, :]
                    if half == 0:
                        e.wait_ge(S["m_gm"], b + 1)
                    e.tensor_tensor(part, part, m_Gm.unsqueeze(1).to_broadcast([P, 4, P]), ALU.mult)\
                        .then_inc(S["m_M"], 1)

                def m_gated(b):
                    e.wait_ge(S["m_y"], 2 * b + 2)
                    e.wait_ge(S["m_xd"], b + 1)
                    if past(b): e.wait_ge(S["m_ytr"], b)
                    e.tensor_tensor(m_y_, bank[0][:, :], m_xD, ALU.add).then_inc(S["m_yx"], 1)
                    e.wait_ge(S["m_yx"], b + 1)
                    e.tensor_tensor(m_y_, m_y_, m_zg_, ALU.mult).then_inc(S["m_y2"], 1)

                def m_root(b):
                    e.wait_ge(S["m_ss"], b + 1)
                    e.tensor_scalar(m_ss_, m_ss_, float(4 * DI * EPS), None, ALU.add).then_inc(S["m_seed"], 1)
                    if past(b): e.wait_ge(S["m_x1"], b)
                    rsqrt_seed(e, m_ss_, m_xh_, m_t_, m_r_, "m_seed", b)

                def m_ylow(b):
                    e.wait_ge(S["m_yhi"], b + 1)
                    e.tensor_tensor(m_yT[:, 1], bank[1][:, :].rearrange("p (k t) -> p k t", t=P),
                                    m_yT[:, 0].bitcast(F32), ALU.subtract).then_inc(S["m_ylo"], 1)

                def m_residual(b):
                    e.wait_ge(S["m_out"], b + 1)
                    e.wait_ge(S["m_rs"], 12 * b + 12)
                    e.scalar_tensor_tensor(out=x_res[:, ds(b * D, D)], in0=bank[2][:, 0:D], scalar=m_r_, in1=x_res[:, ds(b * D, D)],
                                           op0=ALU.mult, op1=ALU.add).then_inc(S["m_x1"], 1)

                def c_norm(b):
                    e.wait_ge(S["c_rs"], 12 * b + 12)
                    if past(b): e.wait_ge(S["c_tr"], b)
                    apply_norm("c", b, c_xn_, x_res[:, ds(b * D, D)], c_cols[1][:, 0:1], c_cols[5])

                def c_bias(b):
                    e.wait_ge(S["c_kv"], b + 1)
                    if past(b): e.wait_ge(S["c_otr"], b)
                    e.tensor_tensor(c_qk[:, D:2 * D], bank[5][:, 0:D], bqk_row[:, D:2 * D], ALU.add)\
                        .then_inc(S["c_kb"], 1)
                    e.tensor_tensor(c_qk[:, 0:D], bank[4][:, 0:D], bqk_row[:, 0:D], ALU.add).then_inc(S["c_qb"], 1)

                def c_rotate(b):
                    e.wait_ge(S["c_rot"], b + 1)
                    e.tensor_tensor(c_qk.rearrange("p (h d) -> p h d", d=DH), c_qk.rearrange("p (h d) -> p h d", d=DH),
                                    const[:, C_COS:C_COS + DH].unsqueeze(1).to_broadcast([P, 2 * HEADS, DH]),
                                    ALU.mult).then_inc(S["c_cos"], 1)
                    e.wait_ge(S["c_cos"], b + 1)
                    e.tensor_tensor(c_rot_, c_rot_, c_qk, ALU.add).then_inc(S["c_qr"], 1)

                def c_residual(b):
                    e.wait_ge(S["c_proj"], b + 1)
                    e.wait_ge(S["c_x1b"], b + 1)
                    e.tensor_tensor(x_res[:, ds(b * D, D)], bank[4][:, 0:D], x_res[:, ds(b * D, D)], ALU.add).then_inc(S["c_x2"], 1)

                def r_norm(b):
                    e.wait_ge(S["r_rs"], 12 * b + 12)
                    if past(b): e.wait_ge(S["r_tr"], b)
                    apply_norm("r", b, r_xn_, x_res[:, ds(b * D, D)], r_cols[1][:, 0:1], r_cols[5])

                def r_update(b):
                    e.wait_ge(S["r_tfi"], 4 * b + 4)
                    if past(b): e.wait_ge(S["r_dhi"], b)
                    e.scalar_tensor_tensor(out=r_tfi_[:, 0:2, :], in0=r_tfi_[:, 0:2, :], scalar=1.0,
                                           in1=d_state[:, :, :], op0=ALU.add, op1=ALU.mult).then_inc(S["r_a"], 1)
                    e.wait_ge(S["r_tg"], 2 * b + 2)
                    e.scalar_tensor_tensor(out=r_tfi_[:, 2:4, :], in0=r_tfi_[:, 2:4, :], scalar=1.0,
                                           in1=r_tg_[:, :, :], op0=ALU.add, op1=ALU.mult).then_inc(S["r_b"], 1)
                    e.wait_ge(S["r_b"], b + 1)
                    e.scalar_tensor_tensor(out=d_state[:, :, :], in0=r_tfi_[:, 0:2, :], scalar=0.5,
                                           in1=r_tfi_[:, 2:4, :], op0=ALU.mult, op1=ALU.add)\
                        .then_inc(S["r_d"], 1)

                def r_state_lo(b):
                    e.wait_ge(S["r_dhi"], b + 1)
                    e.tensor_tensor(d_parts[:, 1], d_state[:, :, :], d_parts[:, 0].bitcast(F32), ALU.subtract)\
                        .then_inc(S["r_dlo"], 1)

                e.memset(c_vx[:, :, DH:VX], 1.0)

                def step(i):
                    b = i - 3
                    if live(b):
                        r_norm(b)
                    b = i
                    if live(b):
                        m_current(b)
                    b = i - 1
                    if live(b):
                        m_gated(b)
                    b = i - 2
                    if live(b):
                        att0["softmax"](e, b, 0)
                        att0["softmax"](e, b, 1)
                    b = i - 1
                    if live(b):
                        m_ylow(b)
                    b = i - 2
                    if live(b):
                        att0["softmax"](e, b, 2)
                    b = i
                    if live(b):
                        lo("m_", b, m_xT[:, 1], bank[0][:, 0:D].rearrange("p (k t) -> p k t", k=2), m_xT[:, 0])
                    b = i - 4
                    if live(b):
                        r_update(b)
                        r_state_lo(b)
                    b = i - 1
                    if live(b):
                        m_root(b)
                    b = i - 2
                    if live(b):
                        att0["softmax"](e, b, 3)
                    b = i - 3
                    if live(b):
                        lo("r_", b, r_T[:, 1], bank[7][:, 0:D].rearrange("p (k t) -> p k t", k=2), r_T[:, 0])
                    b = i - 1
                    if live(b):
                        m_residual(b)
                        row_statistics(e, "c", b, x_res[:, ds(b * D, D)], c_cols, ("m_x1", b + 1))
                    b = i
                    if live(b):
                        m_convolve(b)
                    b = i - 1
                    if live(b):
                        c_norm(b)
                    b = i
                    if live(b):
                        m_silu(b)
                        m_gate(b)
                    b = i - 2
                    if live(b):
                        att0["normalise"](e, b, c_o_, c_ri, ["c_otr"], [b])
                    b = i - 1
                    if live(b):
                        lo("c_", b, c_T[:, 1], bank[3][:, :].rearrange("p (k t) -> p k t", k=4), c_T[:, 0])
                    b = i - 2
                    if live(b):
                        lo("c_o", b, c_oT[:, 1], bank[5][:, 0:D].rearrange("p (k t) -> p k t", k=2), c_oT[:, 0])
                        c_residual(b)
                    b = i
                    if live(b):
                        m_masked(b)
                    b = i - 2
                    if live(b):
                        row_statistics(e, "r", b, x_res[:, ds(b * D, D)], r_cols, ("c_x2", b + 1))
                    b = i
                    if live(b):
                        m_relative(b)
                    b = i - 1
                    if live(b):
                        c_bias(b)
                    b = i
                    if live(b):
                        m_weights(b, 0)
                    b = i - 1
                    if live(b):
                        c_rotate(b)
                    b = i
                    if live(b):
                        m_weights(b, 1)

                pipeline(e, 4, step)

            @block.gpsimd
            def _(e):
                def scale_tokens(b):
                    x3 = m_xt_.rearrange("p (h d) -> p h d", d=HD)
                    e.wait_ge(S["m_xt"], b + 1)
                    e.wait_ge(S["m_cur"], 2 * b + 2)
                    if past(2 * b): e.wait_ge(S["m_y"], 2 * b)
                    e.tensor_tensor(m_xdt_.rearrange("p (h d) -> p h d", d=HD), x3,
                                    c_dt.unsqueeze(2).to_broadcast([P, NH, HD]), ALU.mult).then_inc(S["m_xdt"], 1)
                    e.wait_ge(S["m_xdt"], b + 1)
                    e.tensor_tensor(m_xD.rearrange("p (h d) -> p h d", d=HD), x3,
                                    dpar.unsqueeze(2).to_broadcast([P, NH, HD]), ALU.mult).then_inc(S["m_xd"], 1)

                def rotate(b):
                    e.wait_ge(S["c_kb"], b + 1)
                    e.wait_ge(S["c_qb"], b + 1)
                    if past(b): e.wait_ge(S["c_qtr"], b)
                    e.tensor_tensor(c_rot_.rearrange("p (h o d) -> p h o d", o=2, d=DH // 2),
                                    c_qk.rearrange("p (h o d) -> p h o d", o=2, d=DH // 2)[:, :, ::-1, :],
                                    const[:, C_SIN:C_SIN + DH].rearrange("p (o d) -> p o d", o=2).unsqueeze(1)
                                    .to_broadcast([P, 2 * HEADS, 2, DH // 2]), ALU.mult).then_inc(S["c_rot"], 1)

                def add_bias(b):
                    e.wait_ge(S["c_xn"], b + 1)
                    e.tensor_tensor(x_res[:, ds(b * D, D)], x_res[:, ds(b * D, D)], bo2_row, ALU.add).then_inc(S["c_x1b"], 1)

                def newton(pre, b, xh_, t_, y_):
                    e.wait_ge(S[pre + "_seed"], 3 * b + 3)
                    rsqrt_newton(e, xh_, t_, y_, pre + "_rs", 12 * b)

                def step(i):
                    b = i - 1
                    if live(b):
                        newton("m", b, m_xh_, m_t_, m_r_)
                        newton("c", b, *c_cols[3:])
                    b = i
                    if live(b):
                        scale_tokens(b)
                    b = i - 1
                    if live(b):
                        add_bias(b)
                        rotate(b)
                    b = i - 2
                    if live(b):
                        newton("r", b, *r_cols[3:])

                pipeline(e, 2, step)

        v_row, dbv_row = rows[:, 0:D], rows[:, D:2 * D]
        NQ = D + 2 * KV * DH
        qkv_stage = work[:, 0:2 * NQ].rearrange("p (k n) -> p k n", k=2)
        so_stage = work[:, 768:768 + 2 * D].rearrange("p (k n) -> p k n", k=2)
        gate_stage = work[0:E, 1280:1280 + D]
        jobs1 = []
        for r in range(2):
            jobs1 += [(uo[r * P:(r + 1) * P, :], D, to(w_uo, r * P), 0.5, None),
                      (d_Wq[r * P:(r + 1) * P, :], D, to(w_dq, r * P), 1.0, None),
                      (d_Wk[r * P:(r + 1) * P, :], D, to(w_dk, r * P), 1.0, None),
                      (d_Wv[r * P:(r + 1) * P, :], D, to(w_dv, r * P), 1.0, None)]
        w1 = weights("w1", 4, work[:, 2048:4096], jobs1)
        with phase("between") as block:
            @block.sync
            def _(e):
                for dst, src in ((qkv_stage[:, :, 0:D], s_wq.rearrange("(k p) n -> p k n", p=P)),
                                 (qkv_stage[:, :, D:D + KV * DH], s_wk.rearrange("(k p) n -> p k n", p=P)),
                                 (qkv_stage[:, :, D + KV * DH:NQ], s_wv.rearrange("(k p) n -> p k n", p=P)),
                                 (so_stage, s_wo.rearrange("(k p) n -> p k n", p=P)),
                                 (gcol, s_g.rearrange("(j p) -> p j", p=P)),
                                 (dbq, d_bq.rearrange("(j p) -> p j", p=P)),
                                 (dbk, d_bk.rearrange("(j p) -> p j", p=P)),
                                 (dbv_row, d_bv.partition_broadcast(P)), (lbb, lb_bias.partition_broadcast(P)),
                                 (gate_stage, gate_w)):
                    with nc.allow_non_contiguous_dma(reason="small vectors, once"):
                        e.dma_start(dst, src).then_inc(S["l1_small"], 16)
                w1[0](e)

            @block.tensor
            def _(e):
                w1[1](e)
                e.wait_ge(S["l1_small"], 160)
                for c in range(2):
                    last = e.transpose(bank[4][:, c * E:c * E + E], gate_stage[:, c * P:c * P + P], ident[0:E, 0:E])
                last.then_inc(S["w1_tr"], 1)
                e.wait_ge(S["w1_lo"], len(jobs1))
                project(e, bank[5][:, 0:D], d_parts[:, :, :, :], w_uo, 2, 0, D).then_inc(S["b_v"], 1)

            @block.scalar
            def _(e):
                w1[2](e)
                e.wait_ge(S["w1_tr"], len(jobs1) + 1)
                e.activation(w_gate[:, :, :], bank[4][:, 0:2 * E].rearrange("p (k n) -> p k n", k=2), ACT.Copy)\
                    .then_inc(S["b_dhi"], 1)
                e.wait_ge(S["l1_wg"], 1)
                e.activation(w_sqkv[:, 0], qkv_stage, ACT.Copy).then_inc(S["l1_whi"], 1)
                e.activation(w_so[:, 0], so_stage, ACT.Copy).then_inc(S["l1_whi"], 1)

            @block.vector
            def _(e):
                e.wait_ge(S["l1_small"], 160)
                for k in range(2):
                    last = e.tensor_scalar(qkv_stage[:, k, :], qkv_stage[:, k, :], gcol[:, k:k + 1], None, ALU.mult)
                last.then_inc(S["l1_wg"], 1)
                w1[3](e)
                e.wait_ge(S["l1_whi"], 2)
                e.tensor_tensor(w_sqkv[:, 1], qkv_stage, w_sqkv[:, 0].bitcast(F32), ALU.subtract)
                e.tensor_tensor(w_so[:, 1], so_stage, w_so[:, 0].bitcast(F32), ALU.subtract).then_inc(S["l1_wlo"], 1)
                e.wait_ge(S["b_v"], 1)
                e.tensor_tensor(v_row, bank[5][:, 0:D], bo_row, ALU.add).then_inc(S["b_vrow"], 1)

        wpos[0] = rpos[0] = 0
        s_xo_ = wk(D)
        s_h_ = wk(D)
        s_xn_ = wk(D)
        s_T = wr(2 * D).rearrange("p (s k t) -> p s k t", s=2, k=2)
        NR = D + 2 * KV * DH
        s_qr_ = wk(NR)
        s_qT_ = wk(2 * D).rearrange("p (o k t) -> p o k t", o=2, k=2)
        s_kT_ = wk(P)
        s_vx = wk(KV * VX).rearrange("p (h d) -> p h d", d=VX)
        s_P = [wk(512), wk(512)]
        s_PT = wk(512)
        s_o_ = wk(D)
        s_oT = wr(2 * D).rearrange("p (s k t) -> p s k t", s=2, k=2)
        s_mx, s_ri = tiny[:, 0:4], tiny[:, 4:20]

        s_cols, d_cols, g_cols = stat_cols(20), stat_cols(32), stat_cols(44)
        d_xn_ = wk(D)
        d_ctx_ = wk(D)
        d_T = wr(4 * D).rearrange("p (s k t) -> p s k t", s=2, k=4)
        d_qkT = wk(4 * P).rearrange("p (k t) -> p k t", k=4)
        d_v_ = wk(D)
        d_P_ = wk(P)
        d_PT = wk(P)
        d_mx, d_nm, d_sum, d_ri = (tiny[:, 56 + k:57 + k] for k in range(4))
        g_xn_ = wk(D)
        g_T = wk(D)
        g_mr = tiny[:, 60:62]

        att1 = attention_stage("s", 1.0 / float(np.sqrt(D)), s_qT_, s_kT_.unsqueeze(1).to_broadcast([P, 2, P]),
                               s_vx, lambda h: h % KV, s_P, s_PT, s_mx, [bank[2], bank[3]], bank[4], bank[1], "s_x4")

        with phase("layer1") as block:
            @block.sync
            def _(e):
                def load_output(b):
                    if past(b): e.wait_ge(S["s_u"], b)
                    e.dma_start(s_xo_, tile(xo_dram, b)).then_inc(S["s_xo"], 16)

                def load_context(b):
                    if past(b): e.wait_ge(S["d_tr"], b)
                    e.dma_start(d_ctx_, tile(ctx, b)).then_inc(S["d_ctx"], 16)

                def step(i):
                    b = i
                    if live(b):
                        load_output(b)
                    b = i - 2
                    if live(b):
                        load_context(b)

                pipeline(e, 2, step)

            @block.tensor
            def _(e):
                def s_transpose(b):
                    e.wait_ge(S["s_xn"], b + 1)
                    if past(b): e.wait_ge(S["s_qT"], 2 * b)
                    for c in range(2):
                        last = e.transpose(bank[0][:, c * P:c * P + P], s_xn_[:, c * P:c * P + P], ident)
                    last.then_inc(S["s_tr"], 1)

                def s_project(b):
                    e.wait_ge(S["s_lo"], b + 1)
                    project(e, bank[0][:, 0:NQ], s_T, w_sqkv, 2, 0, NQ).then_inc(S["s_qkv"], 1)

                def s_turn_qk(b):
                    e.wait_ge(S["s_qr"], 2 * b + 2)
                    e.wait_ge(S["s_v"], b + 1)
                    for c in range(3):
                        last = e.transpose(bank[0][:, c * P:c * P + P], s_qr_[:, c * P:c * P + P], ident)
                    last.then_inc(S["s_qtr"], 1)

                def s_turn_o(b):
                    e.wait_ge(S["s_o"], b + 1)
                    for c in range(2):
                        last = e.transpose(bank[1][:, c * P:c * P + P], s_o_[:, c * P:c * P + P], ident)
                    last.then_inc(S["s_otr"], 1)

                def s_out(b):
                    e.wait_ge(S["s_olo"], b + 1)
                    project(e, bank[1][:, 0:D], s_oT, w_so, 2, 0, D).then_inc(S["s_proj"], 1)

                def d_transpose(b):
                    e.wait_ge(S["d_xn"], b + 1)
                    e.wait_ge(S["d_ctx"], 16 * (b + 1))
                    if past(b): e.wait_ge(S["d_qk_sb"], b)
                    for c in range(4):
                        src = (d_xn_ if c < 2 else d_ctx_)[:, (c % 2) * P:(c % 2) * P + P]
                        last = e.transpose(bank[5][:, c * P:c * P + P], src, ident)
                    last.then_inc(S["d_tr"], 1)

                def d_project(b):
                    e.wait_ge(S["d_lo"], b + 1)
                    for c in range(4):
                        last = project_T(e, bank[5][:, c * P:c * P + P], d_T[:, :, 2 * (c // 2):2 * (c // 2) + 2, :],
                                         w_dq if c < 2 else w_dk, (c % 2) * P)
                    last.then_inc(S["d_qk"], 1)
                    if past(b): e.wait_ge(S["d_x5"], b)
                    project(e, bank[6][:, 0:D], d_T[:, :, 2:4, :], w_dv, 2, 0, D).then_inc(S["d_vmm"], 1)

                def d_scores(b):
                    e.wait_ge(S["d_qk_sb"], b + 1)
                    e.wait_ge(S["d_v"], b + 1)
                    for k in range(2):
                        last = e.matmul(bank[6][:, 0:P], d_qkT[:, k, :], d_qkT[:, 2 + k, :], start=k == 0, stop=k == 1)
                    last.then_inc(S["d_sc"], 1)

                def d_turn(b):
                    e.wait_ge(S["d_exp"], b + 1)
                    e.transpose(bank[6][:, 0:P], d_P_, ident).then_inc(S["d_ptr"], 1)

                def d_values(b):
                    e.wait_ge(S["d_pt"], b + 1)
                    e.matmul(bank[6][:, 0:D], d_PT, d_v_, start=True, stop=True).then_inc(S["d_pv"], 1)

                def g_transpose(b):
                    e.wait_ge(S["g_xn"], b + 1)
                    if past(b): e.wait_ge(S["g_lg"], b)
                    for c in range(2):
                        last = e.transpose(bank[7][:, c * P:c * P + P], g_xn_[:, c * P:c * P + P], ident)
                    last.then_inc(S["g_tr"], 1)

                def g_logits(b):
                    e.wait_ge(S["g_xnT"], b + 1)
                    for c in range(2):
                        last = e.matmul(bank[7][:, D:D + E], g_T[:, c * P:c * P + P], w_gate[:, c, :],
                                        start=c == 0, stop=c == 1)
                    last.then_inc(S["g_sum"], 1)

                def step(i):
                    b = i - 2
                    if live(b):
                        att1["turn"](e, b, 3)
                    b = i - 4
                    if live(b):
                        d_turn(b)
                    b = i - 3
                    if live(b):
                        d_transpose(b)
                    b = i - 2
                    if live(b):
                        att1["values"](e, b, 3)
                    b = i - 4
                    if live(b):
                        d_values(b)
                    b = i - 1
                    if live(b):
                        s_turn_qk(b)
                    b = i - 3
                    if live(b):
                        d_project(b)
                    b = i - 1
                    if live(b):
                        att1["scores"](e, b, 0)
                    b = i - 2
                    if live(b):
                        s_turn_o(b)
                    b = i - 1
                    if live(b):
                        att1["scores"](e, b, 1)
                    b = i
                    if live(b):
                        s_transpose(b)
                    b = i - 3
                    if live(b):
                        d_scores(b)
                    b = i - 4
                    if live(b):
                        g_transpose(b)
                    b = i - 2
                    if live(b):
                        s_out(b)
                    b = i - 1
                    if live(b):
                        att1["turn"](e, b, 0)
                        att1["scores"](e, b, 2)
                        att1["values"](e, b, 0)
                        att1["turn"](e, b, 1)
                        att1["scores"](e, b, 3)
                        att1["values"](e, b, 1)
                    b = i - 4
                    if live(b):
                        g_logits(b)
                    b = i - 1
                    if live(b):
                        att1["turn"](e, b, 2)
                    b = i
                    if live(b):
                        s_project(b)
                    b = i - 1
                    if live(b):
                        att1["values"](e, b, 2)

                pipeline(e, 4, step)

            @block.scalar
            def _(e):
                def copy(ready, count, dst, src, done, free=None):
                    if past(count): e.wait_ge(S[ready], count)
                    if free and past(free[1]): e.wait_ge(S[free[0]], free[1])
                    e.activation(dst, src, ACT.Copy).then_inc(S[done], 1)

                def blocks(bk, n):
                    return bank[bk][:, 0:n * P].rearrange("p (k t) -> p k t", k=n)

                def s_tanh(b):
                    e.wait_ge(S["s_u"], b + 1)
                    e.activation(s_h_, s_h_, ACT.Tanh).then_inc(S["s_h"], 1)

                def s_values(b):
                    e.wait_ge(S["s_qr"], 2 * b + 2)
                    if past(b): e.wait_ge(S["s_pv"], 4 * b)
                    e.activation(s_vx[:, :, 0:DH], bank[0][:, D + KV * DH:NQ].rearrange("p (h d) -> p h d", d=DH),
                                 ACT.Copy).then_inc(S["s_v"], 1)

                def s_heads(b):
                    e.wait_ge(S["s_qtr"], b + 1)
                    if past(4 * b): e.wait_ge(S["s_sc"], 4 * b)
                    e.activation(s_kT_, bank[0][:, D:D + P], ACT.Copy).then_inc(S["s_kT"], 1)
                    for odd, mask in enumerate((m_even, m_odd)):
                        e.activation(s_qT_[:, odd], blocks(0, 2), ACT.Copy, scale=mask).then_inc(S["s_qT"], 1)

                def d_heads(b):
                    e.wait_ge(S["d_qk"], b + 1)
                    if past(b): e.wait_ge(S["d_sc"], b)
                    for c in range(4):
                        bias = (dbq if c < 2 else dbk)[:, c % 2:c % 2 + 1]
                        last = e.activation(d_qkT[:, c, :], bank[5][:, c * P:c * P + P], ACT.Identity, bias=bias)
                    last.then_inc(S["d_qk_sb"], 1)

                def d_exp(b):
                    e.wait_ge(S["d_nmax"], b + 1)
                    if past(b): e.wait_ge(S["d_ptr"], b)
                    if past(b): e.wait_ge(S["d_rinv"], b)
                    e.activation(d_P_, bank[6][:, 0:P], ACT.Exp, scale=1.0 / float(np.sqrt(D)), bias=d_nm,
                                 accum_out=d_sum).then_inc(S["d_exp"], 1)

                def step(i):
                    b = i
                    if live(b):
                        s_tanh(b)
                    b = i - 2
                    if live(b):
                        att1["take"](e, b, 3)
                    b = i - 3
                    if live(b):
                        copy("d_tr", b + 1, d_T[:, 0], blocks(5, 4), "d_hi", ("d_vmm", b))
                    b = i - 4
                    if live(b):
                        copy("d_ptr", b + 1, d_PT, bank[6][:, 0:P], "d_pt", ("d_pv", b))
                    b = i - 1
                    if live(b):
                        s_values(b)
                        s_heads(b)
                    b = i - 3
                    if live(b):
                        copy("d_vmm", b + 1, d_v_, bank[6][:, 0:D], "d_v", ("d_pv", b))
                        d_heads(b)
                    b = i - 2
                    if live(b):
                        copy("s_otr", b + 1, s_oT[:, 0], blocks(1, 2), "s_ohi", ("s_proj", b))
                    b = i - 1
                    if live(b):
                        att1["exponents"](e, b, 0)
                        att1["take"](e, b, 0)
                        att1["exponents"](e, b, 1)
                    b = i
                    if live(b):
                        copy("s_tr", b + 1, s_T[:, 0], blocks(0, 2), "s_hi", ("s_qkv", b))
                    b = i - 1
                    if live(b):
                        att1["take"](e, b, 1)
                    b = i - 4
                    if live(b):
                        copy("g_tr", b + 1, g_T, bank[7][:, 0:D], "g_xnT", ("g_sum", b))
                    b = i - 1
                    if live(b):
                        att1["exponents"](e, b, 2)
                        att1["take"](e, b, 2)
                    b = i - 3
                    if live(b):
                        d_exp(b)
                    b = i - 1
                    if live(b):
                        att1["exponents"](e, b, 3)

                pipeline(e, 4, step)

            @block.vector
            def _(e):
                def lo(pre, b, dst, src, high):
                    e.wait_ge(S[pre + "hi"], b + 1)
                    e.tensor_tensor(dst, src, high.bitcast(F32), ALU.subtract).then_inc(S[pre + "lo"], 1)

                def blocks(bk, n):
                    return bank[bk][:, 0:n * P].rearrange("p (k t) -> p k t", k=n)

                def stats(pre, b, src, cols, ready, factor=1.0, add=EPS):
                    row_statistics(e, pre, b, src, cols, ready, factor, add)

                def s_head(b):
                    e.wait_ge(S["s_xo"], 16 * (b + 1))
                    if past(b): e.wait_ge(S["s_x3"], b)
                    e.tensor_tensor(s_h_, s_xo_, v_row, ALU.add).then_inc(S["s_u"], 1)

                def s_join(b):
                    e.wait_ge(S["s_h"], b + 1)
                    e.tensor_tensor(x_res[:, ds(b * D, D)], s_h_, x_res[:, ds(b * D, D)], ALU.add).then_inc(S["s_x3"], 1)
                    stats("s", b, x_res[:, ds(b * D, D)], s_cols, ("s_x3", b + 1), 1.0 + EPS32, EPS * EPS32)

                def normed(pre, b, dst, src, cols, *free):
                    e.wait_ge(S[pre + "_rs"], 12 * b + 12)
                    if past(free[1]): e.wait_ge(S[free[0]], free[1])
                    e.tensor_scalar(dst, src, cols[1][:, 0:1], cols[5], ALU.subtract, ALU.mult)\
                        .then_inc(S[pre + "_xn"], 1)

                def s_rotary(b):
                    e.wait_ge(S["s_qkv"], b + 1)
                    if past(b): e.wait_ge(S["s_qtr"], b)
                    rf = const[:, C_RF:C_RF + DH]
                    e.tensor_tensor(s_qr_[:, 0:D].rearrange("p (h d) -> p h d", d=DH),
                                    bank[0][:, 0:D].rearrange("p (h d) -> p h d", d=DH),
                                    rf.unsqueeze(1).to_broadcast([P, HEADS, DH]), ALU.mult).then_inc(S["s_qr"], 1)
                    for r in range(2):
                        n = D + r * KV * DH
                        last = e.tensor_tensor(s_qr_[:, n:n + KV * DH].rearrange("p (h d) -> p h d", d=DH),
                                               bank[0][:, D:D + KV * DH].rearrange("p (h d) -> p h d", d=DH),
                                               rf.unsqueeze(1).to_broadcast([P, KV, DH]), ALU.mult)
                    last.then_inc(S["s_qr"], 1)

                def s_sum(b):
                    e.wait_ge(S["s_o"], b + 1)
                    e.wait_ge(S["s_xn"], b + 1)
                    e.tensor_tensor(x_res[:, ds(b * D, D)], x_res[:, ds(b * D, D)], s_o_, ALU.add).then_inc(S["s_x3s"], 1)

                def s_residual(b):
                    e.wait_ge(S["s_proj"], b + 1)
                    e.wait_ge(S["s_x3s"], b + 1)
                    e.tensor_tensor(x_res[:, ds(b * D, D)], bank[1][:, 0:D], x_res[:, ds(b * D, D)], ALU.add).then_inc(S["s_x4"], 1)
                    stats("d", b, x_res[:, ds(b * D, D)], d_cols, ("s_x4", b + 1))

                def d_maximum(b):
                    e.wait_ge(S["d_sc"], b + 1)
                    if past(b): e.wait_ge(S["d_nmax"], b)
                    e.tensor_reduce(d_mx, bank[6][:, 0:P], AX.X, ALU.max).then_inc(S["d_max"], 1)
                    e.wait_ge(S["d_max"], b + 1)
                    if past(b): e.wait_ge(S["d_exp"], b)
                    e.tensor_scalar(d_nm, d_mx, -1.0 / float(np.sqrt(D)), None, ALU.mult).then_inc(S["d_nmax"], 1)

                def d_residual(b):
                    e.wait_ge(S["d_exp"], b + 1)
                    if past(b): e.wait_ge(S["d_x5"], b)
                    e.reciprocal(d_ri, d_sum).then_inc(S["d_rinv"], 1)
                    e.wait_ge(S["d_pv"], b + 1)
                    e.wait_ge(S["d_x4b"], b + 1)
                    e.wait_ge(S["d_rinv"], b + 1)
                    e.scalar_tensor_tensor(out=x_res[:, ds(b * D, D)], in0=bank[6][:, 0:D], scalar=d_ri,
                                           in1=x_res[:, ds(b * D, D)], op0=ALU.mult, op1=ALU.add).then_inc(S["d_x5"], 1)
                    stats("g", b, x_res[:, ds(b * D, D)], g_cols, ("d_x5", b + 1))

                def g_norm(b):
                    e.wait_ge(S["g_rs"], 12 * b + 12)
                    e.tensor_scalar(tab[:, ds(b * TAB + 3 * NH, 1)], g_cols[1][:, 0:1], 1.0, None, ALU.mult)
                    e.tensor_scalar(tab[:, ds(b * TAB + 3 * NH + 1, 1)], g_cols[5], 1.0, None, ALU.mult)
                    normed("g", b, g_xn_, x_res[:, ds(b * D, D)], g_cols, "g_tr", b)

                def g_logits(b):
                    e.wait_ge(S["g_sum"], b + 1)
                    e.tensor_tensor(tab[:, ds(b * TAB, E)], bank[7][:, D:D + E], lbb, ALU.add).then_inc(S["g_lg"], 1)

                e.memset(s_vx[:, :, DH:VX], 1.0)

                def step(i):
                    b = i
                    if live(b):
                        s_head(b)
                    b = i - 1
                    if live(b):
                        s_rotary(b)
                    b = i
                    if live(b):
                        s_join(b)
                    b = i - 3
                    if live(b):
                        lo("d_", b, d_T[:, 1], blocks(5, 4), d_T[:, 0])
                    b = i - 4
                    if live(b):
                        d_residual(b)
                    b = i - 2
                    if live(b):
                        att1["normalise"](e, b, s_o_, s_ri, ["s_otr", "s_x3s"], [b, b])
                        s_sum(b)
                    b = i
                    if live(b):
                        normed("s", b, s_xn_, x_res[:, ds(b * D, D)], s_cols, "s_tr", b)
                    b = i - 4
                    if live(b):
                        g_norm(b)
                    b = i - 1
                    if live(b):
                        att1["softmax"](e, b, 0)
                    b = i - 2
                    if live(b):
                        lo("s_o", b, s_oT[:, 1], blocks(1, 2), s_oT[:, 0])
                    b = i - 1
                    if live(b):
                        att1["softmax"](e, b, 1)
                    b = i - 2
                    if live(b):
                        s_residual(b)
                    b = i - 3
                    if live(b):
                        d_maximum(b)
                    b = i - 1
                    if live(b):
                        att1["softmax"](e, b, 2)
                    b = i
                    if live(b):
                        lo("s_", b, s_T[:, 1], blocks(0, 2), s_T[:, 0])
                    b = i - 1
                    if live(b):
                        att1["softmax"](e, b, 3)
                    b = i - 2
                    if live(b):
                        normed("d", b, d_xn_, x_res[:, ds(b * D, D)], d_cols, "d_tr", b)
                    b = i - 4
                    if live(b):
                        g_logits(b)

                pipeline(e, 4, step)

            @block.gpsimd
            def _(e):
                def newton(pre, b, cols):
                    e.wait_ge(S[pre + "_seed"], 3 * b + 3)
                    rsqrt_newton(e, cols[3], cols[4], cols[5], pre + "_rs", 12 * b)

                def add_bias(b):
                    e.wait_ge(S["d_xn"], b + 1)
                    e.tensor_tensor(x_res[:, ds(b * D, D)], x_res[:, ds(b * D, D)], dbv_row, ALU.add).then_inc(S["d_x4b"], 1)

                def step(i):
                    b = i
                    if live(b):
                        newton("s", b, s_cols)
                    b = i - 4
                    if live(b):
                        newton("g", b, g_cols)
                    b = i - 3
                    if live(b):
                        add_bias(b)
                    b = i - 2
                    if live(b):
                        newton("d", b, d_cols)

                pipeline(e, 4, step)

        jobs2 = []
        for x_ in range(E):
            jobs2 += [(e_gate[x_], D, to(w_gu, x_ * 2 * P), 1.0, None), (e_up[x_], D, to(w_gu, (2 * x_ + 1) * P), 1.0, None)]
            for r in range(2):
                jobs2.append((e_down[x_, r * P:(r + 1) * P, :], P, to(w_dn[:, :, x_:x_ + 1, :], r * P), 1.0, None))
        for r in range(2):
            jobs2 += [(sh_gate[r * P:(r + 1) * P, :], D, to(w_gu, (16 + 2 * r) * P), 1.0, None),
                      (sh_up[r * P:(r + 1) * P, :], D, to(w_gu, (17 + 2 * r) * P), 1.0, None),
                      (sh_down[r * P:(r + 1) * P, :], D, to(w_dn[:, :, E:E + 2, :], r * P), 1.0, None)]
        w2 = weights("w2", 4, work[:, 4096:6144], jobs2)
        t_s, t_first, t_second, t_tmp = (work[:, 512 * k:512 * k + NT].rearrange("p (b e) -> p b e", e=E) for k in range(4))
        t_max, t_max2, t_key, t_rcp = (work[:, 2048 + NB * k:2048 + NB * k + NB] for k in range(4))
        t_part, t_mean = work[:, 2304:2304 + 2 * E], work[:, 2336:2336 + 2 * E]
        logits = tab3[:, :, 0:E]
        coef = tab3[:, :, E:2 * E]

        with phase("route") as block:
            @block.sync
            def _(e):
                w2[0](e)

            @block.tensor
            def _(e):
                w2[1](e)
                e.wait_ge(S["t_part"], 1)
                e.matmul(bank[4][:, 0:2 * E], const[:, C_ONE:C_ONE + P], t_part, start=True, stop=True)\
                    .then_inc(S["t_tot"], 1)

            @block.scalar
            def _(e):
                e.activation(t_s, logits, ACT.Exp, scale=-1.0).then_inc(S["t_sig"], 1)
                w2[2](e)

            @block.vector
            def _(e):
                n = 0

                def link(i):
                    nonlocal n
                    n += 1
                    i.then_inc(S["t_chain"], 1)
                    e.wait_ge(S["t_chain"], n)

                def wide(a):
                    return a.unsqueeze(2).to_broadcast([P, NB, E])

                def first_of_max(s_, max_, first_):
                    link(e.tensor_reduce(max_, s_, AX.X, ALU.max))
                    link(e.tensor_tensor(t_tmp, s_, wide(max_), ALU.is_equal))
                    link(e.tensor_tensor(t_tmp, t_tmp, const[:, C_IOTA:C_IOTA + E].unsqueeze(1).to_broadcast([P, NB, E]),
                                         ALU.mult))
                    link(e.tensor_reduce(t_key, t_tmp, AX.X, ALU.max))
                    link(e.tensor_tensor(first_, t_tmp, wide(t_key), ALU.is_equal))

                e.wait_ge(S["t_sig"], 1)
                link(e.tensor_scalar(t_s, t_s, 1.0, None, ALU.add))
                link(e.reciprocal(t_s, t_s))
                first_of_max(t_s, t_max, t_first)
                link(e.scalar_tensor_tensor(out=t_second, in0=t_first, scalar=-4.0, in1=t_s, op0=ALU.mult, op1=ALU.add))
                first_of_max(t_second, t_max2, t_second)
                link(e.tensor_tensor(t_rcp, t_max, t_max2, ALU.add))
                link(e.tensor_scalar(t_rcp, t_rcp, 1e-8, None, ALU.add))
                link(e.reciprocal(t_rcp, t_rcp))
                link(e.tensor_tensor(t_first, t_first, t_second, ALU.add))
                link(e.tensor_tensor(t_s, t_s, t_first, ALU.mult))
                link(e.tensor_tensor(t_s, t_s, wide(t_rcp), ALU.mult))
                e.tensor_reduce(t_part[:, 0:E], t_s.rearrange("p b e -> p e b"), AX.X, ALU.add)
                e.tensor_reduce(t_part[:, E:2 * E], t_first.rearrange("p b e -> p e b"), AX.X, ALU.add)\
                    .then_inc(S["t_part"], 1)
                w2[3](e)
                e.wait_ge(S["t_tot"], 1)
                link(e.tensor_scalar(t_mean[:, E:2 * E], bank[4][:, E:2 * E], 1.0, None, ALU.max))
                link(e.reciprocal(t_mean[:, E:2 * E], t_mean[:, E:2 * E]))
                link(e.scalar_tensor_tensor(out=t_mean[:, 0:E], in0=bank[4][:, 0:E], scalar=0.5, in1=t_mean[:, E:2 * E],
                                            op0=ALU.mult, op1=ALU.mult))
                e.tensor_tensor(coef, t_first, t_mean[:, 0:E].unsqueeze(1).to_broadcast([P, NB, E]), ALU.mult)\
                    .then_inc(S["t_coef"], 1)

        NG = 5
        wpos[0] = rpos[0] = 0
        f_xn_ = [wk(D), wk(D)]
        f_T = [wr(2 * D).rearrange("p (s k t) -> p s k t", s=2, k=2) for _ in range(2)]
        f_t = [wk(2 * P).rearrange("p (x i) -> p x i", x=2) for _ in range(2)]
        f_h_ = [wk(2 * P).rearrange("p (x i) -> p x i", x=2) for _ in range(2)]
        f_hT = [wr(2 * D).rearrange("p (s k t) -> p s k t", s=2, k=2) for _ in range(2)]
        f_coef = [tiny[:, 0:E], tiny[:, E:2 * E]]
        f_stage = [wk(D), wk(D)]

        def pairs(e, steps, tail):
            steps(0)
            steps(1)
            with e.Fori(2, NB // 2 - 1) as h:
                steps(h)
            steps(NB // 2 - 1)
            tail(NB // 2)

        def before(h):
            return not isinstance(h, int) or h > 0

        def after(h):
            return not isinstance(h, int) or h < NB // 2 - 1

        with phase("experts") as block:
            @block.sync
            def _(e):
                def steps(h):
                    for k in range(2):
                        b = 2 * h + k
                        e.wait_ge(S["f_x6"], b + 1)
                        e.dma_start(tile(out, b), f_stage[k]).then_inc(S[f"f_out{k}"], 16)

                pairs(e, steps, lambda h: None)
                for k in range(2):
                    e.wait_ge(S[f"f_out{k}"], 16 * (NB // 2))

            @block.tensor
            def _(e):
                def transpose(b, k):
                    e.wait_ge(S["f_xn"], b + 1)
                    if past(b): e.wait_ge(S["f_lo"], b)
                    for c in range(2):
                        last = e.transpose(bank[6][:, c * P:c * P + P], f_xn_[k][:, c * P:c * P + P], ident)
                    last.then_inc(S["f_tr"], 1)

                def up(n, b, g, q, k):
                    e.wait_ge(S["f_lo"], b + 1)
                    if past(n - 1): e.wait_ge(S["f_h"], n - 1)
                    project(e, bank[q][:, :], f_T[k], w_gu, 2, 4 * P * g, 4 * P * (g + 1)).then_inc(S["f_gu"], 1)

                def turn(n, q):
                    e.wait_ge(S["f_h"], n + 1)
                    if past(n - 1): e.wait_ge(S["f_hlo"], n - 1)
                    for j in range(2):
                        last = e.transpose(bank[2 + q][:, j * P:j * P + P], f_h_[q][:, j, :], ident)
                    last.then_inc(S["f_htr"], 1)

                def down(n, b, g, q, k):
                    e.wait_ge(S["f_hlo"], n + 1)
                    if g == 0:
                        if past(b - 1): e.wait_ge(S["f_x6"], b - 1)
                    for j in range(2):
                        last = mm3(e, bank[4 + k][:, 0:D], (f_hT[q][:, 0, j, :], f_hT[q][:, 1, j, :]),
                                   (w_dn[:, 0, 2 * g + j, :], w_dn[:, 1, 2 * g + j, :]),
                                   g == 0 and j == 0, g == NG - 1 and j == 1)
                    last.then_inc(S["f_acc"], 1)

                def later(h, m):
                    if m < 0:
                        h, m = h - 1, m + 2 * NG
                    return 2 * NG * h + m, 2 * h + m // NG, m % NG, m % 2, m // NG

                def steps(h):
                    for m in range(2 * NG):
                        n, b, g, q, k = later(h, m)
                        up(n, b, g, q, k)
                        if m >= 1 or before(h):
                            n, b, g, q, k = later(h, m - 1)
                            turn(n, q)
                        if m >= 2 or before(h):
                            down(*later(h, m - 2))
                        if m == 2:
                            transpose(2 * h + 1, 1)
                        if m == 7 and after(h):
                            transpose(2 * h + 2, 0)

                def tail(h):
                    n, b, g, q, k = later(h, -1)
                    turn(n, q)
                    down(*later(h, -2))
                    down(*later(h, -1))

                transpose(0, 0)
                pairs(e, steps, tail)

            @block.scalar
            def _(e):
                def high(b, k):
                    e.wait_ge(S["f_tr"], b + 1)
                    if past(NG * (b - 1)): e.wait_ge(S["f_gu"], NG * (b - 1))
                    e.activation(f_T[k][:, 0], bank[6][:, 0:D].rearrange("p (k t) -> p k t", k=2), ACT.Copy)\
                        .then_inc(S["f_hi"], 1)

                def gate(n, q):
                    e.wait_ge(S["f_gu"], n + 1)
                    if past(n - 1): e.wait_ge(S["f_h"], n - 1)
                    e.activation(f_t[q], bank[q][:, :].rearrange("p (x o i) -> p x o i", x=2, o=2)[:, :, 0, :],
                                 ACT.Tanh, scale=0.5).then_inc(S["f_tanh"], 1)

                def hidden(n, q):
                    e.wait_ge(S["f_htr"], n + 1)
                    if past(n - 1): e.wait_ge(S["f_acc"], n - 1)
                    e.activation(f_hT[q][:, 0], bank[2 + q][:, 0:2 * P].rearrange("p (k t) -> p k t", k=2), ACT.Copy)\
                        .then_inc(S["f_hhi"], 1)

                def steps(h):
                    for m in range(2 * NG):
                        n = 2 * NG * h + m
                        gate(n, m % 2)
                        if m >= 1 or before(h):
                            hidden(n - 1, (m - 1) % 2)
                        if m == 2:
                            high(2 * h + 1, 1)
                        if m == 7 and after(h):
                            high(2 * h + 2, 0)

                high(0, 0)
                pairs(e, steps, lambda h: hidden(2 * NG * h - 1, 1))

            @block.vector
            def _(e):
                def norm(b, k):
                    if past(b - 1): e.wait_ge(S["f_tr"], b - 1)
                    if past(NG * (b - 1)): e.wait_ge(S["f_h"], NG * (b - 1))
                    e.tensor_scalar(f_coef[k], tab[:, ds(b * TAB + E, E)], 1.0, None, ALU.mult)
                    e.tensor_scalar(f_xn_[k], x_res[:, ds(b * D, D)], tab[:, ds(b * TAB + 3 * NH, 1)],
                                    tab[:, ds(b * TAB + 3 * NH + 1, 1)], ALU.subtract, ALU.mult)\
                        .then_inc(S["f_xn"], 1)

                def low(b, k):
                    e.wait_ge(S["f_hi"], b + 1)
                    e.tensor_tensor(f_T[k][:, 1], bank[6][:, 0:D].rearrange("p (k t) -> p k t", k=2),
                                    f_T[k][:, 0].bitcast(F32), ALU.subtract).then_inc(S["f_lo"], 1)

                def gated(n, g, q, k):
                    v = bank[q][:, :].rearrange("p (x o i) -> p x o i", x=2, o=2)
                    e.wait_ge(S["f_tanh"], n + 1)
                    e.scalar_tensor_tensor(out=f_t[q], in0=f_t[q], scalar=1.0, in1=v[:, :, 0, :],
                                           op0=ALU.add, op1=ALU.mult).then_inc(S["f_tg"], 1)
                    e.wait_ge(S["f_tg"], n + 1)
                    if past(n - 1): e.wait_ge(S["f_htr"], n - 1)
                    for j in range(2):
                        w = f_coef[k][:, 2 * g + j:2 * g + j + 1] if g < NG - 1 else 0.5
                        last = e.scalar_tensor_tensor(out=f_h_[q][:, j, :], in0=f_t[q][:, j, :], scalar=w,
                                                      in1=v[:, j, 1, :], op0=ALU.mult, op1=ALU.mult)
                    last.then_inc(S["f_h"], 1)

                def hidden(n, q):
                    e.wait_ge(S["f_hhi"], n + 1)
                    e.tensor_tensor(f_hT[q][:, 1], bank[2 + q][:, 0:2 * P].rearrange("p (k t) -> p k t", k=2),
                                    f_hT[q][:, 0].bitcast(F32), ALU.subtract).then_inc(S["f_hlo"], 1)

                def finish(b, k, h_):
                    e.wait_ge(S["f_acc"], NG * (b + 1))
                    if past(16 * h_): e.wait_ge(S[f"f_out{k}"], 16 * h_)
                    e.tensor_tensor(f_stage[k], bank[4 + k][:, 0:D], x_res[:, ds(b * D, D)], ALU.add)\
                        .then_inc(S["f_x6"], 1)

                def steps(h):
                    for m in range(2 * NG):
                        n = 2 * NG * h + m
                        gated(n, m % NG, m % 2, m // NG)
                        if m >= 1 or before(h):
                            hidden(n - 1, (m - 1) % 2)
                        if m == 1:
                            norm(2 * h + 1, 1)
                        if m == 2:
                            low(2 * h + 1, 1)
                            if before(h):
                                finish(2 * h - 1, 1, h - 1)
                        if m == 6 and after(h):
                            norm(2 * h + 2, 0)
                        if m == 7:
                            if after(h):
                                low(2 * h + 2, 0)
                            finish(2 * h, 0, h)

                def tail(h):
                    hidden(2 * NG * h - 1, 1)
                    finish(2 * h - 1, 1, h - 1)

                norm(0, 0)
                low(0, 0)
                pairs(e, steps, tail)


_INS = ["x", "ctx_1024",
        "L0_attn_in_proj_w", "L0_attn_conv_w", "L0_attn_conv_b", "L0_attn_norm_w", "L0_attn_out_proj_w",
        "L0_attn_dt_bias", "L0_attn_A_log", "L0_attn_D_param",
        "L0_xattn_Wq", "L0_xattn_bq", "L0_xattn_Wk", "L0_xattn_bk", "L0_xattn_Wv", "L0_xattn_bv",
        "L0_xattn_Wo", "L0_xattn_bo",
        "L0_ffn_wf", "L0_ffn_uf", "L0_ffn_bf", "L0_ffn_wi", "L0_ffn_ui", "L0_ffn_bi",
        "L0_ffn_wc", "L0_ffn_uc", "L0_ffn_bc", "L0_ffn_wo", "L0_ffn_uo", "L0_ffn_bo", "L0_ffn_in_c",
        "L1_attn_w_q", "L1_attn_w_k", "L1_attn_w_v", "L1_attn_w_o", "L1_attn_g",
        "L1_xattn_Wq", "L1_xattn_bq", "L1_xattn_Wk", "L1_xattn_bk", "L1_xattn_Wv", "L1_xattn_bv",
        "L1_ffn_gate_w", "L1_ffn_lb_bias", "L1_ffn_expert_gate_w", "L1_ffn_expert_up_w",
        "L1_ffn_expert_down_w", "L1_ffn_shared_gate_w", "L1_ffn_shared_up_w", "L1_ffn_shared_down_w"]


def kernel(**inputs):
    import numpy as _np
    import concourse.bacc as _bacc
    from concourse.bass_utils import run_bass_kernel_spmd as _run

    nc = _bacc.Bacc("TRN2", target_bir_lowering=False, num_devices=1)
    arrays, args = {}, []
    for name in _INS:
        a = _np.ascontiguousarray(inputs[name])
        arrays[f"in_{name}"] = a
        args.append(nc.dram_tensor(f"in_{name}", a.shape, mybir.dt.from_np(a.dtype), kind="ExternalInput").ap())
    shape = arrays["in_x"].shape
    out = nc.dram_tensor("out_dram", shape, F32, kind="ExternalOutput").ap()
    xo = nc.dram_tensor("recurrence_out", shape, F32, kind="Internal").ap()
    table = nc.inline_tensor(constant_table(), name="constant_table").ap()
    decoder(nc, args, xo, table, out)
    r = _run(nc, [arrays], core_ids=[0])
    return r.results[0]["out_dram"]
```

```python
from contextlib import ExitStack, contextmanager

import numpy as np

import concourse.bass as bass
from concourse import mybir

P = 128
D = 256
DI = 512
NH = 8
HD = 64
CONV = 4
XBC = DI + 2 * P
HEADS = 16
DH = 16
KV = 4
E = 8
HID = 128
EPS = 1e-5
EPS32 = float(np.finfo(np.float32).eps)

F32 = mybir.dt.float32
F32R = mybir.dt.float32r
I32 = mybir.dt.int32
ALU = mybir.AluOpType
ACT = mybir.ActivationFunctionType
AX = mybir.AxisListType
ds = bass.ds

C_ID, C_UP, C_COS, C_SIN, C_RF, C_EVEN, C_ODD, C_IOTA, C_ONE, C_3_2, C_END = (
    0, 128, 256, 272, 288, 304, 305, 306, 314, 442, 443)


def constant_table():
    t = np.zeros((P, C_END), np.float32)
    t[:, C_ID:C_ID + P] = np.eye(P)
    t[:, C_UP:C_UP + P] = np.triu(np.ones((P, P)))
    pos = np.arange(P, dtype=np.float32)
    inv = (1.0 / np.power(np.float32(10000.0), np.arange(0, DH, 2, dtype=np.float32) / np.float32(DH))).astype(np.float32)
    ang = pos[:, None] * np.concatenate([inv, inv])[None, :]
    t[:, C_COS:C_COS + DH] = np.cos(ang)
    t[:, C_SIN:C_SIN + DH] = np.sin(ang) * np.where(np.arange(DH) < DH // 2, -1.0, 1.0)
    theta = np.power(np.float32(10000.0), (-2.0 * (np.arange(DH) // 2) / DH).astype(np.float32))
    ang = pos[:, None] * theta[None, :]
    t[:, C_RF:C_RF + DH] = np.cos(ang) + np.where(np.arange(P) % 2 == 1, -1.0, 1.0)[:, None] * np.sin(ang)
    t[:, C_EVEN] = (np.arange(P) // DH) % 2 == 0
    t[:, C_ODD] = (np.arange(P) // DH) % 2 == 1
    t[:, C_IOTA:C_IOTA + E] = E - np.arange(E)
    t[:, C_ONE:C_ONE + P] = 1.0
    t[:, C_3_2] = 1.5
    return t


SIGNALS = {
    "consts": """
        small_loaded halved bias_rows_ready bo2_mm start_state bv_hi bv_lo
        w0_load0 w0_load1 w0_load2 w0_load3 w0_load4 w0_load5 w0_load6 w0_load7 w0_scaled w0_tr w0_hi w0_lo consts_ready
    """.split(),
    "steps": """
        p_stats p_chain p_xn p_tr p_xnT p_dt p_min p_act p_nd p_cum p_cumT p_kept p_stored
    """.split(),
    "layer0": """
        m_shift m_guess m_n1 m_n2 m_n3 m_n4 m_n5 m_n6 m_n7 m_n8 m_n9 m_n10 m_n11
        c_shift c_guess c_n1 c_n2 c_n3 c_n4 c_n5 c_n6 c_n7 c_n8 c_n9 c_n10 c_n11
        r_shift r_guess r_n1 r_n2 r_n3 r_n4 r_n5 r_n6 r_n7 r_n8 r_n9 r_n10 r_n11
        m_cur m_xn m_tr m_xnT m_xbc m_raw m_tap m_conv2 m_conv m_z m_ztanh m_zg m_xtanh m_xbcs
        m_xtr m_g m_xt m_xdt m_xd m_gm m_cum m_rel m_exp m_M m_y m_yx m_y2 m_ss m_seed m_rs
        m_ytr m_yhi m_ylo m_out m_x1 c_stats c_aggr c_seed c_rs c_xn c_ctx c_x1b c_tr c_hi c_lo c_q
        c_kv c_kb c_qb c_v c_rot c_cos c_qr c_qtr c_kT c_qT c_sc c_max c_sub c_exp c_ptr c_pt c_pv
        c_rinv c_o c_otr c_ohi c_olo c_proj c_x2 r_stats r_aggr r_seed r_rs r_xn r_tr r_xnT r_fi
        r_tfi r_go r_tg r_xo r_store r_a r_b r_d
    """.split(),
    "between": """
        w1_load0 w1_load1 w1_load2 w1_load3 w1_load4 w1_load5 w1_load6 w1_load7 w1_scaled w1_tr w1_hi w1_lo b_v b_vrow b_gate l1_small
        l1_wg l1_whi l1_wlo
    """.split(),
    "layer1": """
        s_shift s_guess s_n1 s_n2 s_n3 s_n4 s_n5 s_n6 s_n7 s_n8 s_n9 s_n10 s_n11
        d_shift d_guess d_n1 d_n2 d_n3 d_n4 d_n5 d_n6 d_n7 d_n8 d_n9 d_n10 d_n11
        g_shift g_guess g_n1 g_n2 g_n3 g_n4 g_n5 g_n6 g_n7 g_n8 g_n9 g_n10 g_n11
        s_xo s_u s_h s_x3 s_stats s_aggr s_seed s_rs s_xn s_tr s_hi s_lo s_qkv s_qr s_v s_qtr s_kT
        s_qT s_sc s_max s_sub s_exp s_ptr s_pt s_pv s_rinv s_o s_x3s s_otr s_ohi s_olo s_proj s_x4
        d_stats d_aggr d_seed d_rs d_xn d_ctx d_x4b d_tr d_xcT d_qk d_vmm d_qk_sb d_v d_sc d_max
        d_nmax d_exp d_ptr d_pt d_pv d_rinv d_x5 g_stats g_aggr g_seed g_rs g_xn g_tr g_xnT g_lg
        g_sum
    """.split(),
    "route": """
        w2_load0 w2_load1 w2_load2 w2_load3 w2_load4 w2_load5 w2_load6 w2_load7 w2_scaled w2_tr w2_hi w2_lo t_chain t_sig t_part t_tot
        t_coef
    """.split(),
    "experts": """
        f_xn f_tr f_hi f_lo f_gu f_tanh f_tg f_h f_htr f_hhi f_hlo f_acc f_x6 f_out0 f_out1
    """.split(),
}


def decoder(nc, args, xo_dram, cum_dram, table, out):
    (x, ctx, in_proj, conv_w, conv_b, norm_w, out_proj, dt_bias, A_log, D_param,
     c_Wq, c_bq, c_Wk, c_bk, c_Wv, c_bv, c_Wo, c_bo,
     wf, uf, bf, wi, ui, bi, wc, uc, bc, wo, uo, bo, in_c,
     s_wq, s_wk, s_wv, s_wo, s_g, d_Wq, d_bq, d_Wk, d_bk, d_Wv, d_bv,
     gate_w, lb_bias, e_gate, e_up, e_down, sh_gate, sh_up, sh_down) = args
    NB = x.shape[0]
    NT = NB * E

    with ExitStack() as stack:
        def sb(name, shape, dt=F32):
            return stack.enter_context(nc.sbuf_tensor(name, shape, dt))

        S = {name: stack.enter_context(nc.semaphore(name))
             for name in ["const_loaded"] + [f"x_loaded{c}" for c in range(8)]}

        @contextmanager
        def phase(name):
            own = {n: nc.alloc_semaphore(name=n) for n in SIGNALS[name]}
            S.update(own)
            with nc.Block() as block_:
                yield block_
            nc.clear_and_free_semaphores(list(own.values()))
            nc.all_engine_barrier()

        bank = [stack.enter_context(nc.psum_tensor(f"bank{k}", [P, 512], F32)) for k in range(8)]

        def past(count):
            return not isinstance(count, int) or count > 0

        def live(b):
            return not isinstance(b, int) or 0 <= b < NB

        def tile(dram, b):
            return dram[b] if isinstance(b, int) else dram[ds(b, 1)].rearrange("o t d -> t (o d)")

        def pipeline(eng, lag, step):
            for i in range(lag + 1):
                step(i)
            with eng.Fori(lag + 1, NB) as i:
                step(i)
            for i in range(NB, NB + lag):
                step(i)

        def mm3(pe, out_, lhs, rhs, first=True, last=True):
            pe.matmul(out_, lhs[0], rhs[0], start=first, stop=False)
            pe.matmul(out_, lhs[0], rhs[1], start=False, stop=False)
            return pe.matmul(out_, lhs[1], rhs[0], start=False, stop=last)

        def project(pe, out_, act, w, blocks, n0, n1):
            for k in range(blocks):
                last = mm3(pe, out_, (act[:, 0, k, :], act[:, 1, k, :]),
                           (w[:, 0, k, n0:n1], w[:, 1, k, n0:n1]), k == 0, k == blocks - 1)
            return last

        def project32(pe, out_, act, w, blocks, n0, n1):
            for k in range(blocks):
                last = pe.matmul(out_, act[:, k, :], w[:, k, n0:n1], start=k == 0, stop=k == blocks - 1)
            return last

        def project32_T(pe, out_, act, w, n0, first=True, last_=True):
            for k in range(2):
                last = pe.matmul(out_, w[:, k, n0:n0 + P], act[:, k, :], start=first and k == 0,
                                 stop=last_ and k == 1)
            return last

        const = sb("const", [P, C_END])
        ident = const[:, C_ID:C_ID + P]
        upper = const[:, C_UP:C_UP + P]
        m_even, m_odd = const[:, C_EVEN:C_EVEN + 1], const[:, C_ODD:C_ODD + 1]
        x_res = sb("x_res", [P, NB * D])
        TAB = 3 * NH + 2
        tab = sb("tab", [P, NB * TAB])
        tab3 = tab[:, :].rearrange("p (b n) -> p b n", n=TAB)
        w_dt = sb("w_dt", [P, 2, NH])
        small = sb("small", [P, 96])
        rows = sb("rows", [P, 4 * D])
        WORK, WORKR = 9624, 2560
        work = sb("work", [P, WORK])
        workr = sb("workr", [P, WORKR], F32R)
        tiny = sb("tiny", [P, 96])

        def parts_view(region, base, k, n):
            return region[:, base:base + 2 * k * n].rearrange("p (s k n) -> p s k n", s=2, k=k)

        def plain_view(region, base, k, n):
            return region[:, base:base + k * n].rearrange("p (k n) -> p k n", k=k)

        d_state = sb("d_state", [P, 2, P])
        r_tfi_ = sb("r_tfi_", [P, 4, P])
        r_tg_ = sb("r_tg_", [P, 2, P])
        r_xo_ = sb("r_xo_", [P, D])
        w_gate = sb("w_gate", [P, 2, E])
        bvr = sb("bvr", [P, 2, 2], F32R)

        col = {}
        at = [0]

        def small_cols(name, n):
            col[name] = small[:, at[0]:at[0] + n]
            at[0] += n
            return col[name]

        cw = small_cols("cw", 6 * CONV).rearrange("p (j k) -> p j k", k=CONV)
        cb = small_cols("cb", 6)
        expA = small_cols("expA", NH)
        dtb = small_cols("dtb", NH)
        dpar = small_cols("dpar", NH)
        gb = small_cols("gb", 6)
        inc = small_cols("inc", 2)
        bvc = small_cols("bvc", 2)
        gcol = small_cols("gcol", 2)
        dbq = small_cols("dbq", 2)
        dbk = small_cols("dbk", 2)
        lbb = small_cols("lbb", E)
        bqk_row = rows[:, 0:2 * D]
        bo2_row = rows[:, 2 * D:3 * D]
        bo_row = rows[:, 3 * D:4 * D]

        wpos = [0]

        def wk(n):
            a = work[:, wpos[0]:wpos[0] + n]
            wpos[0] += n
            assert wpos[0] <= WORK, wpos
            return a

        rpos = [0]

        def wr(n):
            a = workr[:, rpos[0]:rpos[0] + n]
            rpos[0] += n
            assert rpos[0] <= WORKR, rpos
            return a

        STAGES = 8

        def weights(pre, scratch, jobs):
            stages = [scratch[:, 512 * k:512 * k + 512] for k in range(STAGES)]

            def sync(e):
                for j, (rows_, n, _, _, _) in enumerate(jobs):
                    if past(j - STAGES + 1): e.wait_ge(S[pre + "_tr"], j - STAGES + 1)
                    e.dma_start(stages[j % STAGES][:, 0:n], rows_).then_inc(S[f"{pre}_load{j % STAGES}"], 16)

            def tensor(e):
                scaled = 0
                for j, (_, n, _, _, sc) in enumerate(jobs):
                    e.wait_ge(S[f"{pre}_load{j % STAGES}"], 16 * (j // STAGES + 1))
                    if sc is not None:
                        scaled += 1
                        e.wait_ge(S[pre + "_scaled"], scaled)
                    if past(j - 3): e.wait_ge(S[pre + "_lo"], j - 3)
                    for c in range(n // P):
                        last = e.transpose(bank[j % 4][:, c * P:c * P + P],
                                           stages[j % STAGES][:, c * P:c * P + P], ident)
                    last.then_inc(S[pre + "_tr"], 1)

            def scalar(e):
                for j, (_, n, dst, f, _) in enumerate(jobs):
                    e.wait_ge(S[pre + "_tr"], j + 1)
                    src = bank[j % 4][:, 0:n].rearrange("p (c r) -> p c r", r=P)
                    plain_, place = dst
                    e.activation(place(0), src[:, 0:1] if plain_ else src, ACT.Copy, scale=f)\
                        .then_inc(S[pre + "_hi"], 1)

            def vector(e):
                def scale(j):
                    if j < len(jobs) and jobs[j][4] is not None:
                        e.wait_ge(S[f"{pre}_load{j % STAGES}"], 16 * (j // STAGES + 1))
                        st = stages[j % STAGES][:, 0:jobs[j][1]]
                        e.tensor_tensor(st, st, jobs[j][4], ALU.mult).then_inc(S[pre + "_scaled"], 1)

                for j in range(2):
                    scale(j)
                for j, (_, n, dst, f, _) in enumerate(jobs):
                    e.wait_ge(S[pre + "_hi"], j + 1)
                    src = bank[j % 4][:, 0:n].rearrange("p (c r) -> p c r", r=P)
                    plain_, place = dst
                    if plain_:
                        e.tensor_scalar(place(1), src[:, 1:2], f, None, ALU.mult).then_inc(S[pre + "_lo"], 1)
                    else:
                        e.scalar_tensor_tensor(out=place(1), in0=src, scalar=f, in1=place(0).bitcast(F32),
                                               op0=ALU.mult, op1=ALU.subtract).then_inc(S[pre + "_lo"], 1)
                    scale(j + 2)

            return sync, tensor, scalar, vector

        def to(view, r0):
            return False, lambda part: view[:, part, :, r0:r0 + P]

        def plain(view, r0):
            return True, lambda k: view[:, k:k + 1, r0:r0 + P]

        def settled(e):
            e.wait_ge(S["const_loaded"], 16)

        def rsqrt_seed(e, pre, b, x_, xh_, t_, y_):
            e.wait_ge(S[pre + "_seed"], b + 1)
            e.tensor_scalar(xh_, x_, -0.5, None, ALU.mult)
            e.tensor_scalar(t_.bitcast(I32), x_.bitcast(I32), 1, None, ALU.arith_shift_right)\
                .then_inc(S[pre + "_shift"], 1)
            e.wait_ge(S[pre + "_shift"], b + 1)
            e.tensor_scalar(y_.bitcast(I32), t_.bitcast(I32), -1.0, float(0x5F3759DF), ALU.mult, ALU.add)\
                .then_inc(S[pre + "_guess"], 1)

        def rsqrt_newton(e, pre, b, xh_, t_, y_):
            three_halves = const[:, C_3_2:C_3_2 + 1]
            e.wait_ge(S[pre + "_guess"], b + 1)
            n = 0
            for k in range(3):
                for out_, a_, b_ in ((t_, y_, y_), (t_, t_, xh_), (t_, t_, three_halves), (y_, y_, t_)):
                    if n:
                        e.wait_ge(S[f"{pre}_n{n}"], b + 1)
                    n += 1
                    e.tensor_tensor(out_, a_, b_, ALU.add if b_ is three_halves else ALU.mult)\
                        .then_inc(S[f"{pre}_n{n}" if n < 12 else pre + "_rs"], 1)

        def stat_cols(c):
            return (tiny[:, c:c + 6], tiny[:, c + 6:c + 8], tiny[:, c + 8:c + 9], tiny[:, c + 9:c + 10],
                    tiny[:, c + 10:c + 11], tiny[:, c + 11:c + 12])

        def row_statistics(e, pre, b, src, cols, ready, factor=1.0, add=EPS):
            st, mv, x_, xh_, t_, y_ = cols
            settled(e)
            e.wait_ge(S[ready[0]], ready[1])
            if past(b): e.wait_ge(S[pre + "_xn"], b)
            e.bn_stats(st, src).then_inc(S[pre + "_stats"], 1)
            settled(e)
            e.wait_ge(S[pre + "_stats"], b + 1)
            e.bn_aggr(mv, st).then_inc(S[pre + "_aggr"], 1)
            e.wait_ge(S[pre + "_aggr"], b + 1)
            if past(b): e.wait_ge(S[pre + "_rs"], b)
            e.tensor_scalar(x_, mv[:, 1:2], factor, add, ALU.mult, ALU.add).then_inc(S[pre + "_seed"], 1)
            rsqrt_seed(e, pre, b, x_, xh_, t_, y_)

        layer0_weights = ExitStack()
        w0r = layer0_weights.enter_context(nc.sbuf_tensor("w0r", [P, 6144], F32R))
        w0p = layer0_weights.enter_context(nc.sbuf_tensor("w0p", [P, 6144], F32))
        w_out = parts_view(w0r, 0, 4, D)
        w_cq = parts_view(w0r, 2048, 2, D)
        w_ckv = parts_view(w0r, 3072, 2, 2 * D)
        w_co = parts_view(w0r, 5120, 2, D)
        w_in = plain_view(w0p, 0, 2, DI + XBC)
        w_rx = plain_view(w0p, 2560, 2, 3 * D)
        w_ru = plain_view(w0p, 4096, 2, 3 * D)
        w_rxo = plain_view(w0p, 5632, 2, D)

        nw_row = work[:, 0:DI]
        stage0 = work[:, 2048:6144]
        ff = [(wf, uf), (wi, ui), (wc, uc)]
        jobs0 = [(in_proj[r * P:(r + 1) * P, :], D, plain(w_in, r * P), 1.0, None) for r in range(10)]
        jobs0 += [(out_proj[r * P:(r + 1) * P, :], DI, to(w_out, r * P), 1.0, nw_row) for r in range(2)]
        for r in range(2):
            jobs0 += [(c_Wq[r * P:(r + 1) * P, :], D, to(w_cq, r * P), 1.0, None),
                      (c_Wk[r * P:(r + 1) * P, :], D, to(w_ckv, r * P), 1.0, None),
                      (c_Wv[r * P:(r + 1) * P, :], D, to(w_ckv, D + r * P), 1.0, None),
                      (c_Wo[r * P:(r + 1) * P, :], D, to(w_co, r * P), 1.0, None),
                      (wo[r * P:(r + 1) * P, :], D, plain(w_rxo, r * P), 1.0, None)]
            for g, (wx, wu) in enumerate(ff):
                jobs0 += [(wx[r * P:(r + 1) * P, :], D, plain(w_rx, g * D + r * P), 1.0, None),
                          (wu[r * P:(r + 1) * P, :], D, plain(w_ru, g * D + r * P), 0.5, None)]
        w0 = weights("w0", stage0, jobs0)
        dt_stage = work[0:NH, 512:512 + D]
        bo2_in = work[:, 768:768 + D]
        CHUNK = max(1, NB // 8)

        with phase("consts") as block:
            @block.sync
            def _(e):
                e.dma_start(const[:, :], table).then_inc(S["const_loaded"], 16)
                w0[0](e)

            @block.gpsimd
            def _(e):
                for c in range(NB // CHUNK):
                    e.dma_start(x_res[:, c * CHUNK * D:(c + 1) * CHUNK * D].rearrange("p (b d) -> p b d", d=D),
                                x[c * CHUNK:(c + 1) * CHUNK].rearrange("b t d -> t b d")).then_inc(S[f"x_loaded{c}"], 16)

            @block.tensor
            def _(e):
                e.wait_ge(S["const_loaded"], 16)
                w0[1](e)
                e.wait_ge(S["small_loaded"], 16 * 16)
                for c in range(2):
                    last = e.transpose(bank[4][:, c * NH:c * NH + NH], dt_stage[:, c * P:c * P + P],
                                       ident[0:NH, 0:NH])
                last.then_inc(S["w0_tr"], 1)
                e.wait_ge(S["bv_lo"], 1)
                e.wait_ge(S["w0_lo"], len(jobs0))
                for k in range(2):
                    last = mm3(e, bank[5][:, 0:D], (bvr[:, 0, k:k + 1].to_broadcast([P, P]),
                                                    bvr[:, 1, k:k + 1].to_broadcast([P, P])),
                               (w_co[:, 0, k, :], w_co[:, 1, k, :]), k == 0, k == 1)
                last.then_inc(S["bo2_mm"], 1)

            @block.scalar
            def _(e):
                for dst, src in ((cw, conv_w.rearrange("(j p) o k -> p j (o k)", p=P)),
                                 (cb, conv_b.rearrange("(j p) -> p j", p=P)),
                                 (expA, A_log.partition_broadcast(P)), (dtb, dt_bias.partition_broadcast(P)),
                                 (dpar, D_param.partition_broadcast(P)),
                                 (gb[:, 0:2], bf.rearrange("(j p) -> p j", p=P)),
                                 (gb[:, 2:4], bi.rearrange("(j p) -> p j", p=P)),
                                 (gb[:, 4:6], bc.rearrange("(j p) -> p j", p=P)),
                                 (inc, in_c.rearrange("(j p) -> p j", p=P)),
                                 (bvc, c_bv.rearrange("(j p) -> p j", p=P)),
                                 (bqk_row[:, 0:D], c_bq.partition_broadcast(P)),
                                 (bqk_row[:, D:2 * D], c_bk.partition_broadcast(P)),
                                 (bo2_in, c_bo.partition_broadcast(P)), (bo_row, bo.partition_broadcast(P)),
                                 (nw_row, norm_w.partition_broadcast(P)),
                                 (dt_stage, in_proj[DI + XBC:DI + XBC + NH, :])):
                    with nc.allow_non_contiguous_dma(reason="small vectors, once"):
                        e.dma_start(dst, src).then_inc(S["small_loaded"], 16)
                w0[2](e)
                e.wait_ge(S["w0_tr"], len(jobs0) + 1)
                e.activation(w_dt[:, :, :], bank[4][:, 0:2 * NH].rearrange("p (k n) -> p k n", k=2), ACT.Copy)\
                    .then_inc(S["consts_ready"], 1)
                e.wait_ge(S["small_loaded"], 16 * 16)
                e.activation(expA, expA, ACT.Exp).then_inc(S["consts_ready"], 1)

            @block.vector
            def _(e):
                e.wait_ge(S["const_loaded"], 16)
                e.wait_ge(S["small_loaded"], 16 * 16)
                e.tensor_scalar(small[:, 0:30], small[:, 0:30], 0.5, None, ALU.mult)
                e.tensor_scalar(gb[:, 0:4], gb[:, 0:4], 0.5, None, ALU.mult)
                e.tensor_scalar(inc, inc, 2.0, None, ALU.mult).then_inc(S["halved"], 1)
                e.tensor_scalar(nw_row, nw_row, float(np.sqrt(DI)), None, ALU.mult).then_inc(S["halved"], 1)
                e.tensor_copy(bvr[:, 0, :], bvc).then_inc(S["bv_hi"], 1)
                e.wait_ge(S["bv_hi"], 1)
                e.tensor_tensor(bvr[:, 1, :], bvc, bvr[:, 0, :].bitcast(F32), ALU.subtract).then_inc(S["bv_lo"], 1)
                e.wait_ge(S["halved"], 2)
                e.tensor_copy(d_state[:, :, :], inc.unsqueeze(2).to_broadcast([P, 2, P])).then_inc(S["start_state"], 1)
                w0[3](e)
                e.wait_ge(S["bo2_mm"], 1)
                e.tensor_tensor(bo2_row, bank[5][:, 0:D], bo2_in, ALU.add).then_inc(S["bias_rows_ready"], 1)

        stats0 = work[:, 0:NB * 6].rearrange("p (b n) -> p b n", n=6)
        pn = work[:, 512:512 + 4 * NB].rearrange("p (k b) -> p k b", k=4)
        pxn = [work[:, 1024 + D * k:1024 + D * (k + 1)] for k in range(4)]
        pxT = [work[:, 2048 + D * k:2048 + D * (k + 1)] for k in range(4)]
        pdt = [work[:, 3072 + 512 * k:3072 + 512 * k + NT] for k in range(4)]
        mean_all, rstd_all = tab3[:, :, 3 * NH], tab3[:, :, 3 * NH + 1]
        dt_bank, cum_bank = bank[4], bank[5]

        CR = min(P, NT)
        cumT = work[:, 5120:5120 + NT // CR * P]

        def heads_of(a):
            return a.rearrange("p (b h) -> p b h", h=NH)

        with phase("steps") as block:
            @block.sync
            def _(e):
                e.wait_ge(S["p_kept"], 1)
                e.dma_start(cum_dram.rearrange("(k c) (h t) -> (c h) k t", k=NT // CR, h=NH),
                            cumT[0:CR, :].rearrange("p (k t) -> p k t", t=P)).then_inc(S["p_stored"], 16)
                e.wait_ge(S["p_stored"], 16)

            @block.vector
            def _(e):
                for c in range(NB // CHUNK):
                    e.wait_ge(S[f"x_loaded{c}"], 16)
                    for b in range(c * CHUNK, (c + 1) * CHUNK):
                        e.bn_stats(stats0[:, b, :], x_res[:, b * D:(b + 1) * D])
                n = 0

                def link(i):
                    nonlocal n
                    n += 1
                    i.then_inc(S["p_stats"], 1)
                    e.wait_ge(S["p_stats"], n)

                a, d, v, y = (pn[:, k] for k in range(4))
                link(e.engine_nop())
                e.tensor_tensor(a, stats0[:, :, 1], stats0[:, :, 4], ALU.add)
                e.tensor_tensor(v, stats0[:, :, 2], stats0[:, :, 5], ALU.add)
                link(e.tensor_tensor(d, stats0[:, :, 1], stats0[:, :, 4], ALU.subtract))
                e.tensor_scalar(mean_all, a, 0.5, None, ALU.mult)
                e.tensor_scalar(v, v, 1.0 / D, EPS, ALU.mult, ALU.add)
                link(e.tensor_tensor(d, d, d, ALU.mult))
                link(e.scalar_tensor_tensor(out=v, in0=d, scalar=0.25, in1=v, op0=ALU.mult, op1=ALU.add))
                link(e.tensor_scalar(a.bitcast(I32), v.bitcast(I32), 1, None, ALU.arith_shift_right))
                link(e.tensor_scalar(y.bitcast(I32), a.bitcast(I32), -1.0, float(0x5F3759DF), ALU.mult, ALU.add))
                for k in range(3):
                    link(e.tensor_tensor(a, y, y, ALU.mult))
                    link(e.scalar_tensor_tensor(out=a, in0=a, scalar=-0.5, in1=v, op0=ALU.mult, op1=ALU.mult))
                    link(e.scalar_tensor_tensor(out=rstd_all if k == 2 else y, in0=a, scalar=1.5, in1=y,
                                                op0=ALU.add, op1=ALU.mult))

                def norm(b, k):
                    if past(b - 3): e.wait_ge(S["p_tr"], b - 3)
                    e.tensor_scalar(pxn[k], x_res[:, ds(b * D, D)], tab[:, ds(b * TAB + 3 * NH, 1)],
                                    tab[:, ds(b * TAB + 3 * NH + 1, 1)], ALU.subtract, ALU.mult)\
                        .then_inc(S["p_xn"], 1)

                for k in range(4):
                    norm(k, k)
                with e.Fori(1, NB // 4) as quarter:
                    for k in range(4):
                        norm(4 * quarter + k, k)
                e.wait_ge(S["p_dt"], NB)
                v, ex, dt, nd = pdt
                link(e.tensor_tensor(heads_of(v), heads_of(dt_bank[:, 0:NT]),
                                     dtb.unsqueeze(1).to_broadcast([P, NB, NH]), ALU.add))
                link(e.tensor_scalar(ex, v, -1.0, None, ALU.mult))
                e.tensor_tensor(ex, ex, v, ALU.min).then_inc(S["p_min"], 1)
                e.wait_ge(S["p_act"], 1)
                link(e.scalar_tensor_tensor(out=dt, in0=v, scalar=0.0, in1=nd, op0=ALU.max, op1=ALU.add))
                e.tensor_copy(tab3[:, :, 2 * NH:3 * NH], heads_of(dt))
                link(e.tensor_tensor(heads_of(nd), heads_of(dt), expA.unsqueeze(1).to_broadcast([P, NB, NH]),
                                     ALU.mult))
                e.tensor_copy(tab3[:, :, 0:NH], heads_of(nd)).then_inc(S["p_nd"], 1)
                e.wait_ge(S["p_cum"], 1)
                e.tensor_copy(tab3[:, :, NH:2 * NH], heads_of(cum_bank[:, 0:NT]))

            @block.tensor
            def _(e):
                def transposes(b, k):
                    e.wait_ge(S["p_xn"], b + 1)
                    if past(b - 3): e.wait_ge(S["p_xnT"], b - 3)
                    for c in range(2):
                        last = e.transpose(bank[k][:, c * P:c * P + P], pxn[k][:, c * P:c * P + P], ident)
                    last.then_inc(S["p_tr"], 1)

                def dt_of(b, k):
                    e.wait_ge(S["p_xnT"], b + 1)
                    for c in range(2):
                        last = e.matmul(dt_bank[:, ds(b * NH, NH)], pxT[k][:, c * P:c * P + P], w_dt[:, c, :],
                                        start=c == 0, stop=c == 1)
                    last.then_inc(S["p_dt"], 1)

                for k in range(4):
                    transposes(k, k)
                    if k >= 2:
                        dt_of(k - 2, k - 2)
                with e.Fori(1, NB // 4) as quarter:
                    b = 4 * quarter
                    for k in range(4):
                        transposes(b + k, k)
                        dt_of(b + k - 2, (k - 2) % 4)
                dt_of(NB - 2, 2)
                dt_of(NB - 1, 3)
                e.wait_ge(S["p_nd"], 1)
                e.matmul(cum_bank[:, 0:NT], upper, pdt[3], start=True, stop=True).then_inc(S["p_cum"], 1)
                for k in range(0, NT, CR):
                    last = e.matmul(bank[6][0:CR, k // CR * P:k // CR * P + P], pdt[3][:, k:k + CR], upper,
                                    start=True, stop=True)
                last.then_inc(S["p_cumT"], 1)

            @block.scalar
            def _(e):
                def copy(b, k):
                    e.wait_ge(S["p_tr"], b + 1)
                    if past(b - 3): e.wait_ge(S["p_dt"], b - 3)
                    e.activation(pxT[k], bank[k][:, 0:D], ACT.Copy).then_inc(S["p_xnT"], 1)

                for k in range(4):
                    copy(k, k)
                with e.Fori(1, NB // 4) as quarter:
                    for k in range(4):
                        copy(4 * quarter + k, k)
                e.wait_ge(S["p_min"], 1)
                e.activation(pdt[1], pdt[1], ACT.Exp).then_inc(S["p_chain"], 1)
                e.wait_ge(S["p_chain"], 1)
                e.activation(pdt[3], pdt[1], ACT.Ln, bias=const[:, C_ONE:C_ONE + 1]).then_inc(S["p_act"], 1)
                e.wait_ge(S["p_cumT"], 1)
                e.activation(cumT[0:CR, :], bank[6][0:CR, 0:NT // CR * P], ACT.Copy).then_inc(S["p_kept"], 1)

        wpos[0] = rpos[0] = 0
        m_xn_ = wk(D)
        m_xT = wk(D).rearrange("p (k t) -> p k t", k=2)
        m_raw_ = wk(XBC).rearrange("p (j t) -> p j t", t=P)
        m_acc = wk(XBC).rearrange("p (j t) -> p j t", t=P)
        m_xt_ = wk(DI)
        m_xdt_ = wk(DI)
        m_xD = m_xt_
        m_E = wk(NH * P).rearrange("p (h t) -> p h t", t=P)
        m_zg_ = wk(DI)
        m_y_ = m_raw_[:, 0:4, :].rearrange("p j t -> p (j t)")
        m_yT = wr(2 * DI).rearrange("p (s k t) -> p s k t", s=2, k=4)
        m_Gm = wk(P)
        cur = tiny[:, 0:TAB]
        c_dec, c_dt = cur[:, NH:2 * NH], cur[:, 2 * NH:3 * NH]
        m_ss_, m_xh_, m_t_, m_r_ = (tiny[:, 26 + k:27 + k] for k in range(4))
        c_cols, r_cols = stat_cols(32), stat_cols(68)
        c_xn_ = wk(D)
        c_ctx_ = wk(D)
        c_T = wr(4 * D).rearrange("p (s k t) -> p s k t", s=2, k=4)
        c_qk = wk(2 * D)
        c_rot_ = wk(2 * D)
        c_qT = wk(2 * D).rearrange("p (o k t) -> p o k t", o=2, k=2)
        c_kT_ = wk(D).rearrange("p (k t) -> p k t", k=2)
        VX = DH + 1
        c_vx = wk(HEADS * VX).rearrange("p (h d) -> p h d", d=VX)
        c_P = [wk(512), wk(512)]
        c_PT = wk(512)
        c_o_ = c_qk[:, 0:D]
        c_oT = wr(2 * D).rearrange("p (s k t) -> p s k t", s=2, k=2)
        c_mx = tiny[:, 48:52]
        c_ri = tiny[:, 52:68]
        r_xn_ = wk(D)
        r_T = wk(D).rearrange("p (k t) -> p k t", k=2)

        def head_cols(blk, odd, g):
            return blk * NH + 2 * g + odd

        def attention_stage(pre, scale, qT, kT, vx, kv_of, Pb, PTb, mx, sc_banks, pt_bank, o_bank, o_free):
            def scores(e, b, g):
                e.wait_ge(S[pre + "_kT"], b + 1)
                e.wait_ge(S[pre + "_qT"], 2 * b + 2)
                bk = sc_banks[g % 2]
                if past(4 * b + g - 1): e.wait_ge(S[pre + "_sub"], 4 * b + g - 1)
                for blk in range(2):
                    for odd in range(2):
                        c = (2 * blk + odd) * P
                        last = e.matmul(bk[:, c:c + P], qT[32 * g:32 * g + 32, odd, blk, :],
                                        kT[32 * g:32 * g + 32, blk, :], start=True, stop=True)
                last.then_inc(S[pre + "_sc"], 1)

            def softmax(e, b, g):
                s3 = sc_banks[g % 2][:, :].rearrange("p (h k) -> p h k", k=P)
                e.wait_ge(S[pre + "_sc"], 4 * b + g + 1)
                if past(4 * b + g): e.wait_ge(S[pre + "_sub"], 4 * b + g)
                e.tensor_reduce(mx, s3, AX.X, ALU.max).then_inc(S[pre + "_max"], 1)
                e.wait_ge(S[pre + "_max"], 4 * b + g + 1)
                if past(4 * b + g - 1): e.wait_ge(S[pre + "_ptr"], 4 * b + g - 1)
                e.tensor_tensor(Pb[g % 2].rearrange("p (h k) -> p h k", k=P), s3,
                                mx.unsqueeze(2).to_broadcast([P, 4, P]), ALU.subtract).then_inc(S[pre + "_sub"], 1)

            def exponents(e, b, g):
                e.wait_ge(S[pre + "_sub"], 4 * b + g + 1)
                e.activation(Pb[g % 2], Pb[g % 2], ACT.Exp, scale=scale).then_inc(S[pre + "_exp"], 1)

            def turn(e, b, g):
                e.wait_ge(S[pre + "_exp"], 4 * b + g + 1)
                if g == 0: e.wait_ge(S[pre + "_v"], b + 1)
                if past(4 * b + g): e.wait_ge(S[pre + "_pt"], 4 * b + g)
                for h in range(4):
                    last = e.transpose(pt_bank[:, h * P:h * P + P], Pb[g % 2][:, h * P:h * P + P], ident)
                last.then_inc(S[pre + "_ptr"], 1)

            def take(e, b, g):
                e.wait_ge(S[pre + "_ptr"], 4 * b + g + 1)
                if past(4 * b + g): e.wait_ge(S[pre + "_pv"], 4 * b + g)
                e.activation(PTb, pt_bank[:, :], ACT.Copy).then_inc(S[pre + "_pt"], 1)

            def values(e, b, g):
                e.wait_ge(S[pre + "_pt"], 4 * b + g + 1)
                if g == 0:
                    e.wait_ge(S[pre + "_v"], b + 1)
                    if past(b): e.wait_ge(S[o_free], b)
                for blk in range(2):
                    for odd in range(2):
                        h, c = head_cols(blk, odd, g), (2 * blk + odd) * P
                        last = e.matmul(o_bank[:, h * VX:h * VX + VX], PTb[:, c:c + P], vx[:, kv_of(h), :],
                                        start=True, stop=True)
                last.then_inc(S[pre + "_pv"], 1)

            def normalise(e, b, o_, ri, free, free_count):
                o3 = o_bank[:, 0:HEADS * VX].rearrange("p (h d) -> p h d", d=VX)
                e.wait_ge(S[pre + "_pv"], 4 * b + 4)
                e.reciprocal(ri, o3[:, :, DH]).then_inc(S[pre + "_rinv"], 1)
                e.wait_ge(S[pre + "_rinv"], b + 1)
                for f, c in zip(free, free_count):
                    if past(c): e.wait_ge(S[f], c)
                e.tensor_tensor(o_.rearrange("p (h d) -> p h d", d=DH), o3[:, :, 0:DH],
                                ri.unsqueeze(2).to_broadcast([P, HEADS, DH]), ALU.mult).then_inc(S[pre + "_o"], 1)

            return dict(scores=scores, softmax=softmax, exponents=exponents, turn=turn, take=take,
                        values=values, normalise=normalise)

        att0 = attention_stage("c", DH ** -0.5, c_qT, c_kT_, c_vx, lambda h: h, c_P, c_PT, c_mx,
                               [bank[3], bank[4]], bank[5], bank[6], "c_o")

        with phase("layer0") as block:
            @block.sync
            def _(e):
                def load_sums(b):
                    if past(b): e.wait_ge(S["m_y"], 2 * b)
                    if past(b): e.wait_ge(S["m_ss"], b)
                    src = cum_dram[b] if isinstance(b, int) else cum_dram[ds(b, 1)].rearrange("o n -> (o n)")
                    e.dma_start(m_E.rearrange("p h t -> p (h t)"), src.partition_broadcast(P))\
                        .then_inc(S["m_cum"], 16)

                def load_context(b):
                    if past(b): e.wait_ge(S["c_tr"], b)
                    e.dma_start(c_ctx_, tile(ctx, b)).then_inc(S["c_ctx"], 16)

                def store_output(b):
                    e.wait_ge(S["r_xo"], b + 1)
                    e.dma_start(tile(xo_dram, b), r_xo_[:, :]).then_inc(S["r_store"], 16)

                def step(i):
                    b = i
                    if live(b):
                        load_sums(b)
                    b = i - 4
                    if live(b):
                        store_output(b)
                    b = i
                    if live(b):
                        load_context(b)

                pipeline(e, 4, step)
                e.wait_ge(S["r_store"], 16 * NB)

            @block.tensor
            def _(e):
                def m_transpose(b):
                    e.wait_ge(S["m_xn"], b + 1)
                    if past(b): e.wait_ge(S["m_yx"], b)
                    for c in range(2):
                        last = e.transpose(bank[0][:, c * P:c * P + P], m_xn_[:, c * P:c * P + P], ident)
                    last.then_inc(S["m_tr"], 1)

                def m_project(b):
                    e.wait_ge(S["m_xnT"], b + 1)
                    if past(b): e.wait_ge(S["m_ylo"], b)
                    for j in range(4):
                        project32_T(e, bank[1][:, j * P:j * P + P], m_xT, w_in, DI + j * P)
                    for j in range(2):
                        last = project32_T(e, bank[0][:, j * P:j * P + P], m_xT, w_in, 2 * DI + j * P)
                    last.then_inc(S["m_xbc"], 1)

                def m_gate(b):
                    e.wait_ge(S["m_xnT"], b + 1)
                    if past(b): e.wait_ge(S["m_x1"], b)
                    project32(e, bank[2][:, :], m_xT, w_in, 2, 0, DI).then_inc(S["m_z"], 1)

                def m_tokens(b):
                    e.wait_ge(S["m_xbcs"], b + 1)
                    for j in range(4):
                        last = e.transpose(bank[1][:, j * P:j * P + P], m_acc[:, j, :], ident)
                    last.then_inc(S["m_xtr"], 1)
                    e.matmul(bank[0][:, 0:P], m_acc[:, 4, :], m_acc[:, 5, :], start=True, stop=True)\
                        .then_inc(S["m_g"], 1)

                def m_mix(b, half):
                    e.wait_ge(S["m_M"], 2 * b + 1 + half)
                    if half == 0:
                        e.wait_ge(S["m_xdt"], b + 1)
                        e.wait_ge(S["m_gm"], b + 1)
                    for h in range(4 * half, 4 * half + 4):
                        last = e.matmul(bank[0][:, h * HD:h * HD + HD], m_E[:, h, :],
                                        m_xdt_[:, h * HD:h * HD + HD], start=True, stop=True)
                    last.then_inc(S["m_y"], 1)

                def m_turn(b):
                    e.wait_ge(S["m_y2"], b + 1)
                    e.wait_ge(S["m_xt"], b + 1)
                    for c in range(4):
                        last = e.transpose(bank[1][:, c * P:c * P + P], m_y_[:, c * P:c * P + P], ident)
                    last.then_inc(S["m_ytr"], 1)

                def m_out(b):
                    e.wait_ge(S["m_ylo"], b + 1)
                    e.wait_ge(S["m_zg"], b + 1)
                    project(e, bank[2][:, 0:D], m_yT, w_out, 4, 0, D).then_inc(S["m_out"], 1)

                def c_transpose(b):
                    e.wait_ge(S["c_xn"], b + 1)
                    e.wait_ge(S["c_ctx"], 16 * (b + 1))
                    if past(4 * b): e.wait_ge(S["c_sub"], 4 * b)
                    for c in range(4):
                        src = (c_xn_ if c < 2 else c_ctx_)[:, (c % 2) * P:(c % 2) * P + P]
                        last = e.transpose(bank[3][:, c * P:c * P + P], src, ident)
                    last.then_inc(S["c_tr"], 1)

                def c_project(b):
                    e.wait_ge(S["c_lo"], b + 1)
                    if past(b): e.wait_ge(S["c_x2"], b)
                    if past(b): e.wait_ge(S["c_olo"], b)
                    project(e, bank[4][:, 0:D], c_T[:, :, 0:2, :], w_cq, 2, 0, D).then_inc(S["c_q"], 1)
                    project(e, bank[5][:, :], c_T[:, :, 2:4, :], w_ckv, 2, 0, 2 * D).then_inc(S["c_kv"], 1)

                def c_turn_qk(b):
                    e.wait_ge(S["c_qr"], b + 1)
                    for c in range(4):
                        last = e.transpose(bank[3][:, c * P:c * P + P], c_rot_[:, c * P:c * P + P], ident)
                    last.then_inc(S["c_qtr"], 1)

                def c_turn_o(b):
                    e.wait_ge(S["c_o"], b + 1)
                    e.wait_ge(S["c_pt"], 4 * b + 4)
                    for c in range(2):
                        last = e.transpose(bank[5][:, c * P:c * P + P], c_o_[:, c * P:c * P + P], ident)
                    last.then_inc(S["c_otr"], 1)

                def c_out(b):
                    e.wait_ge(S["c_olo"], b + 1)
                    e.wait_ge(S["c_sub"], 4 * b + 4)
                    project(e, bank[4][:, 0:D], c_oT, w_co, 2, 0, D).then_inc(S["c_proj"], 1)

                def r_transpose(b):
                    e.wait_ge(S["r_xn"], b + 1)
                    if past(b): e.wait_ge(S["r_xo"], b)
                    if past(2 * b): e.wait_ge(S["r_tg"], 2 * b)
                    for c in range(2):
                        last = e.transpose(bank[7][:, c * P:c * P + P], r_xn_[:, c * P:c * P + P], ident)
                    last.then_inc(S["r_tr"], 1)

                def r_forget_input(b):
                    e.wait_ge(S["r_xnT"], b + 1)
                    if past(b): e.wait_ge(S["r_d"], b)
                    for j in range(4):
                        project32_T(e, bank[7][:, j * P:j * P + P], r_T, w_rx, j * P, True, False)
                        last = project32_T(e, bank[7][:, j * P:j * P + P], d_state[:, :, :], w_ru, j * P, False, True)
                    last.then_inc(S["r_fi"], 1)

                def r_candidate_out(b):
                    e.wait_ge(S["r_tfi"], 4 * b + 4)
                    for j in range(2):
                        n = 2 * D + j * P
                        project32_T(e, bank[7][:, j * P:j * P + P], r_T, w_rx, n, True, False)
                        project32_T(e, bank[7][:, j * P:j * P + P], d_state[:, :, :], w_ru, n, False, True)
                    project32(e, bank[7][:, D:2 * D], r_T, w_rxo, 2, 0, D).then_inc(S["r_go"], 1)

                def step(i):
                    b = i - 3
                    if live(b):
                        c_out(b)
                    b = i
                    if live(b):
                        m_transpose(b)
                    b = i - 1
                    if live(b):
                        m_turn(b)
                    b = i - 2
                    if live(b):
                        c_project(b)
                    b = i - 1
                    if live(b):
                        m_out(b)
                    b = i
                    if live(b):
                        m_project(b)
                    b = i - 2
                    if live(b):
                        c_turn_qk(b)
                    b = i
                    if live(b):
                        m_gate(b)
                    b = i - 2
                    if live(b):
                        att0["scores"](e, b, 0)
                        att0["scores"](e, b, 1)
                    b = i - 4
                    if live(b):
                        r_forget_input(b)
                    b = i - 2
                    if live(b):
                        att0["turn"](e, b, 0)
                        att0["scores"](e, b, 2)
                        att0["scores"](e, b, 3)
                        att0["turn"](e, b, 1)
                        att0["values"](e, b, 0)
                    b = i - 4
                    if live(b):
                        r_candidate_out(b)
                    b = i - 2
                    if live(b):
                        att0["values"](e, b, 1)
                        att0["turn"](e, b, 2)
                    b = i
                    if live(b):
                        m_tokens(b)
                    b = i - 2
                    if live(b):
                        att0["values"](e, b, 2)
                        att0["turn"](e, b, 3)
                    b = i - 1
                    if live(b):
                        c_transpose(b)
                    b = i - 3
                    if live(b):
                        r_transpose(b)
                    b = i - 2
                    if live(b):
                        att0["values"](e, b, 3)
                    b = i
                    if live(b):
                        m_mix(b, 0)
                    b = i - 2
                    if live(b):
                        c_turn_o(b)
                    b = i
                    if live(b):
                        m_mix(b, 1)

                pipeline(e, 4, step)

            @block.scalar
            def _(e):
                def hi(pre, b, dst, src, *free):
                    e.wait_ge(S[pre + "_tr"], b + 1)
                    for user in free:
                        if past(b): e.wait_ge(S[user], b)
                    e.activation(dst, src, ACT.Copy).then_inc(S[pre + "_hi"], 1)

                def take_T(ready, b, dst, src, done, *free):
                    e.wait_ge(S[ready], b + 1)
                    for user in free:
                        if past(b): e.wait_ge(S[user], b)
                    e.activation(dst, src, ACT.Copy).then_inc(S[done], 1)

                def m_taps(b):
                    e.wait_ge(S["m_xbc"], b + 1)
                    if past(b): e.wait_ge(S["m_xbcs"], b)
                    if past(b): e.wait_ge(S["m_ytr"], b)
                    if past(b): e.wait_ge(S["m_ss"], b)
                    e.activation(m_raw_[:, 0:4, :], bank[1][:, :].rearrange("p (j t) -> p j t", t=P), ACT.Copy)
                    e.activation(m_raw_[:, 4:6, :], bank[0][:, 0:2 * P].rearrange("p (j t) -> p j t", t=P), ACT.Copy)\
                        .then_inc(S["m_raw"], 1)
                    e.wait_ge(S["m_raw"], b + 1)
                    if past(b): e.wait_ge(S["m_g"], b)
                    if past(b): e.wait_ge(S["m_xtr"], b)
                    for j in range(6):
                        last = e.activation(m_acc[:, j, :], m_raw_[:, j, :], ACT.Identity,
                                            bias=cb[:, j:j + 1], scale=cw[:, j, CONV - 1:CONV])
                    last.then_inc(S["m_tap"], 1)

                def m_gate(b):
                    e.wait_ge(S["m_z"], b + 1)
                    if past(b): e.wait_ge(S["m_y2"], b)
                    e.activation(m_zg_, bank[2][:, :], ACT.Tanh, scale=0.5).then_inc(S["m_ztanh"], 1)

                def m_silu(b):
                    e.wait_ge(S["m_conv"], b + 1)
                    e.activation(m_raw_, m_acc, ACT.Tanh).then_inc(S["m_xtanh"], 1)

                def m_tokens(b):
                    e.wait_ge(S["m_xtr"], b + 1)
                    if past(b): e.wait_ge(S["m_yx"], b)
                    if past(b): e.wait_ge(S["m_xdt"], b)
                    e.activation(m_xt_, bank[1][:, :], ACT.Copy).then_inc(S["m_xt"], 1)

                def m_exp(b, half):
                    e.wait_ge(S["m_rel"], 2 * b + 1 + half)
                    e.activation(m_E[:, 4 * half:4 * half + 4, :], m_E[:, 4 * half:4 * half + 4, :], ACT.Exp,
                                 scale=-1.0).then_inc(S["m_exp"], 1)

                def m_square(b):
                    e.wait_ge(S["m_y2"], b + 1)
                    if past(b): e.wait_ge(S["m_rs"], b)
                    e.activation(m_E[:, 0:4, :].rearrange("p h t -> p (h t)"), m_y_, ACT.Square, accum_out=m_ss_)\
                        .then_inc(S["m_ss"], 1)

                def m_yhi(b):
                    e.wait_ge(S["m_ytr"], b + 1)
                    if past(b): e.wait_ge(S["m_out"], b)
                    e.activation(m_yT[:, 0], bank[1][:, :].rearrange("p (k t) -> p k t", t=P), ACT.Copy)\
                        .then_inc(S["m_yhi"], 1)

                def c_values(b):
                    e.wait_ge(S["c_kb"], b + 1)
                    if past(4 * b): e.wait_ge(S["c_pv"], 4 * b)
                    e.activation(c_vx[:, :, 0:DH], bank[5][:, D:2 * D].rearrange("p (h d) -> p h d", d=DH), ACT.Copy)\
                        .then_inc(S["c_v"], 1)

                def c_heads(b):
                    e.wait_ge(S["c_qtr"], b + 1)
                    if past(4 * b): e.wait_ge(S["c_sc"], 4 * b)
                    e.activation(c_kT_, bank[3][:, D:2 * D].rearrange("p (k t) -> p k t", k=2), ACT.Copy)\
                        .then_inc(S["c_kT"], 1)
                    for odd, mask in enumerate((m_even, m_odd)):
                        e.activation(c_qT[:, odd], bank[3][:, 0:D].rearrange("p (k t) -> p k t", k=2),
                                     ACT.Copy, scale=mask).then_inc(S["c_qT"], 1)

                def c_ohi(b):
                    e.wait_ge(S["c_otr"], b + 1)
                    if past(b): e.wait_ge(S["c_proj"], b)
                    e.activation(c_oT[:, 0], bank[5][:, 0:D].rearrange("p (k t) -> p k t", k=2), ACT.Copy)\
                        .then_inc(S["c_ohi"], 1)

                def r_gates(b):
                    e.wait_ge(S["r_fi"], b + 1)
                    if past(b): e.wait_ge(S["r_d"], b)
                    for j in range(4):
                        e.activation(r_tfi_[:, j, :], bank[7][:, j * P:j * P + P], ACT.Tanh, scale=0.5,
                                     bias=gb[:, j:j + 1]).then_inc(S["r_tfi"], 1)

                def r_candidate(b):
                    e.wait_ge(S["r_go"], b + 1)
                    for j in range(2):
                        e.activation(r_tg_[:, j, :], bank[7][:, j * P:j * P + P], ACT.Tanh,
                                     bias=gb[:, 4 + j:5 + j]).then_inc(S["r_tg"], 1)
                    if past(16 * b): e.wait_ge(S["r_store"], 16 * b)
                    e.activation(r_xo_[:, :], bank[7][:, D:2 * D], ACT.Copy).then_inc(S["r_xo"], 1)

                def step(i):
                    b = i - 1
                    if live(b):
                        m_square(b)
                        m_yhi(b)
                    b = i
                    if live(b):
                        take_T("m_tr", b, m_xT, bank[0][:, 0:D].rearrange("p (k t) -> p k t", k=2), "m_xnT",
                               "m_xbc", "m_z")
                    b = i - 2
                    if live(b):
                        c_heads(b)
                    b = i
                    if live(b):
                        m_taps(b)
                    b = i - 2
                    if live(b):
                        att0["exponents"](e, b, 0)
                        c_values(b)
                    b = i
                    if live(b):
                        m_gate(b)
                    b = i - 2
                    if live(b):
                        att0["take"](e, b, 0)
                        att0["exponents"](e, b, 1)
                    b = i - 4
                    if live(b):
                        r_gates(b)
                    b = i
                    if live(b):
                        m_silu(b)
                        m_exp(b, 0)
                    b = i - 2
                    if live(b):
                        att0["take"](e, b, 1)
                        att0["exponents"](e, b, 2)
                    b = i - 4
                    if live(b):
                        r_candidate(b)
                    b = i - 2
                    if live(b):
                        att0["take"](e, b, 2)
                        att0["exponents"](e, b, 3)
                    b = i
                    if live(b):
                        m_exp(b, 1)
                        m_tokens(b)
                    b = i - 2
                    if live(b):
                        att0["take"](e, b, 3)
                    b = i - 1
                    if live(b):
                        hi("c", b, c_T[:, 0], bank[3][:, :].rearrange("p (k t) -> p k t", k=4), "c_kv")
                    b = i - 2
                    if live(b):
                        c_ohi(b)
                    b = i - 3
                    if live(b):
                        take_T("r_tr", b, r_T, bank[7][:, 0:D].rearrange("p (k t) -> p k t", k=2), "r_xnT", "r_go")

                pipeline(e, 4, step)

            @block.vector
            def _(e):
                def lo(pre, b, dst, src, high):
                    e.wait_ge(S[pre + "hi"], b + 1)
                    e.tensor_tensor(dst, src, high.bitcast(F32), ALU.subtract).then_inc(S[pre + "lo"], 1)

                def apply_norm(pre, b, dst, src, mean, rstd):
                    e.tensor_scalar(dst, src, mean, rstd, ALU.subtract, ALU.mult).then_inc(S[pre + "_xn"], 1)

                def m_current(b):
                    if past(b): e.wait_ge(S["m_rel"], 2 * b)
                    if past(b): e.wait_ge(S["m_xdt"], b)
                    e.tensor_scalar(cur, tab[:, ds(b * TAB, TAB)], 1.0, None, ALU.mult).then_inc(S["m_cur"], 1)
                    e.wait_ge(S["m_cur"], b + 1)
                    if past(b): e.wait_ge(S["m_tr"], b)
                    apply_norm("m", b, m_xn_, x_res[:, ds(b * D, D)], cur[:, 3 * NH:3 * NH + 1],
                               cur[:, 3 * NH + 1:3 * NH + 2])

                def m_convolve(b):
                    e.wait_ge(S["m_tap"], b + 1)
                    for k in range(1, CONV):
                        if k > 1:
                            e.wait_ge(S["m_conv2"], 2 * b + k - 1)
                        for j in range(6):
                            last = e.scalar_tensor_tensor(
                                out=m_acc[:, j, k:P], in0=m_raw_[:, j, 0:P - k],
                                scalar=cw[:, j, CONV - 1 - k:CONV - k], in1=m_acc[:, j, k:P],
                                op0=ALU.mult, op1=ALU.add)
                        last.then_inc(S["m_conv2" if k < CONV - 1 else "m_conv"], 1)

                def m_silu(b):
                    e.wait_ge(S["m_xtanh"], b + 1)
                    e.scalar_tensor_tensor(out=m_acc, in0=m_raw_, scalar=1.0, in1=m_acc,
                                           op0=ALU.add, op1=ALU.mult).then_inc(S["m_xbcs"], 1)

                def m_gate(b):
                    e.wait_ge(S["m_ztanh"], b + 1)
                    e.scalar_tensor_tensor(out=m_zg_, in0=m_zg_, scalar=1.0, in1=bank[2][:, :],
                                           op0=ALU.add, op1=ALU.mult).then_inc(S["m_zg"], 1)

                def m_masked(b):
                    e.wait_ge(S["m_g"], b + 1)
                    if past(b): e.wait_ge(S["m_M"], 2 * b)
                    e.tensor_tensor(m_Gm, bank[0][:, 0:P], upper, ALU.mult).then_inc(S["m_gm"], 1)

                def m_relative(b, half):
                    e.wait_ge(S["m_cum"], 16 * (b + 1))
                    e.wait_ge(S["m_cur"], b + 1)
                    for h in range(4 * half, 4 * half + 4):
                        last = e.tensor_scalar(m_E[:, h, :], m_E[:, h, :], c_dec[:, h:h + 1], 0.0,
                                               ALU.subtract, ALU.max)
                    last.then_inc(S["m_rel"], 1)

                def m_weights(b, half):
                    e.wait_ge(S["m_exp"], 2 * b + 1 + half)
                    part = m_E[:, 4 * half:4 * half + 4, :]
                    if half == 0:
                        e.wait_ge(S["m_gm"], b + 1)
                    e.tensor_tensor(part, part, m_Gm.unsqueeze(1).to_broadcast([P, 4, P]), ALU.mult)\
                        .then_inc(S["m_M"], 1)

                def m_gated(b):
                    e.wait_ge(S["m_y"], 2 * b + 2)
                    e.wait_ge(S["m_xd"], b + 1)
                    e.wait_ge(S["m_zg"], b + 1)
                    if past(b): e.wait_ge(S["m_ytr"], b)
                    e.tensor_tensor(m_y_, bank[0][:, :], m_xD, ALU.add).then_inc(S["m_yx"], 1)
                    e.wait_ge(S["m_yx"], b + 1)
                    e.tensor_tensor(m_y_, m_y_, m_zg_, ALU.mult).then_inc(S["m_y2"], 1)

                def m_root(b):
                    e.wait_ge(S["m_ss"], b + 1)
                    e.tensor_scalar(m_ss_, m_ss_, float(4 * DI * EPS), None, ALU.add).then_inc(S["m_seed"], 1)
                    if past(b): e.wait_ge(S["m_x1"], b)
                    rsqrt_seed(e, "m", b, m_ss_, m_xh_, m_t_, m_r_)

                def m_ylow(b):
                    e.wait_ge(S["m_yhi"], b + 1)
                    e.tensor_tensor(m_yT[:, 1], bank[1][:, :].rearrange("p (k t) -> p k t", t=P),
                                    m_yT[:, 0].bitcast(F32), ALU.subtract).then_inc(S["m_ylo"], 1)

                def m_residual(b):
                    e.wait_ge(S["m_out"], b + 1)
                    e.wait_ge(S["m_rs"], b + 1)
                    e.scalar_tensor_tensor(out=x_res[:, ds(b * D, D)], in0=bank[2][:, 0:D], scalar=m_r_, in1=x_res[:, ds(b * D, D)],
                                           op0=ALU.mult, op1=ALU.add).then_inc(S["m_x1"], 1)

                def c_norm(b):
                    e.wait_ge(S["c_rs"], b + 1)
                    if past(b): e.wait_ge(S["c_tr"], b)
                    apply_norm("c", b, c_xn_, x_res[:, ds(b * D, D)], c_cols[1][:, 0:1], c_cols[5])

                def c_bias(b):
                    e.wait_ge(S["c_kv"], b + 1)
                    if past(b): e.wait_ge(S["c_otr"], b)
                    e.tensor_tensor(c_qk[:, D:2 * D], bank[5][:, 0:D], bqk_row[:, D:2 * D], ALU.add)\
                        .then_inc(S["c_kb"], 1)
                    e.tensor_tensor(c_qk[:, 0:D], bank[4][:, 0:D], bqk_row[:, 0:D], ALU.add).then_inc(S["c_qb"], 1)

                def c_rotate(b):
                    e.wait_ge(S["c_rot"], b + 1)
                    e.tensor_tensor(c_qk.rearrange("p (h d) -> p h d", d=DH), c_qk.rearrange("p (h d) -> p h d", d=DH),
                                    const[:, C_COS:C_COS + DH].unsqueeze(1).to_broadcast([P, 2 * HEADS, DH]),
                                    ALU.mult).then_inc(S["c_cos"], 1)
                    e.wait_ge(S["c_cos"], b + 1)
                    e.tensor_tensor(c_rot_, c_rot_, c_qk, ALU.add).then_inc(S["c_qr"], 1)

                def c_residual(b):
                    e.wait_ge(S["c_proj"], b + 1)
                    e.wait_ge(S["c_x1b"], b + 1)
                    e.tensor_tensor(x_res[:, ds(b * D, D)], bank[4][:, 0:D], x_res[:, ds(b * D, D)], ALU.add).then_inc(S["c_x2"], 1)

                def r_norm(b):
                    e.wait_ge(S["r_rs"], b + 1)
                    if past(b): e.wait_ge(S["r_tr"], b)
                    apply_norm("r", b, r_xn_, x_res[:, ds(b * D, D)], r_cols[1][:, 0:1], r_cols[5])

                def r_update(b):
                    e.wait_ge(S["r_tfi"], 4 * b + 4)
                    e.scalar_tensor_tensor(out=r_tfi_[:, 0:2, :], in0=r_tfi_[:, 0:2, :], scalar=1.0,
                                           in1=d_state[:, :, :], op0=ALU.add, op1=ALU.mult).then_inc(S["r_a"], 1)
                    e.wait_ge(S["r_tg"], 2 * b + 2)
                    e.scalar_tensor_tensor(out=r_tfi_[:, 2:4, :], in0=r_tfi_[:, 2:4, :], scalar=1.0,
                                           in1=r_tg_[:, :, :], op0=ALU.add, op1=ALU.mult).then_inc(S["r_b"], 1)
                    e.wait_ge(S["r_b"], b + 1)
                    e.scalar_tensor_tensor(out=d_state[:, :, :], in0=r_tfi_[:, 0:2, :], scalar=0.5,
                                           in1=r_tfi_[:, 2:4, :], op0=ALU.mult, op1=ALU.add)\
                        .then_inc(S["r_d"], 1)

                e.memset(c_vx[:, :, DH:VX], 1.0)

                def step(i):
                    b = i
                    if live(b):
                        m_current(b)
                    b = i - 3
                    if live(b):
                        lo("c_o", b, c_oT[:, 1], bank[5][:, 0:D].rearrange("p (k t) -> p k t", k=2), c_oT[:, 0])
                    b = i - 1
                    if live(b):
                        m_gated(b)
                    b = i - 3
                    if live(b):
                        c_residual(b)
                    b = i - 1
                    if live(b):
                        m_root(b)
                        m_ylow(b)
                    b = i - 2
                    if live(b):
                        c_bias(b)
                    b = i - 3
                    if live(b):
                        row_statistics(e, "r", b, x_res[:, ds(b * D, D)], r_cols, ("c_x2", b + 1))
                    b = i - 1
                    if live(b):
                        m_residual(b)
                    b = i - 2
                    if live(b):
                        c_rotate(b)
                    b = i - 1
                    if live(b):
                        row_statistics(e, "c", b, x_res[:, ds(b * D, D)], c_cols, ("m_x1", b + 1))
                    b = i
                    if live(b):
                        m_relative(b, 0)
                        m_relative(b, 1)
                    b = i - 2
                    if live(b):
                        att0["softmax"](e, b, 0)
                        att0["softmax"](e, b, 1)
                    b = i
                    if live(b):
                        m_convolve(b)
                    b = i - 2
                    if live(b):
                        att0["softmax"](e, b, 2)
                    b = i
                    if live(b):
                        m_silu(b)
                    b = i - 2
                    if live(b):
                        att0["softmax"](e, b, 3)
                    b = i - 3
                    if live(b):
                        r_norm(b)
                    b = i
                    if live(b):
                        m_gate(b)
                        m_masked(b)
                    b = i - 1
                    if live(b):
                        c_norm(b)
                    b = i - 4
                    if live(b):
                        r_update(b)
                    b = i
                    if live(b):
                        m_weights(b, 0)
                        m_weights(b, 1)
                    b = i - 2
                    if live(b):
                        att0["normalise"](e, b, c_o_, c_ri, ["c_otr"], [b])
                    b = i - 1
                    if live(b):
                        lo("c_", b, c_T[:, 1], bank[3][:, :].rearrange("p (k t) -> p k t", k=4), c_T[:, 0])

                pipeline(e, 4, step)

            @block.gpsimd
            def _(e):
                def scale_tokens(b):
                    x3 = m_xt_.rearrange("p (h d) -> p h d", d=HD)
                    e.wait_ge(S["m_xt"], b + 1)
                    e.wait_ge(S["m_cur"], b + 1)
                    if past(2 * b): e.wait_ge(S["m_y"], 2 * b)
                    e.tensor_tensor(m_xdt_.rearrange("p (h d) -> p h d", d=HD), x3,
                                    c_dt.unsqueeze(2).to_broadcast([P, NH, HD]), ALU.mult).then_inc(S["m_xdt"], 1)
                    e.wait_ge(S["m_xdt"], b + 1)
                    e.tensor_tensor(m_xD.rearrange("p (h d) -> p h d", d=HD), x3,
                                    dpar.unsqueeze(2).to_broadcast([P, NH, HD]), ALU.mult).then_inc(S["m_xd"], 1)

                def rotate(b):
                    e.wait_ge(S["c_kb"], b + 1)
                    e.wait_ge(S["c_qb"], b + 1)
                    if past(b): e.wait_ge(S["c_qtr"], b)
                    e.tensor_tensor(c_rot_.rearrange("p (h o d) -> p h o d", o=2, d=DH // 2),
                                    c_qk.rearrange("p (h o d) -> p h o d", o=2, d=DH // 2)[:, :, ::-1, :],
                                    const[:, C_SIN:C_SIN + DH].rearrange("p (o d) -> p o d", o=2).unsqueeze(1)
                                    .to_broadcast([P, 2 * HEADS, 2, DH // 2]), ALU.mult).then_inc(S["c_rot"], 1)

                def add_bias(b):
                    e.wait_ge(S["c_xn"], b + 1)
                    e.tensor_tensor(x_res[:, ds(b * D, D)], x_res[:, ds(b * D, D)], bo2_row, ALU.add).then_inc(S["c_x1b"], 1)

                def newton(pre, b, xh_, t_, y_):
                    rsqrt_newton(e, pre, b, xh_, t_, y_)

                def step(i):
                    b = i - 1
                    if live(b):
                        newton("m", b, m_xh_, m_t_, m_r_)
                    b = i - 2
                    if live(b):
                        rotate(b)
                    b = i - 1
                    if live(b):
                        newton("c", b, *c_cols[3:])
                    b = i - 3
                    if live(b):
                        newton("r", b, *r_cols[3:])
                    b = i
                    if live(b):
                        scale_tokens(b)
                    b = i - 1
                    if live(b):
                        add_bias(b)

                pipeline(e, 3, step)

        layer0_weights.close()
        w1r = sb("w1r", [P, 15360], F32R)
        w1p = sb("w1p", [P, 2048])
        w_sqkv = parts_view(w1r, 0, 2, D + 2 * KV * DH)
        w_so = parts_view(w1r, 1536, 2, D)
        w_gu = parts_view(w1r, 0, 2, 10 * 2 * P)
        w_dn = parts_view(w1r, 10240, 10, D)
        w_uo = plain_view(w1p, 0, 2, D)
        w_dq = plain_view(w1p, 512, 2, D)
        w_dk = plain_view(w1p, 1024, 2, D)
        w_dv = plain_view(w1p, 1536, 2, D)

        v_row, dbv_row = rows[:, 0:D], rows[:, D:2 * D]
        NQ = D + 2 * KV * DH
        qkv_stage = work[:, 0:2 * NQ].rearrange("p (k n) -> p k n", k=2)
        so_stage = work[:, 768:768 + 2 * D].rearrange("p (k n) -> p k n", k=2)
        gate_stage = work[0:E, 1280:1280 + D]
        jobs1 = []
        for r in range(2):
            jobs1 += [(uo[r * P:(r + 1) * P, :], D, plain(w_uo, r * P), 0.5, None),
                      (d_Wq[r * P:(r + 1) * P, :], D, plain(w_dq, r * P), 1.0, None),
                      (d_Wk[r * P:(r + 1) * P, :], D, plain(w_dk, r * P), 1.0, None),
                      (d_Wv[r * P:(r + 1) * P, :], D, plain(w_dv, r * P), 1.0, None)]
        w1 = weights("w1", work[:, 2048:6144], jobs1)
        with phase("between") as block:
            @block.sync
            def _(e):
                for dst, src in ((qkv_stage[:, :, 0:D], s_wq.rearrange("(k p) n -> p k n", p=P)),
                                 (qkv_stage[:, :, D:D + KV * DH], s_wk.rearrange("(k p) n -> p k n", p=P)),
                                 (qkv_stage[:, :, D + KV * DH:NQ], s_wv.rearrange("(k p) n -> p k n", p=P)),
                                 (so_stage, s_wo.rearrange("(k p) n -> p k n", p=P)),
                                 (gcol, s_g.rearrange("(j p) -> p j", p=P)),
                                 (dbq, d_bq.rearrange("(j p) -> p j", p=P)),
                                 (dbk, d_bk.rearrange("(j p) -> p j", p=P)),
                                 (dbv_row, d_bv.partition_broadcast(P)), (lbb, lb_bias.partition_broadcast(P)),
                                 (gate_stage, gate_w)):
                    with nc.allow_non_contiguous_dma(reason="small vectors, once"):
                        e.dma_start(dst, src).then_inc(S["l1_small"], 16)
                w1[0](e)

            @block.tensor
            def _(e):
                w1[1](e)
                e.wait_ge(S["l1_small"], 160)
                for c in range(2):
                    last = e.transpose(bank[4][:, c * E:c * E + E], gate_stage[:, c * P:c * P + P], ident[0:E, 0:E])
                last.then_inc(S["w1_tr"], 1)
                e.wait_ge(S["w1_lo"], len(jobs1))
                project32(e, bank[5][:, 0:D], d_state[:, :, :], w_uo, 2, 0, D).then_inc(S["b_v"], 1)

            @block.scalar
            def _(e):
                w1[2](e)
                e.wait_ge(S["w1_tr"], len(jobs1) + 1)
                e.activation(w_gate[:, :, :], bank[4][:, 0:2 * E].rearrange("p (k n) -> p k n", k=2), ACT.Copy)\
                    .then_inc(S["b_gate"], 1)
                e.wait_ge(S["l1_wg"], 1)
                e.activation(w_sqkv[:, 0], qkv_stage, ACT.Copy).then_inc(S["l1_whi"], 1)
                e.activation(w_so[:, 0], so_stage, ACT.Copy).then_inc(S["l1_whi"], 1)

            @block.vector
            def _(e):
                e.wait_ge(S["l1_small"], 160)
                for k in range(2):
                    last = e.tensor_scalar(qkv_stage[:, k, :], qkv_stage[:, k, :], gcol[:, k:k + 1], None, ALU.mult)
                last.then_inc(S["l1_wg"], 1)
                w1[3](e)
                e.wait_ge(S["l1_whi"], 2)
                e.tensor_tensor(w_sqkv[:, 1], qkv_stage, w_sqkv[:, 0].bitcast(F32), ALU.subtract)
                e.tensor_tensor(w_so[:, 1], so_stage, w_so[:, 0].bitcast(F32), ALU.subtract).then_inc(S["l1_wlo"], 1)
                e.wait_ge(S["b_v"], 1)
                e.tensor_tensor(v_row, bank[5][:, 0:D], bo_row, ALU.add).then_inc(S["b_vrow"], 1)

        wpos[0] = rpos[0] = 0
        s_xo_ = wk(D)
        s_h_ = wk(D)
        s_xn_ = wk(D)
        s_T = wr(2 * D).rearrange("p (s k t) -> p s k t", s=2, k=2)
        NR = D + 2 * KV * DH
        s_qr_ = wk(NR)
        s_qT_ = wk(2 * D).rearrange("p (o k t) -> p o k t", o=2, k=2)
        s_kT_ = wk(P)
        s_vx = wk(KV * VX).rearrange("p (h d) -> p h d", d=VX)
        s_P = [wk(512), wk(512)]
        s_PT = wk(512)
        s_o_ = wk(D)
        s_oT = wr(2 * D).rearrange("p (s k t) -> p s k t", s=2, k=2)
        s_mx, s_ri = tiny[:, 0:4], tiny[:, 4:20]

        s_cols, d_cols, g_cols = stat_cols(20), stat_cols(32), stat_cols(44)
        d_xn_ = wk(D)
        d_ctx_ = wk(D)
        d_T = wk(2 * D).rearrange("p (k t) -> p k t", k=4)
        d_qkT = wk(4 * P).rearrange("p (k t) -> p k t", k=4)
        d_v_ = wk(D)
        d_P_ = wk(P)
        d_PT = wk(P)
        d_mx, d_nm, d_sum, d_ri = (tiny[:, 56 + k:57 + k] for k in range(4))
        g_xn_ = wk(D)
        g_T = wk(D)
        g_mr = tiny[:, 60:62]

        att1 = attention_stage("s", 1.0 / float(np.sqrt(D)), s_qT_, s_kT_.unsqueeze(1).to_broadcast([P, 2, P]),
                               s_vx, lambda h: h % KV, s_P, s_PT, s_mx, [bank[2], bank[3]], bank[4], bank[1], "s_x4")

        with phase("layer1") as block:
            @block.sync
            def _(e):
                def load_output(b):
                    if past(b): e.wait_ge(S["s_u"], b)
                    e.dma_start(s_xo_, tile(xo_dram, b)).then_inc(S["s_xo"], 16)

                def load_context(b):
                    if past(b): e.wait_ge(S["d_tr"], b)
                    e.dma_start(d_ctx_, tile(ctx, b)).then_inc(S["d_ctx"], 16)

                def step(i):
                    b = i
                    if live(b):
                        load_output(b)
                    b = i - 2
                    if live(b):
                        load_context(b)

                pipeline(e, 2, step)

            @block.tensor
            def _(e):
                def s_transpose(b):
                    e.wait_ge(S["s_xn"], b + 1)
                    if past(b): e.wait_ge(S["s_qT"], 2 * b)
                    for c in range(2):
                        last = e.transpose(bank[0][:, c * P:c * P + P], s_xn_[:, c * P:c * P + P], ident)
                    last.then_inc(S["s_tr"], 1)

                def s_project(b):
                    e.wait_ge(S["s_lo"], b + 1)
                    project(e, bank[0][:, 0:NQ], s_T, w_sqkv, 2, 0, NQ).then_inc(S["s_qkv"], 1)

                def s_turn_qk(b):
                    e.wait_ge(S["s_qr"], 2 * b + 2)
                    e.wait_ge(S["s_v"], b + 1)
                    for c in range(3):
                        last = e.transpose(bank[0][:, c * P:c * P + P], s_qr_[:, c * P:c * P + P], ident)
                    last.then_inc(S["s_qtr"], 1)

                def s_turn_o(b):
                    e.wait_ge(S["s_o"], b + 1)
                    for c in range(2):
                        last = e.transpose(bank[1][:, c * P:c * P + P], s_o_[:, c * P:c * P + P], ident)
                    last.then_inc(S["s_otr"], 1)

                def s_out(b):
                    e.wait_ge(S["s_olo"], b + 1)
                    project(e, bank[1][:, 0:D], s_oT, w_so, 2, 0, D).then_inc(S["s_proj"], 1)

                def d_transpose(b):
                    e.wait_ge(S["d_xn"], b + 1)
                    e.wait_ge(S["d_ctx"], 16 * (b + 1))
                    if past(b): e.wait_ge(S["d_qk_sb"], b)
                    for c in range(4):
                        src = (d_xn_ if c < 2 else d_ctx_)[:, (c % 2) * P:(c % 2) * P + P]
                        last = e.transpose(bank[5][:, c * P:c * P + P], src, ident)
                    last.then_inc(S["d_tr"], 1)

                def d_project(b):
                    e.wait_ge(S["d_xcT"], b + 1)
                    for c in range(4):
                        last = project32_T(e, bank[5][:, c * P:c * P + P], d_T[:, 2 * (c // 2):2 * (c // 2) + 2, :],
                                           w_dq if c < 2 else w_dk, (c % 2) * P)
                    last.then_inc(S["d_qk"], 1)
                    if past(b): e.wait_ge(S["d_x5"], b)
                    project32(e, bank[6][:, 0:D], d_T[:, 2:4, :], w_dv, 2, 0, D).then_inc(S["d_vmm"], 1)

                def d_scores(b):
                    e.wait_ge(S["d_qk_sb"], b + 1)
                    e.wait_ge(S["d_v"], b + 1)
                    for k in range(2):
                        last = e.matmul(bank[6][:, 0:P], d_qkT[:, k, :], d_qkT[:, 2 + k, :], start=k == 0, stop=k == 1)
                    last.then_inc(S["d_sc"], 1)

                def d_turn(b):
                    e.wait_ge(S["d_exp"], b + 1)
                    e.transpose(bank[6][:, 0:P], d_P_, ident).then_inc(S["d_ptr"], 1)

                def d_values(b):
                    e.wait_ge(S["d_pt"], b + 1)
                    e.matmul(bank[6][:, 0:D], d_PT, d_v_, start=True, stop=True).then_inc(S["d_pv"], 1)

                def g_transpose(b):
                    e.wait_ge(S["g_xn"], b + 1)
                    if past(b): e.wait_ge(S["g_lg"], b)
                    for c in range(2):
                        last = e.transpose(bank[7][:, c * P:c * P + P], g_xn_[:, c * P:c * P + P], ident)
                    last.then_inc(S["g_tr"], 1)

                def g_logits(b):
                    e.wait_ge(S["g_xnT"], b + 1)
                    for c in range(2):
                        last = e.matmul(bank[7][:, D:D + E], g_T[:, c * P:c * P + P], w_gate[:, c, :],
                                        start=c == 0, stop=c == 1)
                    last.then_inc(S["g_sum"], 1)

                def step(i):
                    b = i - 2
                    if live(b):
                        att1["values"](e, b, 2)
                        att1["turn"](e, b, 3)
                    b = i - 4
                    if live(b):
                        d_turn(b)
                    b = i - 3
                    if live(b):
                        d_transpose(b)
                    b = i - 2
                    if live(b):
                        att1["values"](e, b, 3)
                    b = i - 4
                    if live(b):
                        d_values(b)
                    b = i - 1
                    if live(b):
                        s_turn_qk(b)
                    b = i - 2
                    if live(b):
                        s_turn_o(b)
                    b = i - 3
                    if live(b):
                        d_project(b)
                    b = i - 1
                    if live(b):
                        att1["scores"](e, b, 0)
                        att1["scores"](e, b, 1)
                    b = i - 2
                    if live(b):
                        s_out(b)
                    b = i
                    if live(b):
                        s_transpose(b)
                    b = i - 1
                    if live(b):
                        att1["scores"](e, b, 2)
                        att1["turn"](e, b, 0)
                    b = i - 4
                    if live(b):
                        g_transpose(b)
                    b = i - 3
                    if live(b):
                        d_scores(b)
                    b = i - 1
                    if live(b):
                        att1["values"](e, b, 0)
                        att1["turn"](e, b, 1)
                        att1["scores"](e, b, 3)
                    b = i - 4
                    if live(b):
                        g_logits(b)
                    b = i - 1
                    if live(b):
                        att1["values"](e, b, 1)
                        att1["turn"](e, b, 2)
                    b = i
                    if live(b):
                        s_project(b)

                pipeline(e, 4, step)

            @block.scalar
            def _(e):
                def copy(ready, count, dst, src, done, free=None):
                    if past(count): e.wait_ge(S[ready], count)
                    if free and past(free[1]): e.wait_ge(S[free[0]], free[1])
                    e.activation(dst, src, ACT.Copy).then_inc(S[done], 1)

                def blocks(bk, n):
                    return bank[bk][:, 0:n * P].rearrange("p (k t) -> p k t", k=n)

                def s_tanh(b):
                    e.wait_ge(S["s_u"], b + 1)
                    e.activation(s_h_, s_h_, ACT.Tanh).then_inc(S["s_h"], 1)

                def s_values(b):
                    e.wait_ge(S["s_qr"], 2 * b + 2)
                    if past(b): e.wait_ge(S["s_pv"], 4 * b)
                    e.activation(s_vx[:, :, 0:DH], bank[0][:, D + KV * DH:NQ].rearrange("p (h d) -> p h d", d=DH),
                                 ACT.Copy).then_inc(S["s_v"], 1)

                def s_heads(b):
                    e.wait_ge(S["s_qtr"], b + 1)
                    if past(4 * b): e.wait_ge(S["s_sc"], 4 * b)
                    e.activation(s_kT_, bank[0][:, D:D + P], ACT.Copy).then_inc(S["s_kT"], 1)
                    for odd, mask in enumerate((m_even, m_odd)):
                        e.activation(s_qT_[:, odd], blocks(0, 2), ACT.Copy, scale=mask).then_inc(S["s_qT"], 1)

                def d_heads(b):
                    e.wait_ge(S["d_qk"], b + 1)
                    if past(b): e.wait_ge(S["d_sc"], b)
                    for c in range(4):
                        bias = (dbq if c < 2 else dbk)[:, c % 2:c % 2 + 1]
                        last = e.activation(d_qkT[:, c, :], bank[5][:, c * P:c * P + P], ACT.Identity, bias=bias)
                    last.then_inc(S["d_qk_sb"], 1)

                def d_exp(b):
                    e.wait_ge(S["d_nmax"], b + 1)
                    if past(b): e.wait_ge(S["d_ptr"], b)
                    if past(b): e.wait_ge(S["d_rinv"], b)
                    e.activation(d_P_, bank[6][:, 0:P], ACT.Exp, scale=1.0 / float(np.sqrt(D)), bias=d_nm,
                                 accum_out=d_sum).then_inc(S["d_exp"], 1)

                def step(i):
                    b = i
                    if live(b):
                        s_tanh(b)
                    b = i - 4
                    if live(b):
                        d_exp(b)
                    b = i - 2
                    if live(b):
                        att1["take"](e, b, 3)
                    b = i - 4
                    if live(b):
                        copy("d_ptr", b + 1, d_PT, bank[6][:, 0:P], "d_pt", ("d_pv", b))
                    b = i - 3
                    if live(b):
                        copy("d_tr", b + 1, d_T, blocks(5, 4), "d_xcT", ("d_vmm", b))
                    b = i - 1
                    if live(b):
                        s_values(b)
                    b = i - 2
                    if live(b):
                        copy("s_otr", b + 1, s_oT[:, 0], blocks(1, 2), "s_ohi", ("s_proj", b))
                    b = i - 1
                    if live(b):
                        s_heads(b)
                    b = i - 3
                    if live(b):
                        copy("d_vmm", b + 1, d_v_, bank[6][:, 0:D], "d_v", ("d_pv", b))
                    b = i - 1
                    if live(b):
                        att1["exponents"](e, b, 0)
                    b = i - 3
                    if live(b):
                        d_heads(b)
                    b = i - 1
                    if live(b):
                        att1["take"](e, b, 0)
                        att1["exponents"](e, b, 1)
                    b = i - 4
                    if live(b):
                        copy("g_tr", b + 1, g_T, bank[7][:, 0:D], "g_xnT", ("g_sum", b))
                    b = i - 1
                    if live(b):
                        att1["take"](e, b, 1)
                    b = i
                    if live(b):
                        copy("s_tr", b + 1, s_T[:, 0], blocks(0, 2), "s_hi", ("s_qkv", b))
                    b = i - 1
                    if live(b):
                        att1["exponents"](e, b, 2)
                        att1["take"](e, b, 2)
                        att1["exponents"](e, b, 3)

                pipeline(e, 4, step)

            @block.vector
            def _(e):
                def lo(pre, b, dst, src, high):
                    e.wait_ge(S[pre + "hi"], b + 1)
                    e.tensor_tensor(dst, src, high.bitcast(F32), ALU.subtract).then_inc(S[pre + "lo"], 1)

                def blocks(bk, n):
                    return bank[bk][:, 0:n * P].rearrange("p (k t) -> p k t", k=n)

                def stats(pre, b, src, cols, ready, factor=1.0, add=EPS):
                    row_statistics(e, pre, b, src, cols, ready, factor, add)

                def s_head(b):
                    e.wait_ge(S["s_xo"], 16 * (b + 1))
                    if past(b): e.wait_ge(S["s_x3"], b)
                    e.tensor_tensor(s_h_, s_xo_, v_row, ALU.add).then_inc(S["s_u"], 1)

                def s_join(b):
                    e.wait_ge(S["s_h"], b + 1)
                    e.tensor_tensor(x_res[:, ds(b * D, D)], s_h_, x_res[:, ds(b * D, D)], ALU.add).then_inc(S["s_x3"], 1)
                    stats("s", b, x_res[:, ds(b * D, D)], s_cols, ("s_x3", b + 1), 1.0 + EPS32, EPS * EPS32)

                def normed(pre, b, dst, src, cols, *free):
                    e.wait_ge(S[pre + "_rs"], b + 1)
                    if past(free[1]): e.wait_ge(S[free[0]], free[1])
                    e.tensor_scalar(dst, src, cols[1][:, 0:1], cols[5], ALU.subtract, ALU.mult)\
                        .then_inc(S[pre + "_xn"], 1)

                def s_rotary(b):
                    e.wait_ge(S["s_qkv"], b + 1)
                    if past(b): e.wait_ge(S["s_qtr"], b)
                    rf = const[:, C_RF:C_RF + DH]
                    e.tensor_tensor(s_qr_[:, 0:D].rearrange("p (h d) -> p h d", d=DH),
                                    bank[0][:, 0:D].rearrange("p (h d) -> p h d", d=DH),
                                    rf.unsqueeze(1).to_broadcast([P, HEADS, DH]), ALU.mult).then_inc(S["s_qr"], 1)
                    for r in range(2):
                        n = D + r * KV * DH
                        last = e.tensor_tensor(s_qr_[:, n:n + KV * DH].rearrange("p (h d) -> p h d", d=DH),
                                               bank[0][:, D:D + KV * DH].rearrange("p (h d) -> p h d", d=DH),
                                               rf.unsqueeze(1).to_broadcast([P, KV, DH]), ALU.mult)
                    last.then_inc(S["s_qr"], 1)

                def s_sum(b):
                    e.wait_ge(S["s_o"], b + 1)
                    e.wait_ge(S["s_xn"], b + 1)
                    e.tensor_tensor(x_res[:, ds(b * D, D)], x_res[:, ds(b * D, D)], s_o_, ALU.add).then_inc(S["s_x3s"], 1)

                def s_residual(b):
                    e.wait_ge(S["s_proj"], b + 1)
                    e.wait_ge(S["s_x3s"], b + 1)
                    e.tensor_tensor(x_res[:, ds(b * D, D)], bank[1][:, 0:D], x_res[:, ds(b * D, D)], ALU.add).then_inc(S["s_x4"], 1)
                    stats("d", b, x_res[:, ds(b * D, D)], d_cols, ("s_x4", b + 1))

                def d_maximum(b):
                    e.wait_ge(S["d_sc"], b + 1)
                    if past(b): e.wait_ge(S["d_nmax"], b)
                    e.tensor_reduce(d_mx, bank[6][:, 0:P], AX.X, ALU.max).then_inc(S["d_max"], 1)
                    e.wait_ge(S["d_max"], b + 1)
                    if past(b): e.wait_ge(S["d_exp"], b)
                    e.tensor_scalar(d_nm, d_mx, -1.0 / float(np.sqrt(D)), None, ALU.mult).then_inc(S["d_nmax"], 1)

                def d_residual(b):
                    e.wait_ge(S["d_exp"], b + 1)
                    if past(b): e.wait_ge(S["d_x5"], b)
                    e.reciprocal(d_ri, d_sum).then_inc(S["d_rinv"], 1)
                    e.wait_ge(S["d_pv"], b + 1)
                    e.wait_ge(S["d_x4b"], b + 1)
                    e.wait_ge(S["d_rinv"], b + 1)
                    e.scalar_tensor_tensor(out=x_res[:, ds(b * D, D)], in0=bank[6][:, 0:D], scalar=d_ri,
                                           in1=x_res[:, ds(b * D, D)], op0=ALU.mult, op1=ALU.add).then_inc(S["d_x5"], 1)
                    stats("g", b, x_res[:, ds(b * D, D)], g_cols, ("d_x5", b + 1))

                def g_norm(b):
                    e.wait_ge(S["g_rs"], b + 1)
                    e.tensor_scalar(tab[:, ds(b * TAB + 3 * NH, 1)], g_cols[1][:, 0:1], 1.0, None, ALU.mult)
                    e.tensor_scalar(tab[:, ds(b * TAB + 3 * NH + 1, 1)], g_cols[5], 1.0, None, ALU.mult)
                    normed("g", b, g_xn_, x_res[:, ds(b * D, D)], g_cols, "g_tr", b)

                def g_logits(b):
                    e.wait_ge(S["g_sum"], b + 1)
                    e.tensor_tensor(tab[:, ds(b * TAB, E)], bank[7][:, D:D + E], lbb, ALU.add).then_inc(S["g_lg"], 1)

                e.memset(s_vx[:, :, DH:VX], 1.0)

                def step(i):
                    b = i
                    if live(b):
                        s_head(b)
                    b = i - 1
                    if live(b):
                        s_rotary(b)
                    b = i
                    if live(b):
                        s_join(b)
                    b = i - 2
                    if live(b):
                        att1["normalise"](e, b, s_o_, s_ri, ["s_otr", "s_x3s"], [b, b])
                    b = i - 4
                    if live(b):
                        d_residual(b)
                    b = i - 2
                    if live(b):
                        s_sum(b)
                        lo("s_o", b, s_oT[:, 1], blocks(1, 2), s_oT[:, 0])
                    b = i
                    if live(b):
                        normed("s", b, s_xn_, x_res[:, ds(b * D, D)], s_cols, "s_tr", b)
                    b = i - 1
                    if live(b):
                        att1["softmax"](e, b, 0)
                    b = i - 4
                    if live(b):
                        g_norm(b)
                    b = i - 1
                    if live(b):
                        att1["softmax"](e, b, 1)
                    b = i - 2
                    if live(b):
                        s_residual(b)
                    b = i - 1
                    if live(b):
                        att1["softmax"](e, b, 2)
                    b = i
                    if live(b):
                        lo("s_", b, s_T[:, 1], blocks(0, 2), s_T[:, 0])
                    b = i - 3
                    if live(b):
                        d_maximum(b)
                    b = i - 1
                    if live(b):
                        att1["softmax"](e, b, 3)
                    b = i - 2
                    if live(b):
                        normed("d", b, d_xn_, x_res[:, ds(b * D, D)], d_cols, "d_tr", b)
                    b = i - 4
                    if live(b):
                        g_logits(b)

                pipeline(e, 4, step)

            @block.gpsimd
            def _(e):
                def newton(pre, b, cols):
                    rsqrt_newton(e, pre, b, cols[3], cols[4], cols[5])

                def add_bias(b):
                    e.wait_ge(S["d_xn"], b + 1)
                    e.tensor_tensor(x_res[:, ds(b * D, D)], x_res[:, ds(b * D, D)], dbv_row, ALU.add).then_inc(S["d_x4b"], 1)

                def step(i):
                    b = i
                    if live(b):
                        newton("s", b, s_cols)
                    b = i - 4
                    if live(b):
                        newton("g", b, g_cols)
                    b = i - 2
                    if live(b):
                        newton("d", b, d_cols)
                        add_bias(b)

                pipeline(e, 4, step)

        jobs2 = []
        for x_ in range(E):
            jobs2 += [(e_gate[x_], D, to(w_gu, x_ * 2 * P), 1.0, None), (e_up[x_], D, to(w_gu, (2 * x_ + 1) * P), 1.0, None)]
            for r in range(2):
                jobs2.append((e_down[x_, r * P:(r + 1) * P, :], P, to(w_dn[:, :, x_:x_ + 1, :], r * P), 1.0, None))
        for r in range(2):
            jobs2 += [(sh_gate[r * P:(r + 1) * P, :], D, to(w_gu, (16 + 2 * r) * P), 1.0, None),
                      (sh_up[r * P:(r + 1) * P, :], D, to(w_gu, (17 + 2 * r) * P), 1.0, None),
                      (sh_down[r * P:(r + 1) * P, :], D, to(w_dn[:, :, E:E + 2, :], r * P), 1.0, None)]
        w2 = weights("w2", work[:, 3072:7168], jobs2)
        t_s, t_first, t_second, t_tmp = (work[:, 512 * k:512 * k + NT].rearrange("p (b e) -> p b e", e=E) for k in range(4))
        t_max, t_max2, t_key, t_rcp = (work[:, 2048 + NB * k:2048 + NB * k + NB] for k in range(4))
        t_part, t_mean = work[:, 2304:2304 + 2 * E], work[:, 2336:2336 + 2 * E]
        logits = tab3[:, :, 0:E]
        coef = tab3[:, :, E:2 * E]

        with phase("route") as block:
            @block.sync
            def _(e):
                w2[0](e)

            @block.tensor
            def _(e):
                w2[1](e)
                e.wait_ge(S["t_part"], 1)
                e.matmul(bank[4][:, 0:2 * E], const[:, C_ONE:C_ONE + P], t_part, start=True, stop=True)\
                    .then_inc(S["t_tot"], 1)

            @block.scalar
            def _(e):
                e.activation(t_s, logits, ACT.Exp, scale=-1.0).then_inc(S["t_sig"], 1)
                w2[2](e)

            @block.vector
            def _(e):
                n = 0

                def link(i):
                    nonlocal n
                    n += 1
                    i.then_inc(S["t_chain"], 1)
                    e.wait_ge(S["t_chain"], n)

                def wide(a):
                    return a.unsqueeze(2).to_broadcast([P, NB, E])

                def first_of_max(s_, max_, first_):
                    link(e.tensor_reduce(max_, s_, AX.X, ALU.max))
                    link(e.tensor_tensor(t_tmp, s_, wide(max_), ALU.is_equal))
                    link(e.tensor_tensor(t_tmp, t_tmp, const[:, C_IOTA:C_IOTA + E].unsqueeze(1).to_broadcast([P, NB, E]),
                                         ALU.mult))
                    link(e.tensor_reduce(t_key, t_tmp, AX.X, ALU.max))
                    link(e.tensor_tensor(first_, t_tmp, wide(t_key), ALU.is_equal))

                e.wait_ge(S["t_sig"], 1)
                link(e.tensor_scalar(t_s, t_s, 1.0, None, ALU.add))
                link(e.reciprocal(t_s, t_s))
                first_of_max(t_s, t_max, t_first)
                link(e.scalar_tensor_tensor(out=t_second, in0=t_first, scalar=-4.0, in1=t_s, op0=ALU.mult, op1=ALU.add))
                first_of_max(t_second, t_max2, t_second)
                link(e.tensor_tensor(t_rcp, t_max, t_max2, ALU.add))
                link(e.tensor_scalar(t_rcp, t_rcp, 1e-8, None, ALU.add))
                link(e.reciprocal(t_rcp, t_rcp))
                link(e.tensor_tensor(t_first, t_first, t_second, ALU.add))
                link(e.tensor_tensor(t_s, t_s, t_first, ALU.mult))
                link(e.tensor_tensor(t_s, t_s, wide(t_rcp), ALU.mult))
                e.tensor_reduce(t_part[:, 0:E], t_s.rearrange("p b e -> p e b"), AX.X, ALU.add)
                e.tensor_reduce(t_part[:, E:2 * E], t_first.rearrange("p b e -> p e b"), AX.X, ALU.add)\
                    .then_inc(S["t_part"], 1)
                w2[3](e)
                e.wait_ge(S["t_tot"], 1)
                link(e.tensor_scalar(t_mean[:, E:2 * E], bank[4][:, E:2 * E], 1.0, None, ALU.max))
                link(e.reciprocal(t_mean[:, E:2 * E], t_mean[:, E:2 * E]))
                link(e.scalar_tensor_tensor(out=t_mean[:, 0:E], in0=bank[4][:, 0:E], scalar=0.5, in1=t_mean[:, E:2 * E],
                                            op0=ALU.mult, op1=ALU.mult))
                e.tensor_tensor(coef, t_first, t_mean[:, 0:E].unsqueeze(1).to_broadcast([P, NB, E]), ALU.mult)\
                    .then_inc(S["t_coef"], 1)

        NG = 5
        wpos[0] = rpos[0] = 0
        f_xn_ = [wk(D), wk(D)]
        f_T = [wr(2 * D).rearrange("p (s k t) -> p s k t", s=2, k=2) for _ in range(2)]
        f_t = [wk(2 * P).rearrange("p (x i) -> p x i", x=2) for _ in range(2)]
        f_h_ = [wk(2 * P).rearrange("p (x i) -> p x i", x=2) for _ in range(2)]
        f_hT = [wr(2 * D).rearrange("p (s k t) -> p s k t", s=2, k=2) for _ in range(2)]
        f_coef = [tiny[:, 0:E], tiny[:, E:2 * E]]
        f_stage = [wk(D), wk(D)]

        def pairs(e, steps, tail):
            steps(0)
            steps(1)
            with e.Fori(2, NB // 2 - 1) as h:
                steps(h)
            steps(NB // 2 - 1)
            tail(NB // 2)

        def before(h):
            return not isinstance(h, int) or h > 0

        def after(h):
            return not isinstance(h, int) or h < NB // 2 - 1

        with phase("experts") as block:
            @block.sync
            def _(e):
                def steps(h):
                    for k in range(2):
                        b = 2 * h + k
                        e.wait_ge(S["f_x6"], b + 1)
                        e.dma_start(tile(out, b), f_stage[k]).then_inc(S[f"f_out{k}"], 16)

                pairs(e, steps, lambda h: None)
                for k in range(2):
                    e.wait_ge(S[f"f_out{k}"], 16 * (NB // 2))

            @block.tensor
            def _(e):
                def transpose(b, k):
                    e.wait_ge(S["f_xn"], b + 1)
                    if past(b): e.wait_ge(S["f_lo"], b)
                    for c in range(2):
                        last = e.transpose(bank[6][:, c * P:c * P + P], f_xn_[k][:, c * P:c * P + P], ident)
                    last.then_inc(S["f_tr"], 1)

                def up(n, b, g, q, k):
                    e.wait_ge(S["f_lo"], b + 1)
                    if past(n - 1): e.wait_ge(S["f_h"], n - 1)
                    project(e, bank[q][:, :], f_T[k], w_gu, 2, 4 * P * g, 4 * P * (g + 1)).then_inc(S["f_gu"], 1)

                def turn(n, q):
                    e.wait_ge(S["f_h"], n + 1)
                    if past(n - 1): e.wait_ge(S["f_hlo"], n - 1)
                    for j in range(2):
                        last = e.transpose(bank[2 + q][:, j * P:j * P + P], f_h_[q][:, j, :], ident)
                    last.then_inc(S["f_htr"], 1)

                def down(n, b, g, q, k):
                    e.wait_ge(S["f_hlo"], n + 1)
                    if g == 0:
                        if past(b - 1): e.wait_ge(S["f_x6"], b - 1)
                    for j in range(2):
                        last = mm3(e, bank[4 + k][:, 0:D], (f_hT[q][:, 0, j, :], f_hT[q][:, 1, j, :]),
                                   (w_dn[:, 0, 2 * g + j, :], w_dn[:, 1, 2 * g + j, :]),
                                   g == 0 and j == 0, g == NG - 1 and j == 1)
                    last.then_inc(S["f_acc"], 1)

                def later(h, m):
                    if m < 0:
                        h, m = h - 1, m + 2 * NG
                    return 2 * NG * h + m, 2 * h + m // NG, m % NG, m % 2, m // NG

                def steps(h):
                    for m in range(2 * NG):
                        n, b, g, q, k = later(h, m)
                        up(n, b, g, q, k)
                        if m >= 1 or before(h):
                            n, b, g, q, k = later(h, m - 1)
                            turn(n, q)
                        if m >= 2 or before(h):
                            down(*later(h, m - 2))
                        if m == 2:
                            transpose(2 * h + 1, 1)
                        if m == 7 and after(h):
                            transpose(2 * h + 2, 0)

                def tail(h):
                    n, b, g, q, k = later(h, -1)
                    turn(n, q)
                    down(*later(h, -2))
                    down(*later(h, -1))

                transpose(0, 0)
                pairs(e, steps, tail)

            @block.scalar
            def _(e):
                def high(b, k):
                    e.wait_ge(S["f_tr"], b + 1)
                    if past(NG * (b - 1)): e.wait_ge(S["f_gu"], NG * (b - 1))
                    e.activation(f_T[k][:, 0], bank[6][:, 0:D].rearrange("p (k t) -> p k t", k=2), ACT.Copy)\
                        .then_inc(S["f_hi"], 1)

                def gate(n, q):
                    e.wait_ge(S["f_gu"], n + 1)
                    if past(n - 1): e.wait_ge(S["f_h"], n - 1)
                    e.activation(f_t[q], bank[q][:, :].rearrange("p (x o i) -> p x o i", x=2, o=2)[:, :, 0, :],
                                 ACT.Tanh, scale=0.5).then_inc(S["f_tanh"], 1)

                def hidden(n, q):
                    e.wait_ge(S["f_htr"], n + 1)
                    if past(n - 1): e.wait_ge(S["f_acc"], n - 1)
                    e.activation(f_hT[q][:, 0], bank[2 + q][:, 0:2 * P].rearrange("p (k t) -> p k t", k=2), ACT.Copy)\
                        .then_inc(S["f_hhi"], 1)

                def steps(h):
                    for m in range(2 * NG):
                        n = 2 * NG * h + m
                        gate(n, m % 2)
                        if m >= 1 or before(h):
                            hidden(n - 1, (m - 1) % 2)
                        if m == 2:
                            high(2 * h + 1, 1)
                        if m == 7 and after(h):
                            high(2 * h + 2, 0)

                high(0, 0)
                pairs(e, steps, lambda h: hidden(2 * NG * h - 1, 1))

            @block.vector
            def _(e):
                def norm(b, k):
                    if past(b - 1): e.wait_ge(S["f_tr"], b - 1)
                    if past(NG * (b - 1)): e.wait_ge(S["f_h"], NG * (b - 1))
                    e.tensor_scalar(f_coef[k], tab[:, ds(b * TAB + E, E)], 1.0, None, ALU.mult)
                    e.tensor_scalar(f_xn_[k], x_res[:, ds(b * D, D)], tab[:, ds(b * TAB + 3 * NH, 1)],
                                    tab[:, ds(b * TAB + 3 * NH + 1, 1)], ALU.subtract, ALU.mult)\
                        .then_inc(S["f_xn"], 1)

                def low(b, k):
                    e.wait_ge(S["f_hi"], b + 1)
                    e.tensor_tensor(f_T[k][:, 1], bank[6][:, 0:D].rearrange("p (k t) -> p k t", k=2),
                                    f_T[k][:, 0].bitcast(F32), ALU.subtract).then_inc(S["f_lo"], 1)

                def gated(n, g, q, k):
                    v = bank[q][:, :].rearrange("p (x o i) -> p x o i", x=2, o=2)
                    e.wait_ge(S["f_tanh"], n + 1)
                    e.scalar_tensor_tensor(out=f_t[q], in0=f_t[q], scalar=1.0, in1=v[:, :, 0, :],
                                           op0=ALU.add, op1=ALU.mult).then_inc(S["f_tg"], 1)
                    e.wait_ge(S["f_tg"], n + 1)
                    if past(n - 1): e.wait_ge(S["f_htr"], n - 1)
                    for j in range(2):
                        w = f_coef[k][:, 2 * g + j:2 * g + j + 1] if g < NG - 1 else 0.5
                        last = e.scalar_tensor_tensor(out=f_h_[q][:, j, :], in0=f_t[q][:, j, :], scalar=w,
                                                      in1=v[:, j, 1, :], op0=ALU.mult, op1=ALU.mult)
                    last.then_inc(S["f_h"], 1)

                def hidden(n, q):
                    e.wait_ge(S["f_hhi"], n + 1)
                    e.tensor_tensor(f_hT[q][:, 1], bank[2 + q][:, 0:2 * P].rearrange("p (k t) -> p k t", k=2),
                                    f_hT[q][:, 0].bitcast(F32), ALU.subtract).then_inc(S["f_hlo"], 1)

                def finish(b, k, h_):
                    e.wait_ge(S["f_acc"], NG * (b + 1))
                    if past(16 * h_): e.wait_ge(S[f"f_out{k}"], 16 * h_)
                    e.tensor_tensor(f_stage[k], bank[4 + k][:, 0:D], x_res[:, ds(b * D, D)], ALU.add)\
                        .then_inc(S["f_x6"], 1)

                def steps(h):
                    for m in range(2 * NG):
                        n = 2 * NG * h + m
                        gated(n, m % NG, m % 2, m // NG)
                        if m >= 1 or before(h):
                            hidden(n - 1, (m - 1) % 2)
                        if m == 1:
                            norm(2 * h + 1, 1)
                        if m == 2:
                            low(2 * h + 1, 1)
                            if before(h):
                                finish(2 * h - 1, 1, h - 1)
                        if m == 6 and after(h):
                            norm(2 * h + 2, 0)
                        if m == 7:
                            if after(h):
                                low(2 * h + 2, 0)
                            finish(2 * h, 0, h)

                def tail(h):
                    hidden(2 * NG * h - 1, 1)
                    finish(2 * h - 1, 1, h - 1)

                norm(0, 0)
                low(0, 0)
                pairs(e, steps, tail)


_INS = ["x", "ctx_1024",
        "L0_attn_in_proj_w", "L0_attn_conv_w", "L0_attn_conv_b", "L0_attn_norm_w", "L0_attn_out_proj_w",
        "L0_attn_dt_bias", "L0_attn_A_log", "L0_attn_D_param",
        "L0_xattn_Wq", "L0_xattn_bq", "L0_xattn_Wk", "L0_xattn_bk", "L0_xattn_Wv", "L0_xattn_bv",
        "L0_xattn_Wo", "L0_xattn_bo",
        "L0_ffn_wf", "L0_ffn_uf", "L0_ffn_bf", "L0_ffn_wi", "L0_ffn_ui", "L0_ffn_bi",
        "L0_ffn_wc", "L0_ffn_uc", "L0_ffn_bc", "L0_ffn_wo", "L0_ffn_uo", "L0_ffn_bo", "L0_ffn_in_c",
        "L1_attn_w_q", "L1_attn_w_k", "L1_attn_w_v", "L1_attn_w_o", "L1_attn_g",
        "L1_xattn_Wq", "L1_xattn_bq", "L1_xattn_Wk", "L1_xattn_bk", "L1_xattn_Wv", "L1_xattn_bv",
        "L1_ffn_gate_w", "L1_ffn_lb_bias", "L1_ffn_expert_gate_w", "L1_ffn_expert_up_w",
        "L1_ffn_expert_down_w", "L1_ffn_shared_gate_w", "L1_ffn_shared_up_w", "L1_ffn_shared_down_w"]


def kernel(**inputs):
    import numpy as _np
    import concourse.bacc as _bacc
    from concourse.bass_utils import run_bass_kernel_spmd as _run

    nc = _bacc.Bacc("TRN2", target_bir_lowering=False, num_devices=1)
    arrays, args = {}, []
    for name in _INS:
        a = _np.ascontiguousarray(inputs[name])
        arrays[f"in_{name}"] = a
        args.append(nc.dram_tensor(f"in_{name}", a.shape, mybir.dt.from_np(a.dtype), kind="ExternalInput").ap())
    shape = arrays["in_x"].shape
    out = nc.dram_tensor("out_dram", shape, F32, kind="ExternalOutput").ap()
    xo = nc.dram_tensor("recurrence_out", shape, F32, kind="Internal").ap()
    table = nc.inline_tensor(constant_table(), name="constant_table").ap()
    cum = nc.dram_tensor("decay_sums", (shape[0], NH * P), F32, kind="Internal").ap()
    decoder(nc, args, xo, cum, table, out)
    r = _run(nc, [arrays], core_ids=[0])
    return r.results[0]["out_dram"]
```
